# Optimizing a Trainium2 kernel written in Bass

```python
import numpy as np
import jax
import jax.numpy as jnp

def _softmax(x, axis=-1):
    return jax.nn.softmax(x, axis=axis)

def _gelu(x):
    return jax.nn.gelu(x, approximate=True)

def _silu(x):
    return jax.nn.silu(x)

def _sigmoid(x):
    return jax.nn.sigmoid(x)

def _layernorm(x, axis=-1, eps=1e-05):
    m = jnp.mean(x, axis=axis, keepdims=True)
    v = jnp.var(x, axis=axis, keepdims=True)
    return (x - m) / jnp.sqrt(v + eps)

def _scatter_add(tgt, idx, src, axis=0):
    return tgt.at[idx].add(src)

def _segment_sum(src, seg, n):
    return jax.ops.segment_sum(src, seg, n)
kernel_name = 'mk_sandwich_d1_jaxref_r4_866f90'

def setup_inputs(seed: int=0):
    np.random.seed(seed)
    _w = jnp.asarray

    def _L0_attn_setup():
        import jax, jax.numpy as jnp
        import numpy as np
        H = 16
        D_MODEL = 512
        HEAD_DIM = D_MODEL // H
        B, S = (4, 512)
        key = jax.random.key(seed)
        ks = jax.random.split(key, 9)
        std = D_MODEL ** (-0.5)
        hidden_states = jax.random.normal(ks[0], (B, S, D_MODEL), dtype=jnp.float32)
        q_w = jax.random.normal(ks[1], (H * HEAD_DIM, D_MODEL), dtype=jnp.float32) * std
        k_w = jax.random.normal(ks[2], (HEAD_DIM, D_MODEL), dtype=jnp.float32) * std
        v_w = jax.random.normal(ks[3], (HEAD_DIM, D_MODEL), dtype=jnp.float32) * std
        o_w = jax.random.normal(ks[4], (D_MODEL, H * HEAD_DIM), dtype=jnp.float32) * std
        q_b = jnp.zeros((H * HEAD_DIM,), dtype=jnp.float32)
        k_b = jnp.zeros((HEAD_DIM,), dtype=jnp.float32)
        v_b = jnp.zeros((HEAD_DIM,), dtype=jnp.float32)
        o_b = jnp.zeros((D_MODEL,), dtype=jnp.float32)
        return {'hidden_states': hidden_states, 'q_w': q_w, 'q_b': q_b, 'k_w': k_w, 'k_b': k_b, 'v_w': v_w, 'v_b': v_b, 'o_w': o_w, 'o_b': o_b}
    _L0_attn_in = _L0_attn_setup()

    def _L0_ffn_setup():
        import jax, jax.numpy as jnp
        import numpy as np
        E = 8
        TOP_K = 2
        H = 512
        I_MOE = 352
        I_SH = 1408
        B, S = (2, 512)

        def _moe_forward(hidden_states, router_weight, gate_up_proj, down_proj, sh_gate_w, sh_up_w, sh_down_w, shared_gate_w):
            b, s, h = hidden_states.shape
            x = hidden_states.reshape(-1, h)
            shared = jnp.einsum('ti,hi->th', jax.nn.silu(x @ sh_gate_w.T) * (x @ sh_up_w.T), sh_down_w)
            logits = x @ router_weight.T
            probs = jax.nn.softmax(logits.astype(jnp.float32), axis=-1)
            top_v, top_i = jax.lax.top_k(probs, TOP_K)
            top_v = top_v / top_v.sum(axis=-1, keepdims=True)
            combine = (jax.nn.one_hot(top_i, E, dtype=top_v.dtype) * top_v[..., None]).sum(axis=1)
            out = jnp.zeros_like(x)
            for e in range(E):
                gu = x @ gate_up_proj[e].T
                gate, up = (gu[:, :I_MOE], gu[:, I_MOE:])
                cur = jax.nn.silu(gate) * up @ down_proj[e].T
                out = out + cur * combine[:, e:e + 1]
            out = out + jax.nn.sigmoid(x @ shared_gate_w.T) * shared
            return out.reshape(b, s, h)
        key = jax.random.key(seed)
        ks = jax.random.split(key, 8)
        scale = 0.02
        return {'hidden_states': jax.random.normal(ks[0], (B, S, H), dtype=jnp.float32), 'router_weight': jax.random.normal(ks[1], (E, H), dtype=jnp.float32) * scale, 'gate_up_proj': jax.random.normal(ks[2], (E, 2 * I_MOE, H), dtype=jnp.float32) * scale, 'down_proj': jax.random.normal(ks[3], (E, H, I_MOE), dtype=jnp.float32) * scale, 'sh_gate_w': jax.random.normal(ks[4], (I_SH, H), dtype=jnp.float32) * scale, 'sh_up_w': jax.random.normal(ks[5], (I_SH, H), dtype=jnp.float32) * scale, 'sh_down_w': jax.random.normal(ks[6], (H, I_SH), dtype=jnp.float32) * scale, 'shared_gate_w': jax.random.normal(ks[7], (1, H), dtype=jnp.float32) * scale}
    _L0_ffn_in = _L0_ffn_setup()
    _d = {'L0_attn_hidden_states': _L0_attn_in['hidden_states'], 'L0_attn_q_w': _L0_attn_in['q_w'], 'L0_attn_q_b': _L0_attn_in['q_b'], 'L0_attn_k_w': _L0_attn_in['k_w'], 'L0_attn_k_b': _L0_attn_in['k_b'], 'L0_attn_v_w': _L0_attn_in['v_w'], 'L0_attn_v_b': _L0_attn_in['v_b'], 'L0_attn_o_w': _L0_attn_in['o_w'], 'L0_attn_o_b': _L0_attn_in['o_b'], 'L0_ffn_router_weight': _L0_ffn_in['router_weight'], 'L0_ffn_gate_up_proj': _L0_ffn_in['gate_up_proj'], 'L0_ffn_down_proj': _L0_ffn_in['down_proj'], 'L0_ffn_sh_gate_w': _L0_ffn_in['sh_gate_w'], 'L0_ffn_sh_up_w': _L0_ffn_in['sh_up_w'], 'L0_ffn_sh_down_w': _L0_ffn_in['sh_down_w'], 'L0_ffn_shared_gate_w': _L0_ffn_in['shared_gate_w']}
    _x0 = _d['L0_attn_hidden_states']
    _d['L0_attn_hidden_states'] = jax.random.normal(jax.random.fold_in(jax.random.key(seed), 1), (8, 512, 512), dtype=_x0.dtype)
    del _x0
    return _d

def reference(L0_attn_hidden_states, L0_attn_q_w, L0_attn_q_b, L0_attn_k_w, L0_attn_k_b, L0_attn_v_w, L0_attn_v_b, L0_attn_o_w, L0_attn_o_b, L0_ffn_router_weight, L0_ffn_gate_up_proj, L0_ffn_down_proj, L0_ffn_sh_gate_w, L0_ffn_sh_up_w, L0_ffn_sh_down_w, L0_ffn_shared_gate_w):

    def _L0_attn_ref(hidden_states, q_w, q_b, k_w, k_b, v_w, v_b, o_w, o_b):
        import jax, jax.numpy as jnp
        import numpy as np
        H = 16
        D_MODEL = 512
        HEAD_DIM = D_MODEL // H
        B, S = (4, 512)
        b, s, _ = hidden_states.shape
        q = (hidden_states @ q_w.T + q_b).reshape(b, s, H, HEAD_DIM)
        k = hidden_states @ k_w.T + k_b
        v = hidden_states @ v_w.T + v_b
        scores = jnp.einsum('bqhd,bkd->bhqk', q, k) / HEAD_DIM ** 0.5
        causal = jnp.triu(jnp.ones((s, s), dtype=bool), k=1)
        scores = jnp.where(causal[None, None], -jnp.inf, scores)
        attn = jax.nn.softmax(scores.astype(jnp.float32), axis=-1).astype(q.dtype)
        out = jnp.einsum('bhqk,bkd->bqhd', attn, v).reshape(b, s, H * HEAD_DIM)
        return out @ o_w.T + o_b

    def _L0_ffn_ref(hidden_states, router_weight, gate_up_proj, down_proj, sh_gate_w, sh_up_w, sh_down_w, shared_gate_w):
        import jax, jax.numpy as jnp
        import numpy as np
        E = 8
        TOP_K = 2
        H = 512
        I_MOE = 352
        I_SH = 1408
        B, S = (2, 512)

        def _moe_forward(hidden_states, router_weight, gate_up_proj, down_proj, sh_gate_w, sh_up_w, sh_down_w, shared_gate_w):
            b, s, h = hidden_states.shape
            x = hidden_states.reshape(-1, h)
            shared = jnp.einsum('ti,hi->th', jax.nn.silu(x @ sh_gate_w.T) * (x @ sh_up_w.T), sh_down_w)
            logits = x @ router_weight.T
            probs = jax.nn.softmax(logits.astype(jnp.float32), axis=-1)
            top_v, top_i = jax.lax.top_k(probs, TOP_K)
            top_v = top_v / top_v.sum(axis=-1, keepdims=True)
            combine = (jax.nn.one_hot(top_i, E, dtype=top_v.dtype) * top_v[..., None]).sum(axis=1)
            out = jnp.zeros_like(x)
            for e in range(E):
                gu = x @ gate_up_proj[e].T
                gate, up = (gu[:, :I_MOE], gu[:, I_MOE:])
                cur = jax.nn.silu(gate) * up @ down_proj[e].T
                out = out + cur * combine[:, e:e + 1]
            out = out + jax.nn.sigmoid(x @ shared_gate_w.T) * shared
            return out.reshape(b, s, h)
        return _moe_forward(hidden_states, router_weight, gate_up_proj, down_proj, sh_gate_w, sh_up_w, sh_down_w, shared_gate_w)
    x = L0_attn_hidden_states
    x = x + _layernorm(_L0_attn_ref(_layernorm(x, axis=-1), L0_attn_q_w, L0_attn_q_b, L0_attn_k_w, L0_attn_k_b, L0_attn_v_w, L0_attn_v_b, L0_attn_o_w, L0_attn_o_b), axis=-1)
    x = x + _layernorm(_L0_ffn_ref(_layernorm(x, axis=-1), L0_ffn_router_weight, L0_ffn_gate_up_proj, L0_ffn_down_proj, L0_ffn_sh_gate_w, L0_ffn_sh_up_w, L0_ffn_sh_down_w, L0_ffn_shared_gate_w), axis=-1)
    return x

_drawn_inputs = setup_inputs


def setup_inputs(seed=0):
    import zlib

    import numpy as np

    out = dict(_drawn_inputs(seed))
    spreads = {'L0_attn_q_b': (0.0, 0.1),
     'L0_attn_k_b': (0.0, 0.1),
     'L0_attn_v_b': (0.0, 0.1),
     'L0_attn_o_b': (0.0, 0.1)}
    factors = {}
    for name, (base, spread) in spreads.items():
        noise = np.random.default_rng([zlib.crc32(name.encode()), seed]).standard_normal(out[name].shape)
        drawn = base * np.exp(spread * noise) if base else spread * noise
        out[name] = jnp.asarray(drawn.astype(out[name].dtype))
    for name, factor in factors.items():
        out[name] = (out[name] * factor).astype(out[name].dtype)
    return out
```

```python
import concourse.bass as bass
from concourse import mybir
from contextlib import ExitStack

F32 = mybir.dt.float32
F32R = mybir.dt.float32r
BF16 = mybir.dt.bfloat16
I32 = mybir.dt.int32
U32 = mybir.dt.uint32
ALU = mybir.AluOpType
ACT = mybir.ActivationFunctionType
AX_X = mybir.AxisListType.X

P = 128
S = 512
NB = 8
D = 512
C = D // P
QT = S // P
H = 16
HD = D // H
HG = P // HD
E = 8
R = E + 1
EPS = 1e-5
SCALE = float(HD) ** -0.5
MASKED = -3.0e38
I_MOE = 352
I_SH = 1408
TS = 512
NTT = NB * QT
NT = (2 * NB * S + E * (TS - 1)) // TS
SC = NT * TS // P
PASSES = ((0, 0), (0, 1), (1, 0))
MAGIC = float(0x5F3759DF - (1 << 22))
NEWTON = 3


class Steps:

    def __init__(self, engine, sem):
        self.engine, self.sem, self.n = engine, sem, 0

    def then_wait(self, instruction):
        instruction.then_inc(self.sem, 1)
        self.n += 1
        self.engine.wait_ge(self.sem, self.n)


class InverseStd:
    STEPS = 4 * NEWTON + 1

    def __init__(self, nc, sb, sem, name, constants):
        self.nc, self.constants = nc, constants
        self.stats = sb("stats" + name, [P, QT, 6])
        self.mean_var = sb("mean_var" + name, [P, QT, 2])
        self.half = sb("half" + name, [P, QT])
        self.bits = sb("bits" + name, [P, QT])
        self.t = sb("t" + name, [P, 3, QT])
        self.rstd = sb("rstd" + name, [P, QT])
        self.bias = sb("bias" + name, [P, QT])
        self.row_six = sem("row_six" + name)
        self.row_var = sem("row_var" + name)
        self.guessed = sem("guessed" + name)
        self.newton = sem("newton" + name)
        self.ready = sem("std_ready" + name)

    def row_stats(self, src, i):
        self.nc.vector.bn_stats(self.stats[:, i, :], src[:, i, :]).then_inc(self.row_six, 1)

    def await_stats(self, n, tiles=QT):
        self.nc.vector.wait_ge(self.row_six, QT * n + tiles)

    def aggregate(self, tiles=range(QT)):
        for i in tiles:
            last = self.nc.vector.bn_aggr(self.mean_var[:, i, :], self.stats[:, i, :])
        if tiles[-1] == QT - 1:
            last.then_inc(self.row_var, 1)

    def halve(self, n):
        self.nc.vector.wait_ge(self.row_var, 3 * n + 1)
        self.nc.vector.tensor_scalar(self.half[:], self.mean_var[:, :, 1], EPS, 0.5, ALU.add,
                                     ALU.mult).then_inc(self.row_var, 1)

    def shift_bits(self, n):
        self.nc.vector.wait_ge(self.row_var, 3 * n + 2)
        self.nc.vector.tensor_scalar(self.bits[:].bitcast(I32), self.half[:].bitcast(I32), 1, None,
                                     ALU.logical_shift_right).then_inc(self.row_var, 1)

    def guess(self, n):
        self.nc.vector.wait_ge(self.row_var, 3 * n + 3)
        self.nc.vector.tensor_scalar(self.t[:, 2, :].bitcast(I32), self.bits[:].bitcast(I32), -1.0, MAGIC,
                                     ALU.mult, ALU.add).then_inc(self.guessed, 1)

    def refine(self, n):
        zero, three_halves = self.constants[:, 0, :], self.constants[:, 1, :]
        a, b, y = self.t[:, 0, :], self.t[:, 1, :], self.t[:, 2, :]
        at = self.STEPS * n
        self.nc.gpsimd.wait_ge(self.guessed, n + 1)

        def step(out, in0, in1, op):
            nonlocal at
            at += 1
            self.nc.gpsimd.tensor_tensor(out, in0, in1, op).then_inc(self.newton, 1)
            self.nc.gpsimd.wait_ge(self.newton, at)

        for k in range(NEWTON):
            step(a, y, y, ALU.mult)
            step(b, a, self.half[:], ALU.mult)
            step(a, three_halves, b, ALU.subtract)
            y_next = self.rstd[:] if k == NEWTON - 1 else y
            step(y_next, y, a, ALU.mult)
        step(b, self.mean_var[:, :, 0], self.rstd[:], ALU.mult)
        self.nc.gpsimd.tensor_tensor(self.bias[:], zero, b, ALU.subtract).then_inc(self.ready, 1)


def build_attention(nc, x, wq, wvk, wo, wr, qb, vkb, ob, x1_out, xn_out, logits, idf, idb, mask, norm_constants):
    ctx = ExitStack()
    with ctx:
        def sb(name, shape, dt=F32):
            return ctx.enter_context(nc.sbuf_tensor("at_" + name, shape, dt))

        def sem(name):
            return ctx.enter_context(nc.semaphore("at_" + name))

        wq_s = [sb(f"wq{j}", [P, C, D], F32R) for j in range(2)]
        wvk_s = [sb(f"wvk{j}", [P, C, 2 * HD], F32R) for j in range(2)]
        wo_s = [sb(f"wo{j}", [P, C, D], F32R) for j in range(2)]
        wr_s = [sb(f"wr{j}", [P, C, R], F32R) for j in range(2)]
        qb_s = sb("qb", [P, C])
        vkb_s = sb("vkb", [2 * HD, 1])
        vks_s = sb("vks", [2 * HD, 1])
        vkbs_s = sb("vkbs", [2 * HD, 1])
        ob_s = sb("ob", [P, D])
        x_in = sb("x_in", [P, QT, D])
        x_res = sb("x_res", [P, QT, D])
        y = sb("y", [P, QT, D])
        xn2 = sb("xn2", [P, QT, D])
        xT = [sb(f"xT{j}", [P, C, S], F32R) for j in range(2)]
        vk = sb("vk", [2 * HD, S])
        vk_h = [sb(f"vk_h{j}", [2 * HD, S], F32R) for j in range(2)]
        q_h = [[sb(f"q_h{j}{r}", [P, S], F32R) for j in range(2)] for r in range(2)]
        Qs = sb("Qs", [3 * HD, H, S], F32R)
        Ks = sb("Ks", [3 * HD, S], F32R)
        V = sb("V", [P, QT, HD])
        PW = QT * (QT + 1) // 2 * P
        Pb = [sb(f"P{r}", [P, PW]) for r in range(3)]
        PT = [sb(f"PT{r}", [P, HG, PW]) for r in range(2)]
        OT = [sb(f"OT{j}", [P, C, S], F32R) for j in range(2)]
        nmax = sb("nmax", [P, 3, QT])
        rsum = sb("rsum", [P, 3, QT])
        rinv = sb("rinv", [P, 3, QT])
        norm = [InverseStd(nc, sb, sem, f"_{of}", norm_constants) for of in ("x", "projection", "x1")]
        lgT = y[0:R, 0, :]

        bank = [ctx.enter_context(nc.psum_tensor(f"at_bank{i}", [P, 512], F32)) for i in range(8)]
        S_ps, T_ps, A_ps = bank[0:4], bank[4:7], bank[7]
        O_ps = [bank[4], bank[5], bank[6], bank[7]]

        w_in, w_split = sem("w_in"), sem("w_split")
        b_in = sem("b_in")
        x_in_s, x_res_s = sem("x_in_s"), sem("x_res_s")
        q_moved = [sem(f"q_moved{c}") for c in range(C)]
        q_spilled = [sem(f"q_spilled{c}") for c in range(C)]
        k_moved = sem("k_moved")
        q_dram = nc.dram_tensor("q_dram", (2, C, P, S), F32, kind="Internal").ap()
        x1_stored, xn_stored = sem("x1_stored"), sem("xn_stored")
        scores, transposed, mixed, projected = sem("scores"), sem("transposed"), sem("mixed"), sem("projected")
        xT1_ps, qkv_ps, v_ps, xT2_ps = sem("xT1_ps"), sem("qkv_ps"), sem("v_ps"), sem("xT2_ps")
        rt_ps, lg_ps = sem("rt_ps"), sem("lg_ps")
        halved, inverted = sem("halved"), sem("inverted")
        max_ready, p_scaled, xT1_lo, xT2_lo, OT_lo = (sem("max_ready"), sem("p_scaled"), sem("xT1_lo"),
                                                      sem("xT2_lo"), sem("OT_lo"))
        qkv_lo, v_ready, y_ready, lg_ready = sem("qkv_lo"), sem("v_ready"), sem("y_ready"), sem("lg_ready")
        p_ready, pt_ready, xT1_hi, xT2_hi, OT_hi = (sem("p_ready"), sem("pt_ready"), sem("xT1_hi"),
                                                    sem("xT2_hi"), sem("OT_hi"))
        qkv_hi, x_normed, y_normed, xn_ready, lgT_ready = (sem("qkv_hi"), sem("x_normed"), sem("y_normed"),
                                                           sem("xn_ready"), sem("lgT_ready"))
        x1_ready = sem("x1_ready")

        POFF = [i * (i + 1) // 2 * P for i in range(QT)]
        TBANK = [(0, 0), (1, 0), (2, 0), (1, (QT - 1) * P)]
        TOFF = [0, QT * P, 2 * QT * P, (2 * QT - 1) * P]
        TW = [QT * P, QT * P, 2 * P]
        TFROM = [0, QT * P, 2 * QT * P]
        AV_STEP = [HG * g + HG + 2 for g in range(C)]

        block = ctx.enter_context(nc.Block())

        def turns(engine, turn):
            turn(0, True, False)
            with engine.Fori(1, NB - 1) as b:
                turn(b, False, False)
            turn(NB - 1, False, True)

        def seq(dram, b):
            return dram[bass.ds(b, 1)].rearrange("o p t d -> p (o t) d")

        @block.sync
        def _(sp):
            sp.dma_start(y[:], wq).then_inc(w_in, 16)
            sp.dma_start(xn2[:], wo).then_inc(w_in, 16)
            sp.dma_start(x_in[:], seq(x, 0)).then_inc(x_in_s, 16)
            sp.dma_start(x_res[:, :, 0:2 * HD], wvk).then_inc(w_in, 16)
            sp.dma_start(x_res[:, :, 2 * HD:2 * HD + R], wr).then_inc(w_in, 16)
            sp.dma_start(qb_s[:], qb).then_inc(b_in, 16)
            sp.dma_start(vkb_s[:], vkb).then_inc(b_in, 16)
            sp.dma_start(ob_s[:], ob.partition_broadcast(P)).then_inc(b_in, 16)

            def store_x1(n):
                sp.wait_ge(x1_ready, QT * n + QT)
                sp.dma_start(seq(x1_out, n), y[:]).then_inc(x1_stored, 16)

            def store_xn(n):
                sp.wait_ge(xn_ready, QT * n + QT)
                sp.dma_start(seq(xn_out, n), xn2[:]).then_inc(xn_stored, 16)

            def move_qkv(n):
                sp.wait_ge(qkv_lo, 5 * n + 1)
                for at, half in ((0, 0), (1, 0), (2, 1)):
                    sp.dma_start(Ks[HD * at:HD * at + HD, :].bitcast(F32),
                                 vk_h[half][HD:2 * HD, :].bitcast(F32)).then_inc(k_moved, 16)
                for c in range(C + 1):
                    if c < C:
                        sp.wait_ge(qkv_lo, 5 * n + 2 + c)
                        for half in range(2):
                            sp.dma_start(q_dram[half, c], q_h[c % 2][half][:].bitcast(F32)).then_inc(q_spilled[c], 16)
                    if c > 0:
                        sp.wait_ge(q_spilled[c - 1], 32 * n + 32)
                        for at, half in ((0, 0), (1, 1), (2, 0)):
                            sp.dma_start(Qs[HD * at:HD * at + HD, HG * (c - 1):HG * c, :].bitcast(F32),
                                         q_dram[half, c - 1].rearrange("(g d) t -> d g t", g=HG)
                                         ).then_inc(q_moved[c - 1], 16)

            move_qkv(0)
            sp.wait_ge(w_split, 4)
            sp.dma_start(x_res[:], seq(x, 0)).then_inc(x_res_s, 16)

            def turn(b, first, last):
                if not last:
                    sp.wait_ge(xT1_ps, C * b + C)
                    sp.dma_start(x_in[:], seq(x, b + 1)).then_inc(x_in_s, 16)
                if not first:
                    sp.wait_ge(x1_ready, QT * b)
                    sp.dma_start(x_res[:], seq(x, b)).then_inc(x_res_s, 16)
                    store_x1(b - 1)
                    store_xn(b - 1)
                if not last:
                    sp.wait_ge(scores, H * QT * b + H * QT)
                    move_qkv(b + 1)

            turns(sp, turn)
            store_x1(NB - 1)
            store_xn(NB - 1)
            sp.wait_ge(x1_stored, 16 * NB)
            sp.wait_ge(xn_stored, 16 * NB)

        @block.tensor
        def _(pe):
            def split_product(out, w, x_, cols, xcols):
                n = 0
                for c in range(C):
                    for i, j in PASSES:
                        last = nc.tensor.matmul(out, w[i][:, c, cols], x_[j][:, c, xcols],
                                                start=(n == 0), stop=(n == 3 * C - 1))
                        n += 1
                return last

            def transpose_x(src, c, out, done):
                for t in range(QT):
                    last = nc.tensor.transpose(out[:, t * P:(t + 1) * P], src[:, t, c * P:(c + 1) * P], idf[:])
                last.then_inc(done, 1)

            def project_qkv(n, u, start=False):
                if u == 0:
                    pe.wait_ge(xT1_lo, C * n + C)
                    if start:
                        pe.wait_ge(w_split, 4)
                if u == 4:
                    pe.wait_ge(qkv_lo, 5 * n + 1)
                if u == 0:
                    last = split_product(S_ps[0][0:2 * HD, :], wvk_s, xT, slice(0, 2 * HD), slice(0, S))
                else:
                    last = split_product(S_ps[u % 4][:], wq_s, xT, slice((u - 1) * P, u * P), slice(0, S))
                last.then_inc(qkv_ps, 1)

            def transpose_v(n):
                pe.wait_ge(pt_ready, 3 * H * n)
                pe.wait_ge(qkv_lo, 5 * n + 1)
                for j in range(QT):
                    last = nc.tensor.matmul(T_ps[0][:, j * HD:(j + 1) * HD], vk[0:HD, j * P:(j + 1) * P],
                                            idf[0:HD, 0:HD], start=True, stop=True)
                last.then_inc(v_ps, 1)

            pe.wait_ge(x_normed, QT)
            for c in range(C):
                transpose_x(x_in, c, S_ps[c], xT1_ps)
            for u in range(5):
                project_qkv(0, u, True)
            transpose_v(0)

            def transpose_xn(n):
                pe.wait_ge(xn_ready, QT * n + QT)
                for c in range(C):
                    transpose_x(xn2, c, S_ps[c], xT2_ps)

            def route(n):
                pe.wait_ge(xT2_lo, C * n + C)
                split_product(S_ps[0][0:R, :], wr_s, xT, slice(0, R), slice(0, S)).then_inc(rt_ps, 1)
                pe.wait_ge(lgT_ready, n + 1)
                for t in range(QT):
                    last = nc.tensor.matmul(S_ps[2][:, t * R:(t + 1) * R], lgT[:, t * P:(t + 1) * P],
                                            idf[0:R, 0:R], start=True, stop=True)
                last.then_inc(lg_ps, 1)

            def turn(b, first, last):
                for s in range(H + 3):
                    if s < H:
                        if s == 0:
                            pe.wait_ge(k_moved, 48 * b + 48)
                            pe.wait_ge(v_ready, b + 1)
                            if not first:
                                pe.wait_ge(lg_ready, b - 1)
                        if s % HG == 0:
                            pe.wait_ge(q_moved[s // HG], 48 * b + 48)
                        for i in range(QT):
                            if s > 0:
                                pe.wait_ge(p_ready, H * QT * b + QT * (s - 1) + i + 1)
                            n = (i + 1) * P
                            nc.tensor.matmul(S_ps[i][:, 0:n], Qs[:, s, i * P:(i + 1) * P], Ks[:, 0:n],
                                             start=True, stop=False)
                            nc.tensor.matmul(S_ps[i][:, i * P:n], idb[:], mask[:],
                                             start=False, stop=True).then_inc(scores, 1)
                    if s == H and not last:
                        pe.wait_ge(x_normed, QT * b + 2 * QT)
                        pe.wait_ge(p_ready, H * QT * b + H * QT)
                        for c in range(C):
                            transpose_x(x_in, c, S_ps[c], xT1_ps)
                    if 2 <= s < H + 2:
                        h = s - 2
                        pe.wait_ge(p_scaled, H * b + h + 1)
                        for tb, tiles in ((0, (0,)), (1, (1, 3)), (2, (2,))):
                            if h > 0:
                                pe.wait_ge(pt_ready, 3 * H * b + 3 * (h - 1) + tb + 1)
                            elif not first:
                                pe.wait_ge(y_ready, QT * b)
                            for j in tiles:
                                for i in range(j, QT):
                                    col = TBANK[j][1] + (i - j) * P
                                    src = POFF[i] + j * P
                                    lastt = nc.tensor.transpose(T_ps[tb][:, col:col + P],
                                                                Pb[h % 3][:, src:src + P], idf[:])
                            lastt.then_inc(transposed, 1)
                    if s == H and not last:
                        project_qkv(b + 1, 0)
                        project_qkv(b + 1, 1)
                    if s == H + 1 and not last:
                        for u in (2, 3, 4):
                            project_qkv(b + 1, u)
                    if s in AV_STEP:
                        g = AV_STEP.index(s)
                        pe.wait_ge(pt_ready, 3 * H * b + 3 * HG * (g + 1))
                        if not first:
                            if g == 0:
                                pe.wait_ge(y_ready, QT * b)
                        if g > 0:
                            pe.wait_ge(OT_lo, C * b + g)
                        for j in range(QT):
                            for k in range(HG):
                                lastt = nc.tensor.matmul(
                                    A_ps[HD * k:HD * k + HD, j * P:S], V[:, j, :],
                                    PT[g % 2][:, k, TOFF[j]:TOFF[j] + (QT - j) * P],
                                    start=(j == 0), stop=(j == QT - 1), tile_position=(0, HD * k))
                        lastt.then_inc(mixed, 1)
                if not first:
                    if not last:
                        pe.wait_ge(qkv_lo, 5 * b + 10)
                    else:
                        pe.wait_ge(p_ready, H * QT * b + H * QT)
                    transpose_xn(b - 1)
                if not last:
                    transpose_v(b + 1)
                for c in range(C):
                    pe.wait_ge(OT_lo, C * b + c + 1)
                    if c == 0 and not last:
                        pe.wait_ge(v_ready, b + 2)
                    for i in range(QT):
                        if c == 0 and i == QT - 1:
                            pe.wait_ge(OT_lo, C * b + C)
                        for n, (j, k) in enumerate(PASSES):
                            lastt = nc.tensor.matmul(O_ps[i][:], OT[j][:, c, i * P:(i + 1) * P], wo_s[k][:, c, :],
                                                     start=(c == 0 and n == 0), stop=(c == C - 1 and n == 2))
                        if c == C - 1:
                            lastt.then_inc(projected, 1)
                if not first:
                    route(b - 1)

            turns(pe, turn)
            pe.wait_ge(lg_ready, NB - 1)
            transpose_xn(NB - 1)
            route(NB - 1)

        @block.vector
        def _(dve):
            dve.wait_ge(b_in, 48)
            nc.vector.memset(vks_s[HD:2 * HD, :], SCALE)
            nc.vector.memset(vks_s[0:HD, :], 1.0).then_inc(w_split, 1)
            dve.wait_ge(w_split, 1)
            nc.vector.tensor_tensor(vkbs_s[:], vkb_s[:], vks_s[:], ALU.mult).then_inc(w_split, 1)

            def whole_norm(k, n, src, ready):
                for i in range(QT):
                    dve.wait_ge(ready, QT * n + i + 1)
                    norm[k].row_stats(src, i)
                norm[k].await_stats(n)
                norm[k].aggregate()
                norm[k].halve(n)
                norm[k].shift_bits(n)
                norm[k].guess(n)

            def low_x(n, c, ps, hi_sem, lo_sem):
                dve.wait_ge(hi_sem, C * n + c + 1)
                nc.vector.tensor_tensor(xT[1][:, c, :], ps[:], xT[0][:, c, :].bitcast(F32),
                                        ALU.subtract).then_inc(lo_sem, 1)

            def low_qkv(n, u):
                dve.wait_ge(qkv_hi, 5 * n + u + 1)
                if u == 0:
                    nc.vector.tensor_copy(vk_h[0][:], vk[:]).then_inc(halved, 1)
                    dve.wait_ge(halved, n + 2)
                    nc.vector.tensor_tensor(vk_h[1][:], vk[:], vk_h[0][:].bitcast(F32),
                                            ALU.subtract).then_inc(qkv_lo, 1)
                else:
                    r = (u - 1) % 2
                    nc.vector.scalar_tensor_tensor(out=q_h[r][1][:], in0=S_ps[u % 4][:], scalar=qb_s[:, u - 1:u],
                                                   in1=q_h[r][0][:].bitcast(F32), op0=ALU.add,
                                                   op1=ALU.subtract).then_inc(qkv_lo, 1)

            def take_v(n):
                dve.wait_ge(v_ps, n + 1)
                nc.vector.tensor_copy(V[:], T_ps[0][:, 0:QT * HD].rearrange("p (t d) -> p t d", t=QT)).then_inc(v_ready, 1)

            dve.wait_ge(x_in_s, 16)
            for i in range(QT):
                norm[0].row_stats(x_in, i)
            norm[0].await_stats(0)
            norm[0].aggregate()
            norm[0].halve(0)
            norm[0].shift_bits(0)
            norm[0].guess(0)
            dve.wait_ge(w_in, 64)
            for src, dst in ((y[:], wq_s), (xn2[:], wo_s), (x_res[:, :, 0:2 * HD], wvk_s),
                             (x_res[:, :, 2 * HD:2 * HD + R], wr_s)):
                last = nc.vector.tensor_copy(dst[0][:], src)
            last.then_inc(halved, 1)
            dve.wait_ge(halved, 1)
            for src, dst in ((y[:], wq_s), (xn2[:], wo_s), (x_res[:, :, 0:2 * HD], wvk_s),
                             (x_res[:, :, 2 * HD:2 * HD + R], wr_s)):
                last = nc.vector.tensor_tensor(dst[1][:], src, dst[0][:].bitcast(F32), ALU.subtract)
            last.then_inc(w_split, 2)
            for c in range(C):
                low_x(0, c, S_ps[c], xT1_hi, xT1_lo)
            for u in range(5):
                low_qkv(0, u)
            take_v(0)

            def take_projection(n):
                dve.wait_ge(x1_stored, 16 * n)
                dve.wait_ge(xn_ready, QT * n)
                dve.wait_ge(projected, QT * n + QT)
                for i in range(QT):
                    last = nc.vector.tensor_tensor(y[:, i, :], O_ps[i][:], ob_s[:], ALU.add)
                    last.then_inc(y_ready, 1)

            def take_logits(n):
                dve.wait_ge(lg_ps, n + 1)
                nc.vector.tensor_copy(logits[:, bass.ds(QT * n, QT), :],
                                      S_ps[2][:, 0:QT * R].rearrange("p (t r) -> p t r", t=QT)).then_inc(lg_ready, 1)

            def low_mixed(n, g):
                dve.wait_ge(OT_hi, C * n + g + 1)
                nc.vector.tensor_tensor(OT[1][:, g, :], A_ps[:], OT[0][:, g, :].bitcast(F32),
                                        ALU.subtract).then_inc(OT_lo, 1)

            def invert(n, h):
                dve.wait_ge(p_ready, H * QT * n + QT * h + QT)
                nc.vector.reciprocal(rinv[:, h % 3, :], rsum[:, h % 3, :]).then_inc(inverted, 1)

            def turn(b, first, last):
                if not first:
                    take_projection(b - 1)
                for s in range(H + 1):
                    norms = []
                    if not first:
                        norms += [(1, b - 1, y, y_ready, 0), (2, b - 1, y, x1_ready, 8)]
                    if not last:
                        norms.append((0, b + 1, x_in, x_in_s, 4))
                    if s < H:
                        ending = [(k, n) for k, n, _, _, at in norms if s == at + QT]
                        for i in range(QT):
                            if i == 0:
                                for k, n in ending:
                                    norm[k].await_stats(n)
                            dve.wait_ge(scores, H * QT * b + QT * s + i + 1)
                            nc.vector.tensor_reduce(nmax[:, s % 3, i:i + 1], S_ps[i][:, 0:(i + 1) * P], AX_X,
                                                    ALU.max, negate=True).then_inc(max_ready, 1)
                            if i == 1 and s >= 1:
                                invert(b, s - 1)
                            for k, n in ending:
                                if i == 0:
                                    norm[k].aggregate()
                                elif i == 1:
                                    norm[k].halve(n)
                                elif i == 2:
                                    norm[k].shift_bits(n)
                                else:
                                    norm[k].guess(n)
                    if s >= 1:
                        h = s - 1
                        if s == H:
                            invert(b, h)
                        dve.wait_ge(inverted, H * b + h + 1)
                        for i in range(QT):
                            o = POFF[i]
                            last_ = nc.vector.tensor_scalar(Pb[h % 3][:, o:o + (i + 1) * P],
                                                            Pb[h % 3][:, o:o + (i + 1) * P],
                                                            rinv[:, h % 3, i:i + 1], None, ALU.mult)
                        last_.then_inc(p_scaled, 1)
                    for k, n, src, ready, at in norms:
                        if at <= s < at + QT:
                            i = s - at
                            dve.wait_ge(ready, 16 * n + 16 if k == 0 else QT * n + i + 1)
                            norm[k].row_stats(src, i)
                    if s - 1 in AV_STEP[:3]:
                        low_mixed(b, AV_STEP.index(s - 1))
                if not last:
                    for c in range(C):
                        low_x(b + 1, c, S_ps[c], xT1_hi, xT1_lo)
                    for u in range(5):
                        low_qkv(b + 1, u)
                low_mixed(b, 3)
                if not first:
                    for c in range(C):
                        low_x(b - 1, c, S_ps[c], xT2_hi, xT2_lo)
                if not last:
                    take_v(b + 1)
                if not first:
                    take_logits(b - 1)

            turns(dve, turn)
            take_projection(NB - 1)
            whole_norm(1, NB - 1, y, y_ready)
            whole_norm(2, NB - 1, y, x1_ready)
            for c in range(C):
                low_x(NB - 1, c, S_ps[c], xT2_hi, xT2_lo)
            take_logits(NB - 1)

        @block.scalar
        def _(act):
            def normalize(dst, src, k, n, i, done):
                act.wait_ge(norm[k].ready, n + 1)
                nc.scalar.activation(dst[:, i, :], src[:, i, :], ACT.Identity, bias=norm[k].bias[:, i:i + 1],
                                     scale=norm[k].rstd[:, i:i + 1]).then_inc(done, 1)

            def high_x(n, c, ps, ps_sem, hi_sem):
                act.wait_ge(ps_sem, C * n + c + 1)
                nc.scalar.activation(xT[0][:, c, :], ps[:], ACT.Copy).then_inc(hi_sem, 1)

            def high_qkv(n, u, start=False):
                act.wait_ge(qkv_ps, 5 * n + u + 1)
                if u == 0:
                    if start:
                        act.wait_ge(w_split, 2)
                    else:
                        act.wait_ge(k_moved, 48 * n)
                    nc.scalar.activation(vk[:], S_ps[0][0:2 * HD, :], ACT.Identity, bias=vkbs_s[:],
                                         scale=vks_s[:]).then_inc(qkv_hi, 1)
                else:
                    if u > 2:
                        act.wait_ge(q_spilled[u - 3], 32 * n + 32)
                    elif not start:
                        act.wait_ge(q_spilled[u + 1], 32 * n)
                    nc.scalar.activation(q_h[(u - 1) % 2][0][:], S_ps[u % 4][:], ACT.Identity,
                                         bias=qb_s[:, u - 1:u]).then_inc(qkv_hi, 1)

            for i in range(QT):
                normalize(x_in, x_in, 0, 0, i, x_normed)
            for c in range(C):
                high_x(0, c, S_ps[c], xT1_ps, xT1_hi)
            for u in range(5):
                high_qkv(0, u, True)

            def high_mixed(n, g, start=False):
                act.wait_ge(mixed, C * n + g + 1)
                if g == 0 and not start:
                    act.wait_ge(projected, QT * n)
                nc.scalar.activation(OT[0][:, g, :], A_ps[:], ACT.Copy).then_inc(OT_hi, 1)

            def take_lgT(n):
                act.wait_ge(rt_ps, n + 1)
                act.wait_ge(x1_stored, 16 * n + 16)
                nc.scalar.activation(lgT, S_ps[0][0:R, :], ACT.Copy).then_inc(lgT_ready, 1)

            def turn(b, first, last):

                def exp(s, i):
                    act.wait_ge(max_ready, H * QT * b + QT * s + i + 1)
                    if i == 0:
                        if s >= 3:
                            act.wait_ge(transposed, 3 * H * b + 3 * (s - 2))
                        elif not first:
                            act.wait_ge(transposed, 3 * H * b)
                    o = POFF[i]
                    nc.scalar.activation(Pb[s % 3][:, o:o + (i + 1) * P], S_ps[i][:, 0:(i + 1) * P], ACT.Exp,
                                         bias=nmax[:, s % 3, i:i + 1], scale=1.0,
                                         accum_out=rsum[:, s % 3, i:i + 1]).then_inc(p_ready, 1)

                def copy_pt(h, tb):
                    act.wait_ge(transposed, 3 * H * b + 3 * h + tb + 1)
                    g = h // HG
                    if h % HG == 0 and tb == 0:
                        if g >= 2:
                            act.wait_ge(mixed, C * b + g - 1)
                        elif not first:
                            act.wait_ge(mixed, C * b)
                    nc.scalar.activation(PT[g % 2][:, h % HG, TFROM[tb]:TFROM[tb] + TW[tb]],
                                         T_ps[tb][:, 0:TW[tb]], ACT.Copy).then_inc(pt_ready, 1)

                for s in range(H + 2):
                    if s < H:
                        exp(s, 0)
                        exp(s, 1)
                    if s - 1 in AV_STEP[:3]:
                        high_mixed(b, AV_STEP.index(s - 1), first)
                    if s == H and not last:
                        for c in range(C):
                            high_x(b + 1, c, S_ps[c], xT1_ps, xT1_hi)
                    if s >= 2:
                        copy_pt(s - 2, 0)
                    if s < H:
                        exp(s, 2)
                    if s >= 2:
                        copy_pt(s - 2, 1)
                    if s < H:
                        exp(s, 3)
                    if s >= 2:
                        copy_pt(s - 2, 2)
                    for i in (0, 1) if s % 2 == 0 else (2, 3):
                        if s in (6, 7) and not first:
                            normalize(y, y, 1, b - 1, i, y_normed)
                        if s in (10, 11) and not last:
                            normalize(x_in, x_in, 0, b + 1, i, x_normed)
                        if s in (14, 15) and not first:
                            act.wait_ge(xn_stored, 16 * b - 16)
                            normalize(xn2, y, 2, b - 1, i, xn_ready)
                    if s == H and not last:
                        high_qkv(b + 1, 0)
                        high_qkv(b + 1, 1)
                if not last:
                    for u in (2, 3, 4):
                        high_qkv(b + 1, u)
                high_mixed(b, 3)
                if not first:
                    for c in range(C):
                        high_x(b - 1, c, S_ps[c], xT2_ps, xT2_hi)
                    take_lgT(b - 1)

            turns(act, turn)
            for i in range(QT):
                normalize(y, y, 1, NB - 1, i, y_normed)
            act.wait_ge(xn_stored, 16 * NB - 16)
            for i in range(QT):
                normalize(xn2, y, 2, NB - 1, i, xn_ready)
            for c in range(C):
                high_x(NB - 1, c, S_ps[c], xT2_ps, xT2_hi)
            take_lgT(NB - 1)

        @block.gpsimd
        def _(pool):
            def add_residual(n):
                norm[1].refine(n)
                pool.wait_ge(x_res_s, 16 * n + 16)
                for i in range(QT):
                    pool.wait_ge(y_normed, QT * n + i + 1)
                    nc.gpsimd.tensor_tensor(y[:, i, :], y[:, i, :], x_res[:, i, :], ALU.add).then_inc(x1_ready, 1)

            def turn(b, first, last):
                if not first:
                    add_residual(b - 1)
                if not last:
                    norm[0].refine(b + 1)
                if not first:
                    norm[2].refine(b - 1)

            norm[0].refine(0)
            turns(pool, turn)
            add_residual(NB - 1)
            norm[2].refine(NB - 1)


def build_routing(nc, logits, gate, weight, slot, token_of_slot, tile_expert, idx_hi=None):
    ctx = ExitStack()
    with ctx:
        def sb(name, shape, dt=F32):
            return ctx.enter_context(nc.sbuf_tensor("ro_" + name, shape, dt))

        def sem(name):
            return ctx.enter_context(nc.semaphore("ro_" + name))

        first_place = sb("first_place", [P, E])
        slots_before = sb("slots_before", [P, E])
        tile_no = sb("tile_no", [P, NT])
        lane_no = sb("lane_no", [P, P])
        column_no = sb("column_no", [P, SC])
        token_no = sb("token_no", [P, NTT])
        before = sb("before", [P, P], BF16)
        ones = sb("ones", [P, P], BF16)
        top = sb("top", [P, 4, NTT])
        inv = sb("inv", [P, NTT])
        prob = sb("prob", [P, NTT, E])
        t1 = sb("t1", [P, NTT, E])
        t2 = sb("t2", [P, NTT, E])
        pick = [sb(f"pick{k}", [P, NTT, E]) for k in range(2)]
        picked = sb("picked", [P, NTT, E], BF16)
        count = [sb(f"count{k}", [P, NTT, E]) for k in range(2)]
        total = sb("total", [P, NTT, E])
        tiles = [sb(f"tiles{k}", [P, E]) for k in range(2)]
        over = sb("over", [P, NT, E])
        base = sb("base", [P, E])
        tile_e = sb("tile_e", [P, NT])
        place = sb("place", [P, 2, NTT])
        digit = sb("digit", [P, 2, 2, NTT], I32)
        digit_f = sb("digit_f", [P, 2, 2, NTT])
        lane_hot = [sb(f"lane_hot{k}", [P, P], F32R) for k in range(4)]
        column_hot = [sb(f"column_hot{k}", [P, SC], F32R) for k in range(4)]
        rank_ps = ctx.enter_context(nc.psum_tensor("ro_rank_ps", [P, NTT * E], F32))
        total_ps = ctx.enter_context(nc.psum_tensor("ro_total_ps", [P, NTT * E], F32))
        inverse_ps = ctx.enter_context(nc.psum_tensor("ro_inverse_ps", [P, 512], F32))

        constants, shifted, exponentials = sem("constants"), sem("shifted"), sem("exponentials")
        negated_gate, picks_ready, counted, hot, used, inverse_done = (
            sem("negated_gate"), sem("picks_ready"), sem("counted"), sem("hot"), sem("used"), sem("inverse_done"))
        own = sem("own")
        block = ctx.enter_context(nc.Block())

        def over_experts(ap):
            return ap.unsqueeze(2).to_broadcast([P, NTT, E])

        def over_tiles(ap):
            return ap.unsqueeze(1).to_broadcast([P, NTT, E])

        @block.gpsimd
        def _(pool):
            nc.gpsimd.iota(first_place[:], [[-1, E]], base=E, channel_multiplier=0, allow_small_or_imprecise_dtypes=True)
            nc.gpsimd.iota(slots_before[:], [[TS, E]], base=0, channel_multiplier=0, allow_small_or_imprecise_dtypes=True)
            nc.gpsimd.iota(tile_no[:], [[1, NT]], base=0, channel_multiplier=0, allow_small_or_imprecise_dtypes=True)
            nc.gpsimd.iota(lane_no[:], [[1, P]], base=0, channel_multiplier=0, allow_small_or_imprecise_dtypes=True)
            nc.gpsimd.iota(column_no[:], [[1, SC]], base=0, channel_multiplier=0, allow_small_or_imprecise_dtypes=True)
            nc.gpsimd.iota(token_no[:], [[P, NTT]], base=0, channel_multiplier=1, allow_small_or_imprecise_dtypes=True)
            nc.gpsimd.memset(ones[:], 1.0).then_inc(constants, 1)
            pool.wait_ge(constants, 1)
            nc.gpsimd.affine_select(out=before[:], in_=ones[:], compare_op=ALU.is_gt, fill=0.0, base=0,
                                    pattern=[[1, P]], channel_multiplier=-1).then_inc(constants, 1)

        @block.scalar
        def _(act):
            act.wait_ge(shifted, 1)
            nc.scalar.activation(prob[:], t1[:], ACT.Exp)
            nc.scalar.activation(gate[:], logits[:, :, E], ACT.Exp, scale=-1.0).then_inc(exponentials, 1)

        @block.tensor
        def _(pe):
            pe.wait_ge(constants, 2)
            pe.wait_ge(picks_ready, 1)
            nc.tensor.matmul(rank_ps[:], before[:], picked[:].rearrange("p t e -> p (t e)"), start=True, stop=True)
            nc.tensor.matmul(total_ps[:], ones[:], picked[:].rearrange("p t e -> p (t e)"),
                             start=True, stop=True).then_inc(counted, 1)
            for n in range(2 * NTT):
                pe.wait_ge(hot, n + 1)
                last = nc.tensor.matmul(inverse_ps[:, 0:SC], lane_hot[n % 4][:], column_hot[n % 4][:],
                                        start=(n == 0), stop=(n == 2 * NTT - 1))
                last.then_inc(used, 1)

        @block.vector
        def _(dve):
            steps = Steps(dve, own)
            dve.wait_ge(constants, 2)
            scores = logits[:, :, 0:E]
            steps.then_wait(nc.vector.tensor_reduce(top[:, 0, :], scores, AX_X, ALU.max))
            nc.vector.tensor_tensor(t1[:], scores, over_experts(top[:, 0, :]), ALU.subtract).then_inc(shifted, 1)
            dve.wait_ge(exponentials, 1)
            steps.then_wait(nc.vector.tensor_scalar(gate[:], gate[:], 1.0, None, ALU.add))
            nc.vector.reciprocal(gate[:], gate[:])
            steps.then_wait(nc.vector.tensor_reduce(top[:, 1, :], prob[:], AX_X, ALU.add))
            steps.then_wait(nc.vector.reciprocal(inv[:], top[:, 1, :]))
            steps.then_wait(nc.vector.tensor_tensor(prob[:], prob[:], over_experts(inv[:]), ALU.mult))
            for k in range(2):
                src = prob if k == 0 else t2
                steps.then_wait(nc.vector.tensor_reduce(top[:, 2 + k, :], src[:], AX_X, ALU.max))
                steps.then_wait(nc.vector.tensor_tensor(t1[:], src[:], over_experts(top[:, 2 + k, :]), ALU.is_equal))
                steps.then_wait(nc.vector.tensor_tensor(t1[:], t1[:], over_tiles(first_place[:]), ALU.mult))
                steps.then_wait(nc.vector.tensor_reduce(inv[:], t1[:], AX_X, ALU.max))
                steps.then_wait(nc.vector.tensor_tensor(pick[k][:], over_tiles(first_place[:]),
                                                        over_experts(inv[:]), ALU.is_equal))
                if k == 0:
                    steps.then_wait(nc.vector.scalar_tensor_tensor(out=t2[:], in0=pick[0][:], scalar=-2.0,
                                                                   in1=prob[:], op0=ALU.mult, op1=ALU.add))
            nc.vector.tensor_tensor(picked[:], pick[0][:], pick[1][:], ALU.add).then_inc(picks_ready, 1)
            steps.then_wait(nc.vector.tensor_tensor(top[:, 1, :], top[:, 2, :], top[:, 3, :], ALU.add))
            steps.then_wait(nc.vector.reciprocal(inv[:], top[:, 1, :]))
            nc.vector.tensor_tensor(weight[:, 0, :], top[:, 2, :], inv[:], ALU.mult)
            nc.vector.tensor_tensor(weight[:, 1, :], top[:, 3, :], inv[:], ALU.mult)
            dve.wait_ge(counted, 1)
            nc.vector.tensor_copy(count[0][:].rearrange("p t e -> p (t e)"), total_ps[:])
            steps.then_wait(nc.vector.tensor_copy(total[:].rearrange("p t e -> p (t e)"), total_ps[:]))
            a, shift = 0, 1
            while shift < NTT:
                nc.vector.tensor_copy(count[1 - a][:, 0:shift, :], count[a][:, 0:shift, :])
                steps.then_wait(nc.vector.tensor_tensor(count[1 - a][:, shift:, :], count[a][:, shift:, :],
                                                        count[a][:, 0:NTT - shift, :], ALU.add))
                a, shift = 1 - a, 2 * shift
            n_of = count[a][:, NTT - 1, :]
            steps.then_wait(nc.vector.tensor_tensor(over[:, 0:E, :], n_of.unsqueeze(2).to_broadcast([P, E, E]),
                                                    slots_before[:].unsqueeze(1).to_broadcast([P, E, E]), ALU.is_gt))
            steps.then_wait(nc.vector.tensor_reduce(tiles[0][:], over[:, 0:E, :], AX_X, ALU.add))
            steps.then_wait(nc.vector.tensor_copy(base[:], tiles[0][:]))
            b, shift = 0, 1
            while shift < E:
                nc.vector.tensor_copy(tiles[1 - b][:, 0:shift], tiles[b][:, 0:shift])
                steps.then_wait(nc.vector.tensor_tensor(tiles[1 - b][:, shift:], tiles[b][:, shift:],
                                                        tiles[b][:, 0:E - shift], ALU.add))
                b, shift = 1 - b, 2 * shift
            end = tiles[b]
            steps.then_wait(nc.vector.tensor_tensor(over[:], tile_no[:].unsqueeze(2).to_broadcast([P, NT, E]),
                                                    end[:].unsqueeze(1).to_broadcast([P, NT, E]), ALU.is_ge))
            steps.then_wait(nc.vector.tensor_reduce(tile_e[:], over[:], AX_X, ALU.add))
            nc.vector.tensor_scalar(tile_expert[:], tile_e[0:1, :], float(E - 1), None, ALU.min)
            steps.then_wait(nc.vector.tensor_tensor(base[:], end[:], base[:], ALU.subtract))
            steps.then_wait(nc.vector.tensor_scalar(base[:], base[:], float(TS), None, ALU.mult))
            steps.then_wait(nc.vector.tensor_tensor(t1[:], count[a][:], total[:], ALU.subtract))
            steps.then_wait(nc.vector.tensor_tensor(t1[:], t1[:], over_tiles(base[:]), ALU.add))
            steps.then_wait(nc.vector.tensor_tensor(t1[:].rearrange("p t e -> p (t e)"),
                                                    t1[:].rearrange("p t e -> p (t e)"), rank_ps[:], ALU.add))
            for k in range(2):
                steps.then_wait(nc.vector.tensor_tensor(t2[:], pick[k][:], t1[:], ALU.mult))
                steps.then_wait(nc.vector.tensor_reduce(place[:, k, :], t2[:], AX_X, ALU.add))
            steps.then_wait(nc.vector.tensor_copy(slot[:], place[:]))
            nc.vector.tensor_scalar(digit[:, 0], slot[:], 7, None, ALU.logical_shift_right)
            steps.then_wait(nc.vector.tensor_scalar(digit[:, 1], slot[:], P - 1, None, ALU.bitwise_and))
            steps.then_wait(nc.vector.tensor_copy(digit_f[:], digit[:]))
            for n in range(2 * NTT):
                k, t = divmod(n, NTT)
                if n >= 4:
                    dve.wait_ge(used, n - 3)
                nc.vector.tensor_scalar(lane_hot[n % 4][:], lane_no[:], digit_f[:, 1, k, t:t + 1],
                                        token_no[:, t:t + 1], ALU.is_equal, ALU.mult)
                nc.vector.tensor_scalar(column_hot[n % 4][:], column_no[:], digit_f[:, 0, k, t:t + 1], None,
                                        ALU.is_equal).then_inc(hot, 1)
            dve.wait_ge(used, 2 * NTT)
            nc.vector.tensor_copy(token_of_slot[:], inverse_ps[:, 0:SC]).then_inc(inverse_done, 1)
            dve.wait_ge(inverse_done, 1)


class GatedProducts:

    def __init__(self, nc, pe, rows, xT, act, gate_up_ps, out_ps, sems):
        self.nc, self.pe, self.rows, self.xT, self.act = nc, pe, rows, xT, act
        self.gate_up_ps, self.out_ps, self.s = gate_up_ps, out_ps, sems
        self.NC = len(rows)

    def gate_up(self, n, c, gate_cols, up_cols):
        pe, m = self.pe, self.rows[c]
        if c >= 2:
            pe.wait_ge(self.s["act_ready"], self.NC * n + c - 1)
        for which, cols in enumerate((gate_cols, up_cols)):
            step = 0
            for k in range(C):
                for i, j in PASSES:
                    last = self.nc.tensor.matmul(self.gate_up_ps[c % 2][which][0:m, :], cols(i, k), self.xT[j][:, k, :],
                                                 start=(step == 0), stop=(step == 3 * C - 1))
                    step += 1
        last.then_inc(self.s["gate_up_done"], 1)

    def down(self, n, c, weights):
        pe, m = self.pe, self.rows[c]
        if c == 0:
            pe.wait_ge(self.s["out_taken"], QT * n)
        pe.wait_ge(self.s["act_ready"], self.NC * n + c + 1)
        for i in range(QT):
            for step, (j, k) in enumerate(PASSES):
                last = self.nc.tensor.matmul(self.out_ps[i][:], self.act[c % 2][j][0:m, i * P:(i + 1) * P], weights(k),
                                             start=(c == 0 and step == 0), stop=(c == self.NC - 1 and step == 2))
            if c == self.NC - 1:
                last.then_inc(self.s["out_done"], 1)
        if c < self.NC - 1:
            last.then_inc(self.s["down_done"], 1)

    def transpose_x(self, src, c, idf):
        ps = self.gate_up_ps[1 - c // 2][c % 2]
        for t in range(QT):
            last = self.nc.tensor.transpose(ps[:, t * P:(t + 1) * P], src[:, t, c * P:(c + 1) * P], idf[:])
        last.then_inc(self.s["xT_done"], 1)


def high_x(nc, n, c, xT, gate_up_ps, s):
    nc.scalar.wait_ge(s["xT_done"], C * n + c + 1)
    nc.scalar.activation(xT[0][:, c, :], gate_up_ps[1 - c // 2][c % 2][:], ACT.Copy).then_inc(s["xT_hi"], 1)


def low_x(nc, n, c, xT, gate_up_ps, s):
    nc.vector.wait_ge(s["xT_hi"], C * n + c + 1)
    nc.vector.tensor_tensor(xT[1][:, c, :], gate_up_ps[1 - c // 2][c % 2][:], xT[0][:, c, :].bitcast(F32),
                            ALU.subtract).then_inc(s["xT_lo"], 1)


def gate_silu(nc, n, c, rows, silu, gate_up_ps, s):
    NC, m = len(rows), rows[c]
    nc.scalar.wait_ge(s["gate_up_done"], NC * n + c + 1)
    nc.scalar.wait_ge(s["act_ready"], NC * n + max(c - 1, 0))
    nc.scalar.activation(silu[c % 2][0:m, :], gate_up_ps[c % 2][0][0:m, :], ACT.Silu).then_inc(s["silu_ready"], 1)


def gate_times_up(nc, n, c, rows, silu, act, gate_up_ps, s):
    NC, m = len(rows), rows[c]
    nc.vector.wait_ge(s["silu_ready"], NC * n + c + 1)
    nc.vector.tensor_tensor(silu[c % 2][0:m, :], silu[c % 2][0:m, :], gate_up_ps[c % 2][1][0:m, :],
                            ALU.mult).then_inc(s["product"], 1)
    nc.vector.wait_ge(s["product"], 2 * (NC * n + c) + 1)
    if c >= 2:
        nc.vector.wait_ge(s["down_done"], (NC - 1) * n + c - 1)
    else:
        nc.vector.wait_ge(s["out_done"], QT * n)
    nc.vector.tensor_copy(act[c % 2][0][0:m, :], silu[c % 2][0:m, :]).then_inc(s["product"], 1)
    nc.vector.wait_ge(s["product"], 2 * (NC * n + c) + 2)
    nc.vector.tensor_tensor(act[c % 2][1][0:m, :], silu[c % 2][0:m, :], act[c % 2][0][0:m, :].bitcast(F32),
                            ALU.subtract).then_inc(s["act_ready"], 1)


GATED_SEMS = ("xT_done", "xT_hi", "xT_lo", "gate_up_done", "silu_ready", "product", "act_ready", "down_done",
              "out_done", "out_taken")


def build_experts(nc, xn, gu, dn, ys, token_of_slot, tile_expert, idf):
    ctx = ExitStack()
    with ctx:
        def sb(name, shape, dt=F32):
            return ctx.enter_context(nc.sbuf_tensor("ex_" + name, shape, dt))

        def sem(name):
            return ctx.enter_context(nc.semaphore("ex_" + name))

        rows = [P] * (I_MOE // P) + [I_MOE % P]
        NC = len(rows)
        gu_in = sb("gu_in", [P, C, 2 * I_MOE])
        dn_in = sb("dn_in", [P, NC, D])
        gu_s = [[sb(f"gu{r}{j}", [P, C, 2 * I_MOE], F32R) for j in range(2)] for r in range(2)]
        dn_s = [[sb(f"dn{r}{j}", [P, NC, D], F32R) for j in range(2)] for r in range(2)]
        xg = [sb(f"xg{r}", [P, QT, D]) for r in range(2)]
        index = [sb(f"index{r}", [P, QT], U32) for r in range(2)]
        xT = [sb(f"xT{j}", [P, C, TS], F32R) for j in range(2)]
        silu = [sb(f"silu{r}", [P, TS]) for r in range(2)]
        act_s = [[sb(f"act{r}{j}", [P, TS], F32R) for j in range(2)] for r in range(2)]
        y_out = sb("y_out", [P, QT, D])
        bank = [ctx.enter_context(nc.psum_tensor(f"ex_bank{i}", [P, 512], F32)) for i in range(8)]
        gate_up_ps, out_ps = [bank[0:2], bank[2:4]], bank[4:8]
        s = {name: sem(name) for name in GATED_SEMS}
        w_in, w_hi, w_lo, w_free = sem("w_in"), sem("w_hi"), sem("w_lo"), sem("w_free")
        gathered = [sem(f"gathered{r}") for r in range(2)]
        index_ready, stored = [sem(f"index_ready{r}") for r in range(2)], sem("stored")
        PIECES = [(0, k) for k in range(C)] + [(1, c) for c in range(NC)]
        TURN = [PIECES[0:3], PIECES[3:5], PIECES[5:7]]
        WN = len(PIECES)

        def piece(which, k, src, halves, j=None):
            m = P if which == 0 else rows[k]
            t = (src[which] if j is None else halves[which][j])
            return t[0:m, k, :]

        block = ctx.enter_context(nc.Block())

        def turns(engine, turn):
            with engine.Fori(0, NT // 2) as pair:
                turn(2 * pair, 0, False)
                turn(2 * pair + 1, 1, False)
            turn(NT - 1, 0, True)

        @block.sync
        def _(sp):
            def load(n):
                e = sp.value_load(tile_expert[0:1, bass.ds(n, 1)], min_val=0, max_val=E - 1)
                sp.dma_start(gu_in[:], gu[bass.ds(e, 1)].rearrange("o p k i -> p (o k) i")).then_inc(w_in, 16)
                full = NC - 1
                sp.dma_start(dn_in[:, 0:full, :], dn[bass.ds(e, 1), 0:full * P].rearrange(
                    "o (c p) d -> p (o c) d", p=P)).then_inc(w_in, 16)
                sp.dma_start(dn_in[0:rows[-1], full, :], dn[bass.ds(e, 1), full * P:I_MOE].rearrange(
                    "o p d -> (o p) d")).then_inc(w_in, 16)

            load(0)

            def turn(n, r, last):
                if not last:
                    sp.wait_ge(w_lo, WN * n + WN)
                    load(n + 1)
                sp.wait_ge(s["out_taken"], QT * n + QT)
                sp.dma_start(ys[bass.ds(n, 1)].rearrange("o p t d -> p (o t) d"), y_out[:]).then_inc(stored, 16)

            turns(sp, turn)
            sp.wait_ge(stored, 16 * NT)

        @block.gpsimd
        def _(pool):
            def gather(n, r, uses):
                nc.gpsimd.tensor_copy(index[r][:], token_of_slot[:, bass.ds(QT * n, QT)]).then_inc(index_ready[r], 1)
                pool.wait_ge(index_ready[r], 1)
                pool.wait_ge(index_ready[r], uses)
                for t in range(QT):
                    pool.indirect_dma_start(out=xg[r][:, t, :], out_offset=None, in_=xn,
                                            in_offset=bass.IndirectOffsetOnAxis(ap=index[r][:, t:t + 1], axis=0)
                                            ).then_inc(gathered[r], 16)

            gather(0, 0, 1)
            gather(1, 1, 1)
            with pool.Fori(2, NT // 2 + 1) as uses:
                pool.wait_ge(s["xT_done"], 2 * C * uses - 3 * C)
                gather(2 * uses - 2, 0, uses)
                pool.wait_ge(s["xT_done"], 2 * C * uses - 2 * C)
                gather(2 * uses - 1, 1, uses)
            pool.wait_ge(s["xT_done"], C * (NT - 2))
            gather(NT - 1, 0, NT // 2 + 1)

        @block.tensor
        def _(pe):
            g = GatedProducts(nc, pe, rows, xT, act_s, gate_up_ps, out_ps, s)
            pe.wait_ge(gathered[0], 16 * QT)
            for c in range(C):
                g.transpose_x(xg[0], c, idf)

            def turn(n, r, last):
                def gate(c):
                    return lambda j, k: gu_s[r][j][:, k, c * P:c * P + rows[c]]

                def up(c):
                    return lambda j, k: gu_s[r][j][:, k, I_MOE + c * P:I_MOE + c * P + rows[c]]

                pe.wait_ge(s["xT_lo"], C * n + C)
                pe.wait_ge(w_lo, WN * n + WN)
                for c in range(NC):
                    g.gate_up(n, c, gate(c), up(c))
                    if c == NC - 1 and not last:
                        pe.wait_ge(gathered[1 - r], 16 * QT * ((n - r) // 2 + 1 + r) if isinstance(n, int)
                                   else 8 * QT * (n - r) + 16 * QT * (1 + r))
                        pe.wait_ge(s["act_ready"], NC * n + NC - 1)
                        g.transpose_x(xg[1 - r], 0, idf)
                        g.transpose_x(xg[1 - r], 1, idf)
                    if c > 0:
                        g.down(n, c - 1, lambda k: dn_s[r][k][0:rows[c - 1], c - 1, :])
                if not last:
                    pe.wait_ge(s["act_ready"], NC * n + NC)
                    g.transpose_x(xg[1 - r], 2, idf)
                    g.transpose_x(xg[1 - r], 3, idf)
                g.down(n, NC - 1, lambda k: dn_s[r][k][0:rows[NC - 1], NC - 1, :])

            turns(pe, turn)

        def split_hi(n, r, q):
            which, k = PIECES[q]
            nc.scalar.wait_ge(w_in, 48 * n + 48)
            nc.scalar.activation(piece(which, k, None, (gu_s[r], dn_s[r]), 0), piece(which, k, (gu_in, dn_in), None),
                                 ACT.Copy).then_inc(w_hi, 1)

        def split_lo(n, r, q):
            which, k = PIECES[q]
            nc.vector.wait_ge(w_hi, WN * n + q + 1)
            nc.vector.tensor_tensor(piece(which, k, None, (gu_s[r], dn_s[r]), 1), piece(which, k, (gu_in, dn_in), None),
                                    piece(which, k, None, (gu_s[r], dn_s[r]), 0).bitcast(F32),
                                    ALU.subtract).then_inc(w_lo, 1)

        @block.scalar
        def _(act):
            for q in range(WN):
                split_hi(0, 0, q)
            for c in range(C):
                high_x(nc, 0, c, xT, gate_up_ps, s)

            def turn(n, r, last):
                q = 0
                for c in range(NC):
                    gate_silu(nc, n, c, rows, silu, gate_up_ps, s)
                    if not last:
                        for _ in TURN[c]:
                            if q == 0:
                                act.wait_ge(s["out_done"], QT * n)
                            split_hi(n + 1, 1 - r, q)
                            q += 1
                if not last:
                    for c in range(C):
                        high_x(nc, n + 1, c, xT, gate_up_ps, s)
                act.wait_ge(stored, 16 * n)
                for i in range(QT):
                    act.wait_ge(s["out_done"], QT * n + i + 1)
                    nc.scalar.activation(y_out[:, i, :], out_ps[i][:], ACT.Copy).then_inc(s["out_taken"], 1)

            turns(act, turn)

        @block.vector
        def _(dve):
            for q in range(WN):
                split_lo(0, 0, q)
            for c in range(C):
                low_x(nc, 0, c, xT, gate_up_ps, s)

            def turn(n, r, last):
                q = 0
                for c in range(NC):
                    gate_times_up(nc, n, c, rows, silu, act_s, gate_up_ps, s)
                    if not last:
                        for _ in TURN[c]:
                            split_lo(n + 1, 1 - r, q)
                            q += 1
                if not last:
                    for c in range(C):
                        low_x(nc, n + 1, c, xT, gate_up_ps, s)

            turns(dve, turn)


def build_shared(nc, xn, shg, shu, shd, ys, x1, out, gate, weight, slot, idf, norm_constants):
    ctx = ExitStack()
    with ctx:
        def sb(name, shape, dt=F32):
            return ctx.enter_context(nc.sbuf_tensor("sh_" + name, shape, dt))

        def sem(name):
            return ctx.enter_context(nc.semaphore("sh_" + name))

        NC = I_SH // P
        rows = [P] * NC
        gate_s = [sb(f"gate{j}", [P, C, I_SH], F32R) for j in range(2)]
        up_s = [sb(f"up{j}", [P, C, I_SH], F32R) for j in range(2)]
        dn_s = [sb(f"dn{j}", [P, NC, D], F32R) for j in range(2)]
        x_in = sb("x_in", [P, QT, D])
        xT = [sb(f"xT{j}", [P, C, TS], F32R) for j in range(2)]
        silu = [sb(f"silu{r}", [P, TS]) for r in range(2)]
        act_s = [[sb(f"act{r}{j}", [P, TS], F32R) for j in range(2)] for r in range(2)]
        f = sb("f", [P, QT, D])
        yk = [sb(f"yk{k}", [P, QT, D]) for k in range(2)]
        index = sb("index", [P, 2, QT], U32)
        scales = sb("scales", [P, 3, QT])
        norm = InverseStd(nc, sb, sem, "", norm_constants)
        bank = [ctx.enter_context(nc.psum_tensor(f"sh_bank{i}", [P, 512], F32)) for i in range(8)]
        gate_up_ps, out_ps = [bank[0:2], bank[2:4]], bank[4:8]
        s = {name: sem(name) for name in GATED_SEMS}
        w_in, w_hi, w_lo = [sem(f"w_in{r}") for r in range(2)], sem("w_hi"), sem("w_lo")
        x_in_s, x1_in, stored = sem("x_in_s"), sem("x1_in"), sem("stored")
        index_ready = sem("index_ready")
        gathered = [sem(f"gathered{i}") for i in range(QT)]
        scales_ready, added, normed, finished = sem("scales_ready"), sem("added"), sem("normed"), sem("finished")
        stage = [f, yk[0]]
        block = ctx.enter_context(nc.Block())

        def seq(dram, b):
            return dram[bass.ds(b, 1)].rearrange("o p t d -> p (o t) d")

        def turns(engine, turn):
            with engine.Fori(0, NB - 1) as b:
                turn(b, False)
            turn(NB - 1, True)

        @block.sync
        def _(sp):
            sp.dma_start(x_in[:], seq(xn, 0)).then_inc(x_in_s, 16)
            for c in range(NC):
                r = c % 2
                if c >= 2:
                    sp.wait_ge(w_lo, c - 1)
                cols = slice(c * P, (c + 1) * P)
                sp.dma_start(stage[r][:, :, 0:P], shg[:, :, cols]).then_inc(w_in[r], 16)
                sp.dma_start(stage[r][:, :, P:2 * P], shu[:, :, cols]).then_inc(w_in[r], 16)
                sp.dma_start(stage[r][:, 0, 2 * P:4 * P], shd[:, c, 0:2 * P]).then_inc(w_in[r], 16)
                sp.dma_start(stage[r][:, 1, 2 * P:4 * P], shd[:, c, 2 * P:4 * P]).then_inc(w_in[r], 16)

            def turn(b, last):
                if not last:
                    sp.wait_ge(s["xT_done"], C * b + C)
                    sp.dma_start(x_in[:], seq(xn, b + 1)).then_inc(x_in_s, 16)
                sp.wait_ge(added, 2 * QT * b + 2 * QT)
                sp.dma_start(yk[0][:], seq(x1, b)).then_inc(x1_in, 16)
                sp.wait_ge(finished, QT * b + QT)
                sp.dma_start(seq(out, b), f[:]).then_inc(stored, 16)

            turns(sp, turn)
            sp.wait_ge(stored, 16 * NB)

        @block.tensor
        def _(pe):
            g = GatedProducts(nc, pe, rows, xT, act_s, gate_up_ps, out_ps, s)
            pe.wait_ge(x_in_s, 16)
            for c in range(C):
                g.transpose_x(x_in, c, idf)

            def turn(b, last):
                pe.wait_ge(s["xT_lo"], C * b + C)
                for c in range(NC):
                    pe.wait_ge(w_lo, c + 1)
                    g.gate_up(b, c, lambda j, k: gate_s[j][:, k, c * P:(c + 1) * P],
                              lambda j, k: up_s[j][:, k, c * P:(c + 1) * P])
                    if c == NC - 1 and not last:
                        pe.wait_ge(x_in_s, 16 * b + 32)
                        pe.wait_ge(s["act_ready"], NC * b + NC - 1)
                        g.transpose_x(x_in, 0, idf)
                        g.transpose_x(x_in, 1, idf)
                    if c > 0:
                        g.down(b, c - 1, lambda k: dn_s[k][:, c - 1, :])
                if not last:
                    pe.wait_ge(s["act_ready"], NC * b + NC)
                    g.transpose_x(x_in, 2, idf)
                    g.transpose_x(x_in, 3, idf)
                g.down(b, NC - 1, lambda k: dn_s[k][:, NC - 1, :])

            turns(pe, turn)

        def pieces(c, j):
            r, cols = c % 2, slice(c * P, (c + 1) * P)
            return [(gate_s[j][:, :, cols], stage[r][:, :, 0:P]), (up_s[j][:, :, cols], stage[r][:, :, P:2 * P]),
                    (dn_s[j][:, c, :].rearrange("p (a d) -> p a d", a=2), stage[r][:, 0:2, 2 * P:4 * P])]

        @block.scalar
        def _(act):
            def split_hi(c):
                act.wait_ge(w_in[c % 2], 64 * (c // 2) + 64)
                for dst, src in pieces(c, 0):
                    last = nc.scalar.activation(dst, src, ACT.Copy)
                last.then_inc(w_hi, 1)

            split_hi(0)
            for c in range(C):
                high_x(nc, 0, c, xT, gate_up_ps, s)
            for c in range(1, NC):
                split_hi(c)
                gate_silu(nc, 0, c - 1, rows, silu, gate_up_ps, s)

            def normalize(b):
                for i in range(QT):
                    act.wait_ge(norm.ready, b + 1)
                    nc.scalar.activation(f[:, i, :], f[:, i, :], ACT.Identity, bias=norm.bias[:, i:i + 1],
                                         scale=norm.rstd[:, i:i + 1]).then_inc(normed, 1)

            def turn(b, last, begun=0):
                for c in range(begun, NC):
                    gate_silu(nc, b, c, rows, silu, gate_up_ps, s)
                    if c == 3 and begun == 0:
                        normalize(b - 1)
                if not last:
                    for c in range(C):
                        high_x(nc, b + 1, c, xT, gate_up_ps, s)
                act.wait_ge(scales_ready, b + 1)
                act.wait_ge(stored, 16 * b)
                for i in range(QT):
                    act.wait_ge(s["out_done"], QT * b + i + 1)
                    nc.scalar.activation(f[:, i, :], out_ps[i][:], ACT.Copy,
                                         scale=scales[:, 2, i:i + 1]).then_inc(s["out_taken"], 1)

            turn(0, False, NC - 1)
            with act.Fori(1, NB - 1) as b:
                turn(b, False)
            turn(NB - 1, True)
            normalize(NB - 1)

        @block.vector
        def _(dve):
            def split_lo(c):
                dve.wait_ge(w_hi, c + 1)
                for (dst, src), (high, _) in zip(pieces(c, 1), pieces(c, 0)):
                    last = nc.vector.tensor_tensor(dst, src, high.bitcast(F32), ALU.subtract)
                last.then_inc(w_lo, 1)

            split_lo(0)
            for c in range(C):
                low_x(nc, 0, c, xT, gate_up_ps, s)
            for c in range(1, NC):
                split_lo(c)
                gate_times_up(nc, 0, c - 1, rows, silu, act_s, gate_up_ps, s)

            def turn(b, last, begun=0):
                for c in range(begun, NC):
                    gate_times_up(nc, b, c, rows, silu, act_s, gate_up_ps, s)
                if not last:
                    for c in range(C):
                        low_x(nc, b + 1, c, xT, gate_up_ps, s)
                dve.wait_ge(normed, QT * b)
                nc.vector.tensor_copy(scales[:, 0:2, :], weight[:, :, bass.ds(QT * b, QT)])
                nc.vector.tensor_copy(scales[:, 2, :], gate[:, bass.ds(QT * b, QT)]).then_inc(scales_ready, 1)
                for i in range(QT):
                    if i > 0:
                        norm.await_stats(b, i)
                    dve.wait_ge(s["out_taken"], QT * b + i + 1)
                    dve.wait_ge(gathered[i], 32 * b + 32)
                    for k in range(2):
                        nc.vector.scalar_tensor_tensor(out=f[:, i, :], in0=yk[k][:, i, :], scalar=scales[:, k, i:i + 1],
                                                       in1=f[:, i, :], op0=ALU.mult, op1=ALU.add).then_inc(added, 1)
                        if k == 0 and i > 0:
                            norm.aggregate([i - 1])
                        dve.wait_ge(added, 2 * QT * b + 2 * i + k + 1)
                    norm.row_stats(f, i)
                norm.await_stats(b)
                nc.vector.memset(norm.half[:], 0.0)
                norm.aggregate([QT - 1])
                norm.halve(b)
                norm.shift_bits(b)
                norm.guess(b)

            turn(0, False, NC - 1)
            with dve.Fori(1, NB - 1) as b:
                turn(b, False)
            turn(NB - 1, True)

        @block.gpsimd
        def _(pool):
            def turn(b, turns_begun):
                nc.gpsimd.tensor_copy(index[:], slot[:, :, bass.ds(QT * b, QT)]).then_inc(index_ready, 1)
                pool.wait_ge(w_lo, NC)
                pool.wait_ge(index_ready, turns_begun)
                for i in range(QT):
                    for k in range(2):
                        pool.indirect_dma_start(out=yk[k][:, i, :], out_offset=None, in_=ys,
                                                in_offset=bass.IndirectOffsetOnAxis(ap=index[:, k, i:i + 1], axis=0)
                                                ).then_inc(gathered[i], 16)
                norm.refine(b)
                for i in range(QT):
                    pool.wait_ge(normed, QT * b + i + 1)
                    pool.wait_ge(x1_in, 16 * b + 16)
                    nc.gpsimd.tensor_tensor(f[:, i, :], f[:, i, :], yk[0][:, i, :], ALU.add).then_inc(finished, 1)

            with pool.Fori(1, NB + 1) as turns_begun:
                turn(turns_begun - 1, turns_begun)


def build_constants(nc, idf, idb, mask, norm_constants):
    with nc.semaphore("made") as made, nc.Block() as block:
        @block.gpsimd
        def _(pool):
            nc.gpsimd.memset(idf[:], 0.0)
            nc.gpsimd.memset(norm_constants[:, 0, :], 0.0)
            nc.gpsimd.memset(norm_constants[:, 1, :], 1.5)
            nc.gpsimd.memset(mask[:], 0.0).then_inc(made, 1)
            pool.wait_ge(made, 1)
            nc.gpsimd.affine_select(out=idf[:], in_=idf[:], compare_op=ALU.not_equal, fill=1.0, base=0,
                                    pattern=[[-1, P]], channel_multiplier=1)
            nc.gpsimd.affine_select(out=mask[:], in_=mask[:], compare_op=ALU.is_ge, fill=MASKED, base=0,
                                    pattern=[[-1, P]], channel_multiplier=1).then_inc(made, 1)
            pool.wait_ge(made, 2)
            nc.gpsimd.tensor_copy(idb[:], idf[:]).then_inc(made, 1)
            pool.wait_ge(made, 3)


def build_layer(nc, x, wq, wvk, wo, wr, qb, vkb, ob, gu, dn, shg, shu, shd, out):
    def scratch(name, rows):
        return nc.dram_tensor(name, (rows, D), F32, kind="Internal").ap()

    def by_sequence(dram):
        return dram.rearrange("(b t p) d -> b p t d", t=QT, p=P)

    x1, xn, ys = scratch("x1", NB * S), scratch("xn", NB * S), scratch("ys", NT * TS)
    with ExitStack() as ctx:
        def sb(name, shape, dt=F32):
            return ctx.enter_context(nc.sbuf_tensor(name, shape, dt))

        idf, idb, mask = sb("idf", [P, P]), sb("idb", [P, P], BF16), sb("mask", [P, P], BF16)
        norm_constants = sb("norm_constants", [P, 2, QT])
        logits = sb("logits", [P, NTT, R])
        build_constants(nc, idf, idb, mask, norm_constants)
        build_attention(nc, by_sequence(x), wq, wvk, wo, wr, qb, vkb, ob, by_sequence(x1), by_sequence(xn),
                        logits, idf, idb, mask, norm_constants)
        gate = sb("gate", [P, NTT])
        weight = sb("weight", [P, 2, NTT])
        slot = sb("slot", [P, 2, NTT], I32)
        token_of_slot = sb("token_of_slot", [P, SC], I32)
        tile_expert = sb("tile_expert", [1, NT], I32)
        build_routing(nc, logits, gate, weight, slot, token_of_slot, tile_expert)
        build_experts(nc, xn, gu, dn, ys.rearrange("(n t p) d -> n p t d", t=QT, p=P), token_of_slot, tile_expert, idf)
        build_shared(nc, by_sequence(xn), shg, shu, shd, ys, by_sequence(x1), by_sequence(out), gate, weight, slot, idf,
                     norm_constants)


def kernel(**inputs):
    import numpy as np
    import concourse.bacc as bacc
    from concourse.bass_utils import run_bass_kernel_spmd

    a = {k.split("_", 2)[2]: np.asarray(v) for k, v in inputs.items()}

    def chunked(w):
        return np.ascontiguousarray(w.T.reshape(-1, P, w.shape[0]).transpose(1, 0, 2))

    arrays = {
        "x_in": a["hidden_states"].reshape(NB * S, D),
        "wq_in": chunked(a["q_w"]),
        "wvk_in": chunked(np.concatenate([a["v_w"], a["k_w"]])),
        "wo_in": chunked(a["o_w"]),
        "wr_in": chunked(np.concatenate([a["router_weight"], a["shared_gate_w"]])),
        "qb_in": np.ascontiguousarray(a["q_b"].reshape(C, P).T),
        "vkb_in": np.concatenate([a["v_b"], a["k_b"]]).reshape(2 * HD, 1),
        "ob_in": a["o_b"],
        "gu_in": np.stack([chunked(w) for w in a["gate_up_proj"]]),
        "dn_in": np.ascontiguousarray(a["down_proj"].transpose(0, 2, 1)),
        "shg_in": chunked(a["sh_gate_w"]),
        "shu_in": chunked(a["sh_up_w"]),
        "shd_in": chunked(a["sh_down_w"]),
    }
    nc = bacc.Bacc("TRN2", target_bir_lowering=False, num_devices=1)
    args = [nc.dram_tensor(k, v.shape, F32, kind="ExternalInput").ap() for k, v in arrays.items()]
    out = nc.dram_tensor("out", (NB * S, D), F32, kind="ExternalOutput").ap()
    build_layer(nc, *args, out)
    r = run_bass_kernel_spmd(nc, [arrays], core_ids=[0])
    return r.results[0]["out"].reshape(NB, S, D)
```

```python
import concourse.bass as bass
from concourse import mybir
from contextlib import ExitStack

F32 = mybir.dt.float32
F32R = mybir.dt.float32r
BF16 = mybir.dt.bfloat16
I32 = mybir.dt.int32
U32 = mybir.dt.uint32
ALU = mybir.AluOpType
ACT = mybir.ActivationFunctionType
AX_X = mybir.AxisListType.X

P = 128
S = 512
NB = 8
D = 512
C = D // P
QT = S // P
H = 16
HD = D // H
HG = P // HD
E = 8
R = E + 1
EPS = 1e-5
SCALE = float(HD) ** -0.5
MASKED = -3.0e38
I_MOE = 352
I_SH = 1408
TS = 512
NTT = NB * QT
NT = (2 * NB * S + E * (TS - 1)) // TS
SC = NT * TS // P
PASSES = ((0, 0), (0, 1), (1, 0))
MAGIC = float(0x5F3759DF - (1 << 22))
NEWTON = 3


class Steps:

    def __init__(self, engine, sem):
        self.engine, self.sem, self.n = engine, sem, 0

    def then_wait(self, instruction):
        instruction.then_inc(self.sem, 1)
        self.n += 1
        self.engine.wait_ge(self.sem, self.n)


class InverseStd:
    STEPS = 4 * NEWTON + 1

    def __init__(self, nc, sb, sem, name, constants):
        self.nc, self.constants = nc, constants
        self.stats = sb("stats" + name, [P, QT, 6])
        self.mean_var = sb("mean_var" + name, [P, QT, 2])
        self.half = sb("half" + name, [P, QT])
        self.bits = sb("bits" + name, [P, QT])
        self.t = sb("t" + name, [P, 3, QT])
        self.rstd = sb("rstd" + name, [P, QT])
        self.bias = sb("bias" + name, [P, QT])
        self.row_six = sem("row_six" + name)
        self.row_var = sem("row_var" + name)
        self.guessed = sem("guessed" + name)
        self.newton = sem("newton" + name)
        self.ready = sem("std_ready" + name)

    def row_stats(self, src, i):
        self.nc.vector.bn_stats(self.stats[:, i, :], src[:, i, :]).then_inc(self.row_six, 1)

    def await_stats(self, n, tiles=QT):
        self.nc.vector.wait_ge(self.row_six, QT * n + tiles)

    def aggregate(self, tiles=range(QT)):
        for i in tiles:
            last = self.nc.vector.bn_aggr(self.mean_var[:, i, :], self.stats[:, i, :])
        if tiles[-1] == QT - 1:
            last.then_inc(self.row_var, 1)

    def halve(self, n):
        self.nc.vector.wait_ge(self.row_var, 3 * n + 1)
        self.nc.vector.tensor_scalar(self.half[:], self.mean_var[:, :, 1], EPS, 0.5, ALU.add,
                                     ALU.mult).then_inc(self.row_var, 1)

    def shift_bits(self, n):
        self.nc.vector.wait_ge(self.row_var, 3 * n + 2)
        self.nc.vector.tensor_scalar(self.bits[:].bitcast(I32), self.half[:].bitcast(I32), 1, None,
                                     ALU.logical_shift_right).then_inc(self.row_var, 1)

    def guess(self, n):
        self.nc.vector.wait_ge(self.row_var, 3 * n + 3)
        self.nc.vector.tensor_scalar(self.t[:, 2, :].bitcast(I32), self.bits[:].bitcast(I32), -1.0, MAGIC,
                                     ALU.mult, ALU.add).then_inc(self.guessed, 1)

    def refine(self, n):
        zero, three_halves = self.constants[:, 0, :], self.constants[:, 1, :]
        a, b, y = self.t[:, 0, :], self.t[:, 1, :], self.t[:, 2, :]
        at = self.STEPS * n
        self.nc.gpsimd.wait_ge(self.guessed, n + 1)

        def step(out, in0, in1, op):
            nonlocal at
            at += 1
            self.nc.gpsimd.tensor_tensor(out, in0, in1, op).then_inc(self.newton, 1)
            self.nc.gpsimd.wait_ge(self.newton, at)

        for k in range(NEWTON):
            step(a, y, y, ALU.mult)
            step(b, a, self.half[:], ALU.mult)
            step(a, three_halves, b, ALU.subtract)
            y_next = self.rstd[:] if k == NEWTON - 1 else y
            step(y_next, y, a, ALU.mult)
        step(b, self.mean_var[:, :, 0], self.rstd[:], ALU.mult)
        self.nc.gpsimd.tensor_tensor(self.bias[:], zero, b, ALU.subtract).then_inc(self.ready, 1)


def build_attention(nc, x, wq, wvk, wo, wr, qb, vkb, ob, x1_out, xn_out, logits, idf, idb, mask, norm_constants):
    ctx = ExitStack()
    with ctx:
        def sb(name, shape, dt=F32):
            return ctx.enter_context(nc.sbuf_tensor("at_" + name, shape, dt))

        def sem(name):
            return ctx.enter_context(nc.semaphore("at_" + name))

        wq_s = [sb(f"wq{j}", [P, C, D], F32R) for j in range(2)]
        wvk_s = [sb(f"wvk{j}", [P, C, 2 * HD], F32R) for j in range(2)]
        wo_s = [sb(f"wo{j}", [P, C, D], F32R) for j in range(2)]
        wr_s = [sb(f"wr{j}", [P, C, R], F32R) for j in range(2)]
        qb_s = sb("qb", [P, C])
        vkb_s = sb("vkb", [2 * HD, 1])
        vks_s = sb("vks", [2 * HD, 1])
        vkbs_s = sb("vkbs", [2 * HD, 1])
        ob_s = sb("ob", [P, D])
        x_in = sb("x_in", [P, QT, D])
        x_res = sb("x_res", [P, QT, D])
        y = sb("y", [P, QT, D])
        xn2 = sb("xn2", [P, QT, D])
        xT = [sb(f"xT{j}", [P, C, S], F32R) for j in range(2)]
        vk = sb("vk", [2 * HD, S])
        vk_h = [sb(f"vk_h{j}", [2 * HD, S], F32R) for j in range(2)]
        q_h = [[sb(f"q_h{j}{r}", [P, S], F32R) for j in range(2)] for r in range(2)]
        Qs = sb("Qs", [3 * HD, H, S], F32R)
        Ks = sb("Ks", [3 * HD, S], F32R)
        V = sb("V", [P, QT, HD])
        ones_f = sb("ones_f", [P, QT, HD])
        PW = QT * (QT + 1) // 2 * P
        minus_max = [sb(f"minus_max{r}", [P, QT, P], F32R) for r in range(3)]
        PT = [sb(f"PT{r}", [P, HG, PW]) for r in range(2)]
        OT = [sb(f"OT{j}", [P, C, S], F32R) for j in range(2)]
        nmax = sb("nmax", [P, 3, QT])
        over_sum, mixed_f = sb("over_sum", [P, S]), sb("mixed_f", [P, S])
        ones = sb("ones", [P, P], F32R)
        norm = [InverseStd(nc, sb, sem, f"_{of}", norm_constants) for of in ("x", "projection", "x1")]
        lgT = over_sum[0:R, :]

        bank = [ctx.enter_context(nc.psum_tensor(f"at_bank{i}", [P, 512], F32)) for i in range(8)]
        S_ps, T_ps = bank[0:3], bank[4:7]
        sum_ps, A_ps = bank[3], bank[7]
        X_ps = bank[0:4]
        O_ps = [bank[4], bank[5], bank[6], bank[7]]

        w_in, w_split = sem("w_in"), sem("w_split")
        b_in = sem("b_in")
        x_in_s, x_res_s = sem("x_in_s"), sem("x_res_s")
        q_moved = [sem(f"q_moved{c}") for c in range(C)]
        q_spilled = [sem(f"q_spilled{c}") for c in range(C)]
        k_moved = sem("k_moved")
        q_dram = nc.dram_tensor("q_dram", (2, C, P, S), F32, kind="Internal").ap()
        x1_stored, xn_stored = sem("x1_stored"), sem("xn_stored")
        scores, shifted, summed, mixed, projected = (sem("scores"), sem("shifted"), sem("summed"), sem("mixed"),
                                                     sem("projected"))
        xT1_ps, qkv_ps, v_ps, xT2_ps = sem("xT1_ps"), sem("qkv_ps"), sem("v_ps"), sem("xT2_ps")
        rt_ps, lg_ps = sem("rt_ps"), sem("lg_ps")
        halved, inverted, mixed_taken = sem("halved"), sem("inverted"), sem("mixed_taken")
        max_ready, xT1_lo, xT2_lo, OT_lo = sem("max_ready"), sem("xT1_lo"), sem("xT2_lo"), sem("OT_lo")
        qkv_lo, v_ready, y_ready, lg_ready = sem("qkv_lo"), sem("v_ready"), sem("y_ready"), sem("lg_ready")
        pt_ready, xT1_hi, xT2_hi, OT_hi = sem("pt_ready"), sem("xT1_hi"), sem("xT2_hi"), sem("OT_hi")
        qkv_hi, x_normed, y_normed, xn_ready, lgT_ready = (sem("qkv_hi"), sem("x_normed"), sem("y_normed"),
                                                           sem("xn_ready"), sem("lgT_ready"))
        x1_ready, diagonal_ready, ones_ready = sem("x1_ready"), sem("diagonal_ready"), sem("ones_ready")

        S_UNITS = [((2, 0), (0, (QT - 1) * P)), ((3, 0),), ((1, 0),)]
        T_UNITS = [((0, 0),), ((3, 0), (1, P)), ((2, 0),)]
        TOFF = [0, (QT + 1) * P, 2 * QT * P, QT * P]
        TFROM = [0, QT * P, 2 * QT * P]
        TW = [QT * P, QT * P, 2 * P]
        UNIT_PS = [S_ps[0], S_ps[1], S_ps[2], S_ps[0], S_ps[1]]
        AV_STEP = [HG * g + HG + 1 for g in range(C)]

        block = ctx.enter_context(nc.Block())

        def turns(engine, turn):
            turn(0, True, False)
            with engine.Fori(1, NB - 1) as b:
                turn(b, False, False)
            turn(NB - 1, False, True)

        def seq(dram, b):
            return dram[bass.ds(b, 1)].rearrange("o p t d -> p (o t) d")

        @block.sync
        def _(sp):
            sp.dma_start(y[:], wq).then_inc(w_in, 16)
            sp.dma_start(xn2[:], wo).then_inc(w_in, 16)
            sp.dma_start(x_in[:], seq(x, 0)).then_inc(x_in_s, 16)
            sp.dma_start(x_res[:, :, 0:2 * HD], wvk).then_inc(w_in, 16)
            sp.dma_start(x_res[:, :, 2 * HD:2 * HD + R], wr).then_inc(w_in, 16)
            sp.dma_start(qb_s[:], qb).then_inc(b_in, 16)
            sp.dma_start(vkb_s[:], vkb).then_inc(b_in, 16)
            sp.dma_start(ob_s[:], ob.partition_broadcast(P)).then_inc(b_in, 16)

            def store_x1(n):
                sp.wait_ge(x1_ready, QT * n + QT)
                sp.dma_start(seq(x1_out, n), y[:]).then_inc(x1_stored, 16)

            def store_xn(n):
                sp.wait_ge(xn_ready, QT * n + QT)
                sp.dma_start(seq(xn_out, n), xn2[:]).then_inc(xn_stored, 16)

            def move_qkv(n):
                sp.wait_ge(qkv_lo, 5 * n + 1)
                for at, half in ((0, 0), (1, 0), (2, 1)):
                    sp.dma_start(Ks[HD * at:HD * at + HD, :].bitcast(F32),
                                 vk_h[half][HD:2 * HD, :].bitcast(F32)).then_inc(k_moved, 16)
                for c in range(C + 1):
                    if c < C:
                        sp.wait_ge(qkv_lo, 5 * n + 2 + c)
                        for half in range(2):
                            sp.dma_start(q_dram[half, c], q_h[c % 2][half][:].bitcast(F32)).then_inc(q_spilled[c], 16)
                    if c > 0:
                        sp.wait_ge(q_spilled[c - 1], 32 * n + 32)
                        for at, half in ((0, 0), (1, 1), (2, 0)):
                            sp.dma_start(Qs[HD * at:HD * at + HD, HG * (c - 1):HG * c, :].bitcast(F32),
                                         q_dram[half, c - 1].rearrange("(g d) t -> d g t", g=HG)
                                         ).then_inc(q_moved[c - 1], 16)

            move_qkv(0)
            sp.wait_ge(w_split, 4)
            sp.dma_start(x_res[:], seq(x, 0)).then_inc(x_res_s, 16)

            def turn(b, first, last):
                if not last:
                    sp.wait_ge(xT1_ps, C * b + C)
                    sp.dma_start(x_in[:], seq(x, b + 1)).then_inc(x_in_s, 16)
                if not first:
                    sp.wait_ge(x1_ready, QT * b)
                    sp.dma_start(x_res[:], seq(x, b)).then_inc(x_res_s, 16)
                    store_x1(b - 1)
                if not last:
                    sp.wait_ge(shifted, 3 * H * b + 3 * H)
                    move_qkv(b + 1)
                if not first:
                    store_xn(b - 1)

            turns(sp, turn)
            store_x1(NB - 1)
            store_xn(NB - 1)
            sp.wait_ge(x1_stored, 16 * NB)
            sp.wait_ge(xn_stored, 16 * NB)

        @block.tensor
        def _(pe):
            def split_product(out, w, x_, cols, xcols):
                n = 0
                for c in range(C):
                    for i, j in PASSES:
                        last = nc.tensor.matmul(out, w[i][:, c, cols], x_[j][:, c, xcols],
                                                start=(n == 0), stop=(n == 3 * C - 1))
                        n += 1
                return last

            def transpose_x(src, c, out, done):
                for t in range(QT):
                    last = nc.tensor.transpose(out[:, t * P:(t + 1) * P], src[:, t, c * P:(c + 1) * P], idf[:])
                last.then_inc(done, 1)

            def project_qkv(n, u, start=False):
                if u == 0:
                    pe.wait_ge(xT1_lo, C * n + C)
                    if start:
                        pe.wait_ge(w_split, 4)
                if u >= 3:
                    pe.wait_ge(qkv_lo, 5 * n + u - 2)
                if u == 0:
                    last = split_product(S_ps[0][0:2 * HD, :], wvk_s, xT, slice(0, 2 * HD), slice(0, S))
                else:
                    last = split_product(UNIT_PS[u][:], wq_s, xT, slice((u - 1) * P, u * P), slice(0, S))
                last.then_inc(qkv_ps, 1)

            def transpose_v(n):
                pe.wait_ge(pt_ready, 3 * H * n)
                pe.wait_ge(qkv_lo, 5 * n + 1)
                for j in range(QT):
                    last = nc.tensor.matmul(T_ps[0][:, j * HD:(j + 1) * HD], vk[0:HD, j * P:(j + 1) * P],
                                            idf[0:HD, 0:HD], start=True, stop=True)
                last.then_inc(v_ps, 1)

            pe.wait_ge(ones_ready, 2)
            pe.wait_ge(x_normed, QT)
            for c in range(C):
                transpose_x(x_in, c, X_ps[c], xT1_ps)
            for u in range(5):
                project_qkv(0, u, True)
            transpose_v(0)

            def transpose_xn(n):
                pe.wait_ge(xn_ready, QT * n + QT)
                for c in range(C):
                    transpose_x(xn2, c, X_ps[c], xT2_ps)

            def route(n):
                pe.wait_ge(xT2_lo, C * n + C)
                split_product(sum_ps[0:R, :], wr_s, xT, slice(0, R), slice(0, S)).then_inc(rt_ps, 1)

            def transpose_logits(n):
                pe.wait_ge(lgT_ready, n + 1)
                for t in range(QT):
                    last = nc.tensor.matmul(sum_ps[:, t * R:(t + 1) * R], lgT[:, t * P:(t + 1) * P],
                                            idf[0:R, 0:R], start=True, stop=True)
                last.then_inc(lg_ps, 1)

            def over_keys(weights, out, g):
                for j in range(QT):
                    for k in range(HG):
                        last = nc.tensor.matmul(out[HD * k:HD * k + HD, j * P:S], weights[:, j, :],
                                                PT[g % 2][:, k, TOFF[j]:TOFF[j] + (QT - j) * P],
                                                start=(j == 0), stop=(j == QT - 1), tile_position=(0, HD * k))
                return last

            def query_scores(n, s):
                if s == 0:
                    pe.wait_ge(qkv_lo, 5 * n + 5)
                    pe.wait_ge(k_moved, 48 * n + 48)
                if s % HG == 0:
                    pe.wait_ge(q_moved[s // HG], 48 * n + 48)
                for u, tiles in enumerate(S_UNITS):
                    if s > 0:
                        pe.wait_ge(max_ready, 3 * H * n + 3 * (s - 1) + u + 1)
                    for i, col in tiles:
                        nc.tensor.matmul(S_ps[u][:, col:col + (i + 1) * P], Qs[:, s, i * P:(i + 1) * P],
                                         Ks[:, 0:(i + 1) * P], start=((i, col) == tiles[0]), stop=False)
                    i, col = tiles[0]
                    nc.tensor.matmul(S_ps[u][:, col + i * P:col + (i + len(tiles)) * P], idb[:, 0, :],
                                     mask[:, 0:len(tiles), :].rearrange("p t k -> p (t k)"),
                                     start=False, stop=True).then_inc(scores, 1)

            query_scores(0, 0)

            def turn(b, first, last):
                for s in range(1, H + 2):
                    if s < H:
                        query_scores(b, s)
                    if s == H and not last:
                        pe.wait_ge(x_normed, QT * b + 2 * QT)
                        pe.wait_ge(max_ready, 3 * H * b + 3 * H)
                        for c in range(C):
                            if c == C - 1:
                                pe.wait_ge(inverted, QT * (C * b + C - 1))
                            transpose_x(x_in, c, X_ps[c], xT1_ps)
                    if s <= H:
                        h = s - 1
                        if h == 0:
                            pe.wait_ge(v_ready, b + 1)
                        pe.wait_ge(diagonal_ready, H * b + h + 1)
                        for tb, tiles in enumerate(T_UNITS):
                            if h > 0:
                                pe.wait_ge(pt_ready, 3 * H * b + 3 * (h - 1) + tb + 1)
                            elif not first:
                                pe.wait_ge(y_ready, QT * b)
                            for j, col in tiles:
                                n = (QT - j) * P
                                nc.tensor.matmul(T_ps[tb][:, col:col + n], Ks[:, j * P:(j + 1) * P], Qs[:, h, j * P:S],
                                                 start=((j, col) == tiles[0]), stop=False)
                            nc.tensor.matmul(T_ps[tb][:, 0:len(tiles) * P], mask[:, 0, :],
                                             idb[:, 0:len(tiles), :].rearrange("p t k -> p (t k)"), start=False, stop=False)
                            for j, col in tiles:
                                n = (QT - j) * P
                                lastt = nc.tensor.matmul(T_ps[tb][:, col:col + n], ones[:],
                                                         minus_max[h % 3][:, j:QT, :].rearrange("p i k -> p (i k)"),
                                                         start=False, stop=((j, col) == tiles[-1]))
                            lastt.then_inc(shifted, 1)
                    if s == H and not last:
                        project_qkv(b + 1, 0)
                        project_qkv(b + 1, 1)
                    if s == H + 1 and not last:
                        for u in (2, 3, 4):
                            project_qkv(b + 1, u)
                    if s in AV_STEP:
                        g = AV_STEP.index(s)
                        pe.wait_ge(pt_ready, 3 * H * b + 3 * HG * (g + 1))
                        if g > 0:
                            pe.wait_ge(inverted, QT * (C * b + g))
                        elif not first:
                            pe.wait_ge(lg_ready, b)
                        over_keys(ones_f, sum_ps, g).then_inc(summed, 1)
                    if s - 1 in AV_STEP or s == H + 1:
                        g = C - 1 if s == H + 1 else AV_STEP.index(s - 1)
                        if g > 0:
                            pe.wait_ge(mixed_taken, C * b + g)
                        over_keys(V, A_ps, g).then_inc(mixed, 1)
                if not last:
                    transpose_v(b + 1)
                if not first:
                    if not last:
                        pe.wait_ge(qkv_lo, 5 * b + 10)
                    pe.wait_ge(inverted, QT * (C * b + C))
                    transpose_xn(b - 1)
                for c in range(C):
                    if c == C - 2:
                        if not first:
                            route(b - 1)
                        if not last:
                            query_scores(b + 1, 0)
                    pe.wait_ge(OT_lo, C * b + c + 1)
                    if c == 0 and not last:
                        pe.wait_ge(v_ready, b + 2)
                    for i in range(QT):
                        if c == 0 and i == QT - 1:
                            pe.wait_ge(mixed_taken, C * b + C)
                        for n, (j, k) in enumerate(PASSES):
                            lastt = nc.tensor.matmul(O_ps[i][:], OT[j][:, c, i * P:(i + 1) * P], wo_s[k][:, c, :],
                                                     start=(c == 0 and n == 0), stop=(c == C - 1 and n == 2))
                        if c == C - 1:
                            lastt.then_inc(projected, 1)
                if not first:
                    transpose_logits(b - 1)

            turns(pe, turn)
            pe.wait_ge(lg_ready, NB)
            transpose_xn(NB - 1)
            route(NB - 1)
            transpose_logits(NB - 1)

        @block.vector
        def _(dve):
            dve.wait_ge(b_in, 48)
            nc.vector.memset(vks_s[HD:2 * HD, :], SCALE).then_inc(lg_ready, 1)
            nc.vector.memset(vks_s[0:HD, :], 1.0).then_inc(w_split, 1)
            dve.wait_ge(w_split, 1)
            nc.vector.tensor_tensor(vkbs_s[:], vkb_s[:], vks_s[:], ALU.mult).then_inc(w_split, 1)

            def whole_norm(k, n, src, ready):
                for i in range(QT):
                    dve.wait_ge(ready, QT * n + i + 1)
                    norm[k].row_stats(src, i)
                norm[k].await_stats(n)
                norm[k].aggregate()
                norm[k].halve(n)
                norm[k].shift_bits(n)
                norm[k].guess(n)

            def low_x(n, c, ps, hi_sem, lo_sem):
                dve.wait_ge(hi_sem, C * n + c + 1)
                nc.vector.tensor_tensor(xT[1][:, c, :], ps[:], xT[0][:, c, :].bitcast(F32),
                                        ALU.subtract).then_inc(lo_sem, 1)

            def low_qkv(n, u):
                dve.wait_ge(qkv_hi, 5 * n + u + 1)
                if u == 0:
                    nc.vector.tensor_copy(vk_h[0][:], vk[:]).then_inc(halved, 1)
                    dve.wait_ge(halved, n + 2)
                    nc.vector.tensor_tensor(vk_h[1][:], vk[:], vk_h[0][:].bitcast(F32),
                                            ALU.subtract).then_inc(qkv_lo, 1)
                else:
                    r = (u - 1) % 2
                    nc.vector.scalar_tensor_tensor(out=q_h[r][1][:], in0=UNIT_PS[u][:], scalar=qb_s[:, u - 1:u],
                                                   in1=q_h[r][0][:].bitcast(F32), op0=ALU.add,
                                                   op1=ALU.subtract).then_inc(qkv_lo, 1)

            def take_v(n):
                dve.wait_ge(v_ps, n + 1)
                nc.vector.tensor_copy(V[:], T_ps[0][:, 0:QT * HD].rearrange("p (t d) -> p t d", t=QT)).then_inc(v_ready, 1)

            dve.wait_ge(x_in_s, 16)
            for i in range(QT):
                norm[0].row_stats(x_in, i)
            norm[0].await_stats(0)
            norm[0].aggregate()
            norm[0].halve(0)
            norm[0].shift_bits(0)
            norm[0].guess(0)
            dve.wait_ge(w_in, 64)
            for src, dst in ((y[:], wq_s), (xn2[:], wo_s), (x_res[:, :, 0:2 * HD], wvk_s),
                             (x_res[:, :, 2 * HD:2 * HD + R], wr_s)):
                last = nc.vector.tensor_copy(dst[0][:], src)
            last.then_inc(halved, 1)
            dve.wait_ge(halved, 1)
            for src, dst in ((y[:], wq_s), (xn2[:], wo_s), (x_res[:, :, 0:2 * HD], wvk_s),
                             (x_res[:, :, 2 * HD:2 * HD + R], wr_s)):
                last = nc.vector.tensor_tensor(dst[1][:], src, dst[0][:].bitcast(F32), ALU.subtract)
            last.then_inc(w_split, 2)
            for c in range(C):
                low_x(0, c, X_ps[c], xT1_hi, xT1_lo)
            for u in range(5):
                low_qkv(0, u)
            take_v(0)

            def take_projection(n, first):
                if not first:
                    dve.wait_ge(x1_stored, 16 * n)
                    dve.wait_ge(xn_ready, QT * n)
                for i in range(QT):
                    dve.wait_ge(projected, QT * n + i + 1)
                    last = nc.vector.tensor_tensor(y[:, i, :], O_ps[i][:], ob_s[:], ALU.add)
                    last.then_inc(y_ready, 1)

            def take_logits(n):
                dve.wait_ge(lg_ps, n + 1)
                nc.vector.tensor_copy(logits[:, bass.ds(QT * n, QT), :],
                                      sum_ps[:, 0:QT * R].rearrange("p (t r) -> p t r", t=QT)).then_inc(lg_ready, 1)

            def invert_sums(n, g, i):
                dve.wait_ge(summed, C * n + g + 1)
                nc.vector.reciprocal(over_sum[:, i * P:(i + 1) * P], sum_ps[:, i * P:(i + 1) * P]).then_inc(inverted, 1)

            def maxima(n, s, u, start):
                if u == 0:
                    if s >= 3:
                        dve.wait_ge(diagonal_ready, H * n + s - 2)
                    elif not start:
                        dve.wait_ge(diagonal_ready, H * n)
                dve.wait_ge(scores, 3 * H * n + 3 * s + u + 1)
                for i, col in S_UNITS[u]:
                    last = nc.vector.tensor_reduce(nmax[:, s % 3, i:i + 1], S_ps[u][:, col:col + (i + 1) * P],
                                                   AX_X, ALU.max, negate=True)
                last.then_inc(max_ready, 1)

            def scale_mixed(n, g):
                dve.wait_ge(mixed, C * n + g + 1)
                dve.wait_ge(inverted, QT * (C * n + g + 1))
                nc.vector.tensor_tensor(mixed_f[:], A_ps[:], over_sum[:], ALU.mult).then_inc(mixed_taken, 1)

            def low_mixed(n, g):
                dve.wait_ge(OT_hi, C * n + g + 1)
                nc.vector.tensor_tensor(OT[1][:, g, :], mixed_f[:], OT[0][:, g, :].bitcast(F32),
                                        ALU.subtract).then_inc(OT_lo, 1)

            def turn(b, first, last):
                norms = []
                if not first:
                    norms += [(1, b - 1, y, y_ready, 0), (2, b - 1, y, x1_ready, 10)]
                if not last:
                    norms.append((0, b + 1, x_in, x_in_s, 4))
                for s in range(H):
                    ending = [(k, n) for k, n, _, _, at in norms if s == at + QT]
                    for u in range(3) if s > 0 else ():
                        if u == 0:
                            for k, n in ending:
                                norm[k].await_stats(n)
                        maxima(b, s, u, first)
                        for k, n in ending:
                            (norm[k].aggregate, lambda: norm[k].halve(n), lambda: norm[k].shift_bits(n))[u]()
                        if s - 1 in AV_STEP:
                            invert_sums(b, AV_STEP.index(s - 1), u)
                    for k, n, src, ready, at in norms:
                        if at <= s < at + QT:
                            i = s - at
                            dve.wait_ge(ready, 16 * n + 16 if k == 0 else QT * n + i + 1)
                            norm[k].row_stats(src, i)
                    for k, n in ending:
                        norm[k].guess(n)
                    if s - 1 in AV_STEP:
                        invert_sums(b, AV_STEP.index(s - 1), QT - 1)
                    if s - 2 in AV_STEP:
                        scale_mixed(b, AV_STEP.index(s - 2))
                    if s - 3 in AV_STEP:
                        low_mixed(b, AV_STEP.index(s - 3))
                if not last:
                    for c in range(C):
                        low_x(b + 1, c, X_ps[c], xT1_hi, xT1_lo)
                low_mixed(b, C - 2)
                if not last:
                    for u in range(5):
                        low_qkv(b + 1, u)
                for i in range(QT):
                    invert_sums(b, C - 1, i)
                scale_mixed(b, C - 1)
                if not last:
                    take_v(b + 1)
                low_mixed(b, C - 1)
                if not first:
                    for c in range(C):
                        low_x(b - 1, c, X_ps[c], xT2_hi, xT2_lo)
                if not last:
                    for u in range(3):
                        maxima(b + 1, 0, u, False)
                take_projection(b, first)
                if not first:
                    take_logits(b - 1)

            for u in range(3):
                maxima(0, 0, u, True)
            turns(dve, turn)
            whole_norm(1, NB - 1, y, y_ready)
            whole_norm(2, NB - 1, y, x1_ready)
            for c in range(C):
                low_x(NB - 1, c, X_ps[c], xT2_hi, xT2_lo)
            take_logits(NB - 1)

        @block.scalar
        def _(act):
            def normalize(dst, src, k, n, i, done):
                act.wait_ge(norm[k].ready, n + 1)
                nc.scalar.activation(dst[:, i, :], src[:, i, :], ACT.Identity, bias=norm[k].bias[:, i:i + 1],
                                     scale=norm[k].rstd[:, i:i + 1]).then_inc(done, 1)

            def high_x(n, c, ps, ps_sem, hi_sem):
                act.wait_ge(ps_sem, C * n + c + 1)
                nc.scalar.activation(xT[0][:, c, :], ps[:], ACT.Copy).then_inc(hi_sem, 1)

            def high_qkv(n, u, start=False):
                act.wait_ge(qkv_ps, 5 * n + u + 1)
                if u == 0:
                    if start:
                        act.wait_ge(w_split, 2)
                    else:
                        act.wait_ge(k_moved, 48 * n)
                    nc.scalar.activation(vk[:], S_ps[0][0:2 * HD, :], ACT.Identity, bias=vkbs_s[:],
                                         scale=vks_s[:]).then_inc(qkv_hi, 1)
                else:
                    if u > 2:
                        act.wait_ge(q_spilled[u - 3], 32 * n + 32)
                    elif not start:
                        act.wait_ge(q_spilled[u + 1], 32 * n)
                    nc.scalar.activation(q_h[(u - 1) % 2][0][:], UNIT_PS[u][:], ACT.Identity,
                                         bias=qb_s[:, u - 1:u]).then_inc(qkv_hi, 1)

            for i in range(QT):
                normalize(x_in, x_in, 0, 0, i, x_normed)
            for c in range(C):
                high_x(0, c, X_ps[c], xT1_ps, xT1_hi)
            for u in range(5):
                high_qkv(0, u, True)

            def high_mixed(n, g, start=False):
                act.wait_ge(mixed_taken, C * n + g + 1)
                if g == 0 and not start:
                    act.wait_ge(projected, QT * n)
                nc.scalar.activation(OT[0][:, g, :], mixed_f[:], ACT.Copy).then_inc(OT_hi, 1)

            def take_lgT(n):
                act.wait_ge(rt_ps, n + 1)
                nc.scalar.activation(lgT, sum_ps[0:R, :], ACT.Copy).then_inc(lgT_ready, 1)

            def turn(b, first, last):
                def exp(h, tb):
                    act.wait_ge(shifted, 3 * H * b + 3 * h + tb + 1)
                    g = h // HG
                    if h % HG == 0 and tb == 0:
                        if g >= 2:
                            act.wait_ge(mixed, C * b + g - 1)
                        elif not first:
                            act.wait_ge(mixed, C * b)
                    nc.scalar.activation(PT[g % 2][:, h % HG, TFROM[tb]:TFROM[tb] + TW[tb]],
                                         T_ps[tb][:, 0:TW[tb]], ACT.Exp).then_inc(pt_ready, 1)

                for s in range(1, H + 1):
                    if s - 3 in AV_STEP[:C - 2]:
                        high_mixed(b, AV_STEP.index(s - 3), first)
                    if s == H and not last:
                        for c in range(C):
                            high_x(b + 1, c, X_ps[c], xT1_ps, xT1_hi)
                    if s == H:
                        high_mixed(b, C - 2)
                    for tb in range(3):
                        exp(s - 1, tb)
                    for i in (0, 1) if s % 2 == 0 else (2, 3):
                        if s in (8, 9) and not first:
                            normalize(y, y, 1, b - 1, i, y_normed)
                        if s in (12, 13) and not last:
                            normalize(x_in, x_in, 0, b + 1, i, x_normed)
                    if s == H and not last:
                        high_qkv(b + 1, 0)
                        high_qkv(b + 1, 1)
                if not last:
                    for u in (2, 3, 4):
                        high_qkv(b + 1, u)
                if not first:
                    act.wait_ge(xn_stored, 16 * b - 16)
                    for i in range(QT):
                        normalize(xn2, y, 2, b - 1, i, xn_ready)
                high_mixed(b, C - 1)
                if not first:
                    for c in range(C):
                        high_x(b - 1, c, X_ps[c], xT2_ps, xT2_hi)
                    take_lgT(b - 1)

            turns(act, turn)
            for i in range(QT):
                normalize(y, y, 1, NB - 1, i, y_normed)
            act.wait_ge(xn_stored, 16 * NB - 16)
            for i in range(QT):
                normalize(xn2, y, 2, NB - 1, i, xn_ready)
            for c in range(C):
                high_x(NB - 1, c, X_ps[c], xT2_ps, xT2_hi)
            take_lgT(NB - 1)

        @block.gpsimd
        def _(pool):
            def add_residual(n, i):
                pool.wait_ge(x_res_s, 16 * n + 16)
                pool.wait_ge(y_normed, QT * n + i + 1)
                nc.gpsimd.tensor_tensor(y[:, i, :], y[:, i, :], x_res[:, i, :], ALU.add).then_inc(x1_ready, 1)

            nc.gpsimd.memset(ones_f[:], 1.0).then_inc(ones_ready, 1)
            pool.wait_ge(ones_ready, 1)
            nc.gpsimd.tensor_copy(ones[:], ones_f[:].rearrange("p t d -> p (t d)")).then_inc(ones_ready, 1)

            def turn(b, first, last):
                for h in range(H):
                    pool.wait_ge(max_ready, 3 * H * b + 3 * h + 3)
                    if h >= 3:
                        pool.wait_ge(shifted, 3 * H * b + 3 * (h - 2))
                    elif not first:
                        pool.wait_ge(shifted, 3 * H * b)
                    nc.gpsimd.tensor_tensor(minus_max[h % 3][:], idf[:].unsqueeze(1).to_broadcast([P, QT, P]),
                                            nmax[:, h % 3, :].unsqueeze(2).to_broadcast([P, QT, P]),
                                            ALU.mult).then_inc(diagonal_ready, 1)
                    if h == 5 and not first:
                        norm[1].refine(b - 1)
                    if h == 8 and not last:
                        norm[0].refine(b + 1)
                    if 8 <= h < 8 + QT and not first:
                        add_residual(b - 1, h - 8)
                if not first:
                    norm[2].refine(b - 1)

            norm[0].refine(0)
            turns(pool, turn)
            norm[1].refine(NB - 1)
            for i in range(QT):
                add_residual(NB - 1, i)
            norm[2].refine(NB - 1)


def build_routing(nc, logits, gate, weight, slot, token_of_slot, tile_expert, idx_hi=None):
    ctx = ExitStack()
    with ctx:
        def sb(name, shape, dt=F32):
            return ctx.enter_context(nc.sbuf_tensor("ro_" + name, shape, dt))

        def sem(name):
            return ctx.enter_context(nc.semaphore("ro_" + name))

        first_place = sb("first_place", [P, E])
        slots_before = sb("slots_before", [P, E])
        tile_no = sb("tile_no", [P, NT])
        lane_no = sb("lane_no", [P, P])
        column_no = sb("column_no", [P, SC])
        token_no = sb("token_no", [P, NTT])
        before = sb("before", [P, P], BF16)
        ones = sb("ones", [P, P], BF16)
        top = sb("top", [P, 4, NTT])
        inv = sb("inv", [P, NTT])
        prob = sb("prob", [P, NTT, E])
        t1 = sb("t1", [P, NTT, E])
        t2 = sb("t2", [P, NTT, E])
        pick = [sb(f"pick{k}", [P, NTT, E]) for k in range(2)]
        picked = sb("picked", [P, NTT, E], BF16)
        count = [sb(f"count{k}", [P, NTT, E]) for k in range(2)]
        total = sb("total", [P, NTT, E])
        tiles = [sb(f"tiles{k}", [P, E]) for k in range(2)]
        over = sb("over", [P, NT, E])
        base = sb("base", [P, E])
        tile_e = sb("tile_e", [P, NT])
        place = sb("place", [P, 2, NTT])
        digit = sb("digit", [P, 2, 2, NTT], I32)
        digit_f = sb("digit_f", [P, 2, 2, NTT])
        lane_hot = [sb(f"lane_hot{k}", [P, P], F32R) for k in range(4)]
        column_hot = sb("column_hot", [P, 2, NTT, SC], F32R)
        rank_ps = ctx.enter_context(nc.psum_tensor("ro_rank_ps", [P, NTT * E], F32))
        total_ps = ctx.enter_context(nc.psum_tensor("ro_total_ps", [P, NTT * E], F32))
        inverse_ps = ctx.enter_context(nc.psum_tensor("ro_inverse_ps", [P, 512], F32))

        constants, shifted, exponentials = sem("constants"), sem("shifted"), sem("exponentials")
        negated_gate, picks_ready, counted, hot, used, inverse_done = (
            sem("negated_gate"), sem("picks_ready"), sem("counted"), sem("hot"), sem("used"), sem("inverse_done"))
        own = sem("own")
        PART = NTT // 4
        block = ctx.enter_context(nc.Block())

        def over_experts(ap):
            return ap.unsqueeze(2).to_broadcast([P, NTT, E])

        def over_tiles(ap):
            return ap.unsqueeze(1).to_broadcast([P, NTT, E])

        @block.gpsimd
        def _(pool):
            nc.gpsimd.iota(first_place[:], [[-1, E]], base=E, channel_multiplier=0, allow_small_or_imprecise_dtypes=True)
            nc.gpsimd.iota(slots_before[:], [[TS, E]], base=0, channel_multiplier=0, allow_small_or_imprecise_dtypes=True)
            nc.gpsimd.iota(tile_no[:], [[1, NT]], base=0, channel_multiplier=0, allow_small_or_imprecise_dtypes=True)
            nc.gpsimd.iota(lane_no[:], [[1, P]], base=0, channel_multiplier=0, allow_small_or_imprecise_dtypes=True)
            nc.gpsimd.iota(column_no[:], [[1, SC]], base=0, channel_multiplier=0, allow_small_or_imprecise_dtypes=True)
            nc.gpsimd.iota(token_no[:], [[P, NTT]], base=0, channel_multiplier=1, allow_small_or_imprecise_dtypes=True)
            nc.gpsimd.memset(ones[:], 1.0).then_inc(constants, 1)
            pool.wait_ge(constants, 1)
            nc.gpsimd.affine_select(out=before[:], in_=ones[:], compare_op=ALU.is_gt, fill=0.0, base=0,
                                    pattern=[[1, P]], channel_multiplier=-1).then_inc(constants, 1)

        @block.scalar
        def _(act):
            act.wait_ge(shifted, 1)
            nc.scalar.activation(prob[:], t1[:], ACT.Exp)
            nc.scalar.activation(gate[:], logits[:, :, E], ACT.Exp, scale=-1.0).then_inc(exponentials, 1)

        @block.tensor
        def _(pe):
            pe.wait_ge(constants, 2)
            pe.wait_ge(picks_ready, 1)
            nc.tensor.matmul(rank_ps[:], before[:], picked[:].rearrange("p t e -> p (t e)"), start=True, stop=True)
            nc.tensor.matmul(total_ps[:], ones[:], picked[:].rearrange("p t e -> p (t e)"),
                             start=True, stop=True).then_inc(counted, 1)
            for n in range(2 * NTT):
                pe.wait_ge(hot, n + 1)
                last = nc.tensor.matmul(inverse_ps[:, 0:SC], lane_hot[n % 4][:],
                                        column_hot[:, n // NTT, n % NTT, :],
                                        start=(n == 0), stop=(n == 2 * NTT - 1))
                last.then_inc(used, 1)

        @block.vector
        def _(dve):
            steps = Steps(dve, own)
            dve.wait_ge(constants, 2)
            scores = logits[:, :, 0:E]
            steps.then_wait(nc.vector.tensor_reduce(top[:, 0, :], scores, AX_X, ALU.max))
            nc.vector.tensor_tensor(t1[:], scores, over_experts(top[:, 0, :]), ALU.subtract).then_inc(shifted, 1)
            dve.wait_ge(exponentials, 1)
            steps.then_wait(nc.vector.tensor_scalar(gate[:], gate[:], 1.0, None, ALU.add))
            nc.vector.reciprocal(gate[:], gate[:])
            steps.then_wait(nc.vector.tensor_reduce(top[:, 1, :], prob[:], AX_X, ALU.add))
            steps.then_wait(nc.vector.reciprocal(inv[:], top[:, 1, :]))
            steps.then_wait(nc.vector.tensor_tensor(prob[:], prob[:], over_experts(inv[:]), ALU.mult))
            for k in range(2):
                src = prob if k == 0 else t2
                steps.then_wait(nc.vector.tensor_reduce(top[:, 2 + k, :], src[:], AX_X, ALU.max))
                steps.then_wait(nc.vector.tensor_tensor(t1[:], src[:], over_experts(top[:, 2 + k, :]), ALU.is_equal))
                steps.then_wait(nc.vector.tensor_tensor(t1[:], t1[:], over_tiles(first_place[:]), ALU.mult))
                steps.then_wait(nc.vector.tensor_reduce(inv[:], t1[:], AX_X, ALU.max))
                steps.then_wait(nc.vector.tensor_tensor(pick[k][:], over_tiles(first_place[:]),
                                                        over_experts(inv[:]), ALU.is_equal))
                if k == 0:
                    steps.then_wait(nc.vector.scalar_tensor_tensor(out=t2[:], in0=pick[0][:], scalar=-2.0,
                                                                   in1=prob[:], op0=ALU.mult, op1=ALU.add))
            nc.vector.tensor_tensor(picked[:], pick[0][:], pick[1][:], ALU.add).then_inc(picks_ready, 1)
            steps.then_wait(nc.vector.tensor_tensor(top[:, 1, :], top[:, 2, :], top[:, 3, :], ALU.add))
            steps.then_wait(nc.vector.reciprocal(inv[:], top[:, 1, :]))
            nc.vector.tensor_tensor(weight[:, 0, :], top[:, 2, :], inv[:], ALU.mult)
            nc.vector.tensor_tensor(weight[:, 1, :], top[:, 3, :], inv[:], ALU.mult)
            dve.wait_ge(counted, 1)
            nc.vector.tensor_copy(count[0][:].rearrange("p t e -> p (t e)"), total_ps[:])
            steps.then_wait(nc.vector.tensor_copy(total[:].rearrange("p t e -> p (t e)"), total_ps[:]))
            a, shift = 0, 1
            while shift < NTT:
                nc.vector.tensor_copy(count[1 - a][:, 0:shift, :], count[a][:, 0:shift, :])
                steps.then_wait(nc.vector.tensor_tensor(count[1 - a][:, shift:, :], count[a][:, shift:, :],
                                                        count[a][:, 0:NTT - shift, :], ALU.add))
                a, shift = 1 - a, 2 * shift
            n_of = count[a][:, NTT - 1, :]
            steps.then_wait(nc.vector.tensor_tensor(over[:, 0:E, :], n_of.unsqueeze(2).to_broadcast([P, E, E]),
                                                    slots_before[:].unsqueeze(1).to_broadcast([P, E, E]), ALU.is_gt))
            steps.then_wait(nc.vector.tensor_reduce(tiles[0][:], over[:, 0:E, :], AX_X, ALU.add))
            steps.then_wait(nc.vector.tensor_copy(base[:], tiles[0][:]))
            b, shift = 0, 1
            while shift < E:
                nc.vector.tensor_copy(tiles[1 - b][:, 0:shift], tiles[b][:, 0:shift])
                steps.then_wait(nc.vector.tensor_tensor(tiles[1 - b][:, shift:], tiles[b][:, shift:],
                                                        tiles[b][:, 0:E - shift], ALU.add))
                b, shift = 1 - b, 2 * shift
            end = tiles[b]
            steps.then_wait(nc.vector.tensor_tensor(over[:], tile_no[:].unsqueeze(2).to_broadcast([P, NT, E]),
                                                    end[:].unsqueeze(1).to_broadcast([P, NT, E]), ALU.is_ge))
            steps.then_wait(nc.vector.tensor_reduce(tile_e[:], over[:], AX_X, ALU.add))
            nc.vector.tensor_scalar(tile_expert[:], tile_e[0:1, :], float(E - 1), None, ALU.min)
            steps.then_wait(nc.vector.tensor_tensor(base[:], end[:], base[:], ALU.subtract))
            steps.then_wait(nc.vector.tensor_scalar(base[:], base[:], float(TS), None, ALU.mult))
            steps.then_wait(nc.vector.tensor_tensor(t1[:], count[a][:], total[:], ALU.subtract))
            steps.then_wait(nc.vector.tensor_tensor(t1[:], t1[:], over_tiles(base[:]), ALU.add))
            steps.then_wait(nc.vector.tensor_tensor(t1[:].rearrange("p t e -> p (t e)"),
                                                    t1[:].rearrange("p t e -> p (t e)"), rank_ps[:], ALU.add))
            for k in range(2):
                steps.then_wait(nc.vector.tensor_tensor(t2[:], pick[k][:], t1[:], ALU.mult))
                steps.then_wait(nc.vector.tensor_reduce(place[:, k, :], t2[:], AX_X, ALU.add))
            steps.then_wait(nc.vector.tensor_copy(slot[:], place[:]))
            nc.vector.tensor_scalar(digit[:, 0], slot[:], 7, None, ALU.logical_shift_right)
            steps.then_wait(nc.vector.tensor_scalar(digit[:, 1], slot[:], P - 1, None, ALU.bitwise_and))
            steps.then_wait(nc.vector.tensor_copy(digit_f[:], digit[:]))
            for n in range(2 * NTT):
                k, t = divmod(n, NTT)
                if t % PART == 0:
                    nc.vector.tensor_tensor(column_hot[:, k, t:t + PART, :],
                                            column_no[:].unsqueeze(1).to_broadcast([P, PART, SC]),
                                            digit_f[:, 0, k, t:t + PART].unsqueeze(2).to_broadcast([P, PART, SC]),
                                            ALU.is_equal)
                if n >= 4:
                    dve.wait_ge(used, n - 3)
                nc.vector.tensor_scalar(lane_hot[n % 4][:], lane_no[:], digit_f[:, 1, k, t:t + 1],
                                        token_no[:, t:t + 1], ALU.is_equal, ALU.mult).then_inc(hot, 1)
            dve.wait_ge(used, 2 * NTT)
            nc.vector.tensor_copy(token_of_slot[:], inverse_ps[:, 0:SC]).then_inc(inverse_done, 1)
            dve.wait_ge(inverse_done, 1)


class GatedProducts:

    def __init__(self, nc, pe, rows, xT, act, gate_up_ps, out_ps, sems):
        self.nc, self.pe, self.rows, self.xT, self.act = nc, pe, rows, xT, act
        self.gate_up_ps, self.out_ps, self.s = gate_up_ps, out_ps, sems
        self.NC = len(rows)

    def gate_up(self, n, c, gate_cols, up_cols):
        pe, m = self.pe, self.rows[c]
        if c >= 2:
            pe.wait_ge(self.s["act_ready"], self.NC * n + c - 1)
        for which, cols in enumerate((gate_cols, up_cols)):
            step = 0
            for k in range(C):
                for i, j in PASSES:
                    last = self.nc.tensor.matmul(self.gate_up_ps[c % 2][which][0:m, :], cols(i, k), self.xT[j][:, k, :],
                                                 start=(step == 0), stop=(step == 3 * C - 1))
                    step += 1
        last.then_inc(self.s["gate_up_done"], 1)

    def down(self, n, c, weights):
        pe, m = self.pe, self.rows[c]
        if c == 0:
            pe.wait_ge(self.s["out_taken"], QT * n)
        pe.wait_ge(self.s["act_ready"], self.NC * n + c + 1)
        for i in range(QT):
            for step, (j, k) in enumerate(PASSES):
                last = self.nc.tensor.matmul(self.out_ps[i][:], self.act[c % 2][j][0:m, i * P:(i + 1) * P], weights(k),
                                             start=(c == 0 and step == 0), stop=(c == self.NC - 1 and step == 2))
            if c == self.NC - 1:
                last.then_inc(self.s["out_done"], 1)
        if c < self.NC - 1:
            last.then_inc(self.s["down_done"], 1)

    def transpose_x(self, src, c, idf):
        ps = self.gate_up_ps[1 - c // 2][c % 2]
        for t in range(QT):
            last = self.nc.tensor.transpose(ps[:, t * P:(t + 1) * P], src[:, t, c * P:(c + 1) * P], idf[:])
        last.then_inc(self.s["xT_done"], 1)


def high_x(nc, n, c, xT, gate_up_ps, s):
    nc.scalar.wait_ge(s["xT_done"], C * n + c + 1)
    nc.scalar.activation(xT[0][:, c, :], gate_up_ps[1 - c // 2][c % 2][:], ACT.Copy).then_inc(s["xT_hi"], 1)


def low_x(nc, n, c, xT, gate_up_ps, s):
    nc.vector.wait_ge(s["xT_hi"], C * n + c + 1)
    nc.vector.tensor_tensor(xT[1][:, c, :], gate_up_ps[1 - c // 2][c % 2][:], xT[0][:, c, :].bitcast(F32),
                            ALU.subtract).then_inc(s["xT_lo"], 1)


def gate_silu(nc, n, c, rows, silu, gate_up_ps, s):
    NC, m = len(rows), rows[c]
    nc.scalar.wait_ge(s["gate_up_done"], NC * n + c + 1)
    nc.scalar.wait_ge(s["act_ready"], NC * n + max(c - 1, 0))
    nc.scalar.activation(silu[c % 2][0:m, :], gate_up_ps[c % 2][0][0:m, :], ACT.Silu).then_inc(s["silu_ready"], 1)


def gate_times_up(nc, n, c, rows, silu, act, gate_up_ps, s):
    NC, m = len(rows), rows[c]
    nc.vector.wait_ge(s["silu_ready"], NC * n + c + 1)
    nc.vector.tensor_tensor(silu[c % 2][0:m, :], silu[c % 2][0:m, :], gate_up_ps[c % 2][1][0:m, :],
                            ALU.mult).then_inc(s["product"], 1)
    nc.vector.wait_ge(s["product"], 2 * (NC * n + c) + 1)
    if c >= 2:
        nc.vector.wait_ge(s["down_done"], (NC - 1) * n + c - 1)
    else:
        nc.vector.wait_ge(s["out_done"], QT * n)
    nc.vector.tensor_copy(act[c % 2][0][0:m, :], silu[c % 2][0:m, :]).then_inc(s["product"], 1)
    nc.vector.wait_ge(s["product"], 2 * (NC * n + c) + 2)
    nc.vector.tensor_tensor(act[c % 2][1][0:m, :], silu[c % 2][0:m, :], act[c % 2][0][0:m, :].bitcast(F32),
                            ALU.subtract).then_inc(s["act_ready"], 1)


GATED_SEMS = ("xT_done", "xT_hi", "xT_lo", "gate_up_done", "silu_ready", "product", "act_ready", "down_done",
              "out_done", "out_taken")


def build_experts(nc, xn, gu, dn, ys, token_of_slot, tile_expert, idf):
    ctx = ExitStack()
    with ctx:
        def sb(name, shape, dt=F32):
            return ctx.enter_context(nc.sbuf_tensor("ex_" + name, shape, dt))

        def sem(name):
            return ctx.enter_context(nc.semaphore("ex_" + name))

        rows = [P] * (I_MOE // P) + [I_MOE % P]
        NC = len(rows)
        gu_in = sb("gu_in", [P, C, 2 * I_MOE])
        dn_in = sb("dn_in", [P, NC, D])
        gu_s = [[sb(f"gu{r}{j}", [P, C, 2 * I_MOE], F32R) for j in range(2)] for r in range(2)]
        dn_s = [[sb(f"dn{r}{j}", [P, NC, D], F32R) for j in range(2)] for r in range(2)]
        xg = [sb(f"xg{r}", [P, QT, D]) for r in range(2)]
        index = [sb(f"index{r}", [P, QT], U32) for r in range(2)]
        xT = [sb(f"xT{j}", [P, C, TS], F32R) for j in range(2)]
        silu = [sb(f"silu{r}", [P, TS]) for r in range(2)]
        act_s = [[sb(f"act{r}{j}", [P, TS], F32R) for j in range(2)] for r in range(2)]
        y_out = sb("y_out", [P, QT, D])
        bank = [ctx.enter_context(nc.psum_tensor(f"ex_bank{i}", [P, 512], F32)) for i in range(8)]
        gate_up_ps, out_ps = [bank[0:2], bank[2:4]], bank[4:8]
        s = {name: sem(name) for name in GATED_SEMS}
        w_in, w_hi, w_lo, w_free = sem("w_in"), sem("w_hi"), sem("w_lo"), sem("w_free")
        gathered = [sem(f"gathered{r}") for r in range(2)]
        index_ready, stored = [sem(f"index_ready{r}") for r in range(2)], sem("stored")
        PIECES = [(0, k) for k in range(C)] + [(1, c) for c in range(NC)]
        TURN = [PIECES[0:3], PIECES[3:5], PIECES[5:7]]
        WN = len(PIECES)

        def piece(which, k, src, halves, j=None):
            m = P if which == 0 else rows[k]
            t = (src[which] if j is None else halves[which][j])
            return t[0:m, k, :]

        block = ctx.enter_context(nc.Block())

        def turns(engine, turn):
            with engine.Fori(0, NT // 2) as pair:
                turn(2 * pair, 0, False)
                turn(2 * pair + 1, 1, False)
            turn(NT - 1, 0, True)

        @block.sync
        def _(sp):
            def load(n):
                e = sp.value_load(tile_expert[0:1, bass.ds(n, 1)], min_val=0, max_val=E - 1)
                sp.dma_start(gu_in[:], gu[bass.ds(e, 1)].rearrange("o p k i -> p (o k) i")).then_inc(w_in, 16)
                full = NC - 1
                sp.dma_start(dn_in[:, 0:full, :], dn[bass.ds(e, 1), 0:full * P].rearrange(
                    "o (c p) d -> p (o c) d", p=P)).then_inc(w_in, 16)
                sp.dma_start(dn_in[0:rows[-1], full, :], dn[bass.ds(e, 1), full * P:I_MOE].rearrange(
                    "o p d -> (o p) d")).then_inc(w_in, 16)

            load(0)

            def turn(n, r, last):
                if not last:
                    sp.wait_ge(w_lo, WN * n + WN)
                    load(n + 1)
                sp.wait_ge(s["out_taken"], QT * n + QT)
                sp.dma_start(ys[bass.ds(n, 1)].rearrange("o p t d -> p (o t) d"), y_out[:]).then_inc(stored, 16)

            turns(sp, turn)
            sp.wait_ge(stored, 16 * NT)

        @block.gpsimd
        def _(pool):
            def gather(n, r, uses):
                nc.gpsimd.tensor_copy(index[r][:], token_of_slot[:, bass.ds(QT * n, QT)]).then_inc(index_ready[r], 1)
                pool.wait_ge(index_ready[r], 1)
                pool.wait_ge(index_ready[r], uses)
                for t in range(QT):
                    pool.indirect_dma_start(out=xg[r][:, t, :], out_offset=None, in_=xn,
                                            in_offset=bass.IndirectOffsetOnAxis(ap=index[r][:, t:t + 1], axis=0)
                                            ).then_inc(gathered[r], 16)

            gather(0, 0, 1)
            gather(1, 1, 1)
            with pool.Fori(2, NT // 2 + 1) as uses:
                pool.wait_ge(s["xT_done"], 2 * C * uses - 3 * C)
                gather(2 * uses - 2, 0, uses)
                pool.wait_ge(s["xT_done"], 2 * C * uses - 2 * C)
                gather(2 * uses - 1, 1, uses)
            pool.wait_ge(s["xT_done"], C * (NT - 2))
            gather(NT - 1, 0, NT // 2 + 1)

        @block.tensor
        def _(pe):
            g = GatedProducts(nc, pe, rows, xT, act_s, gate_up_ps, out_ps, s)
            pe.wait_ge(gathered[0], 16 * QT)
            for c in range(C):
                g.transpose_x(xg[0], c, idf)

            def turn(n, r, last):
                def gate(c):
                    return lambda j, k: gu_s[r][j][:, k, c * P:c * P + rows[c]]

                def up(c):
                    return lambda j, k: gu_s[r][j][:, k, I_MOE + c * P:I_MOE + c * P + rows[c]]

                pe.wait_ge(s["xT_lo"], C * n + C)
                pe.wait_ge(w_lo, WN * n + WN)
                for c in range(NC):
                    g.gate_up(n, c, gate(c), up(c))
                    if c == NC - 1 and not last:
                        pe.wait_ge(gathered[1 - r], 16 * QT * ((n - r) // 2 + 1 + r) if isinstance(n, int)
                                   else 8 * QT * (n - r) + 16 * QT * (1 + r))
                        pe.wait_ge(s["act_ready"], NC * n + NC - 1)
                        g.transpose_x(xg[1 - r], 0, idf)
                        g.transpose_x(xg[1 - r], 1, idf)
                    if c > 0:
                        g.down(n, c - 1, lambda k: dn_s[r][k][0:rows[c - 1], c - 1, :])
                if not last:
                    pe.wait_ge(s["act_ready"], NC * n + NC)
                    g.transpose_x(xg[1 - r], 2, idf)
                    g.transpose_x(xg[1 - r], 3, idf)
                g.down(n, NC - 1, lambda k: dn_s[r][k][0:rows[NC - 1], NC - 1, :])

            turns(pe, turn)

        def split_hi(n, r, q):
            which, k = PIECES[q]
            nc.scalar.wait_ge(w_in, 48 * n + 48)
            nc.scalar.activation(piece(which, k, None, (gu_s[r], dn_s[r]), 0), piece(which, k, (gu_in, dn_in), None),
                                 ACT.Copy).then_inc(w_hi, 1)

        def split_lo(n, r, q):
            which, k = PIECES[q]
            nc.vector.wait_ge(w_hi, WN * n + q + 1)
            nc.vector.tensor_tensor(piece(which, k, None, (gu_s[r], dn_s[r]), 1), piece(which, k, (gu_in, dn_in), None),
                                    piece(which, k, None, (gu_s[r], dn_s[r]), 0).bitcast(F32),
                                    ALU.subtract).then_inc(w_lo, 1)

        @block.scalar
        def _(act):
            for q in range(WN):
                split_hi(0, 0, q)
            for c in range(C):
                high_x(nc, 0, c, xT, gate_up_ps, s)

            def turn(n, r, last):
                q = 0
                for c in range(NC):
                    gate_silu(nc, n, c, rows, silu, gate_up_ps, s)
                    if not last:
                        for _ in TURN[c]:
                            if q == 0:
                                act.wait_ge(s["out_done"], QT * n)
                            split_hi(n + 1, 1 - r, q)
                            q += 1
                if not last:
                    for c in range(C):
                        high_x(nc, n + 1, c, xT, gate_up_ps, s)
                act.wait_ge(stored, 16 * n)
                for i in range(QT):
                    act.wait_ge(s["out_done"], QT * n + i + 1)
                    nc.scalar.activation(y_out[:, i, :], out_ps[i][:], ACT.Copy).then_inc(s["out_taken"], 1)

            turns(act, turn)

        @block.vector
        def _(dve):
            for q in range(WN):
                split_lo(0, 0, q)
            for c in range(C):
                low_x(nc, 0, c, xT, gate_up_ps, s)

            def turn(n, r, last):
                q = 0
                for c in range(NC):
                    gate_times_up(nc, n, c, rows, silu, act_s, gate_up_ps, s)
                    if not last:
                        for _ in TURN[c]:
                            split_lo(n + 1, 1 - r, q)
                            q += 1
                if not last:
                    for c in range(C):
                        low_x(nc, n + 1, c, xT, gate_up_ps, s)

            turns(dve, turn)


def build_shared(nc, xn, shg, shu, shd, ys, x1, out, gate, weight, slot, idf, norm_constants):
    ctx = ExitStack()
    with ctx:
        def sb(name, shape, dt=F32):
            return ctx.enter_context(nc.sbuf_tensor("sh_" + name, shape, dt))

        def sem(name):
            return ctx.enter_context(nc.semaphore("sh_" + name))

        NC = I_SH // P
        rows = [P] * NC
        gate_s = [sb(f"gate{j}", [P, C, I_SH], F32R) for j in range(2)]
        up_s = [sb(f"up{j}", [P, C, I_SH], F32R) for j in range(2)]
        dn_s = [sb(f"dn{j}", [P, NC, D], F32R) for j in range(2)]
        x_in = sb("x_in", [P, QT, D])
        xT = [sb(f"xT{j}", [P, C, TS], F32R) for j in range(2)]
        silu = [sb(f"silu{r}", [P, TS]) for r in range(2)]
        act_s = [[sb(f"act{r}{j}", [P, TS], F32R) for j in range(2)] for r in range(2)]
        f = sb("f", [P, QT, D])
        yk = [sb(f"yk{k}", [P, QT, D]) for k in range(2)]
        index = sb("index", [P, 2, QT], U32)
        scales = sb("scales", [P, 3, QT])
        norm = InverseStd(nc, sb, sem, "", norm_constants)
        bank = [ctx.enter_context(nc.psum_tensor(f"sh_bank{i}", [P, 512], F32)) for i in range(8)]
        gate_up_ps, out_ps = [bank[0:2], bank[2:4]], bank[4:8]
        s = {name: sem(name) for name in GATED_SEMS}
        w_in, w_hi, w_lo = [sem(f"w_in{r}") for r in range(2)], sem("w_hi"), sem("w_lo")
        x_in_s, x1_in, stored = sem("x_in_s"), sem("x1_in"), sem("stored")
        index_ready = sem("index_ready")
        gathered = [sem(f"gathered{i}") for i in range(QT)]
        scales_ready, added, normed, finished = sem("scales_ready"), sem("added"), sem("normed"), sem("finished")
        stage = [f, yk[0]]
        block = ctx.enter_context(nc.Block())

        def seq(dram, b):
            return dram[bass.ds(b, 1)].rearrange("o p t d -> p (o t) d")

        def turns(engine, turn):
            with engine.Fori(0, NB - 1) as b:
                turn(b, False)
            turn(NB - 1, True)

        @block.sync
        def _(sp):
            sp.dma_start(x_in[:], seq(xn, 0)).then_inc(x_in_s, 16)
            for c in range(NC):
                r = c % 2
                if c >= 2:
                    sp.wait_ge(w_lo, c - 1)
                cols = slice(c * P, (c + 1) * P)
                sp.dma_start(stage[r][:, :, 0:P], shg[:, :, cols]).then_inc(w_in[r], 16)
                sp.dma_start(stage[r][:, :, P:2 * P], shu[:, :, cols]).then_inc(w_in[r], 16)
                sp.dma_start(stage[r][:, 0, 2 * P:4 * P], shd[:, c, 0:2 * P]).then_inc(w_in[r], 16)
                sp.dma_start(stage[r][:, 1, 2 * P:4 * P], shd[:, c, 2 * P:4 * P]).then_inc(w_in[r], 16)

            def turn(b, last):
                if not last:
                    sp.wait_ge(s["xT_done"], C * b + C)
                    sp.dma_start(x_in[:], seq(xn, b + 1)).then_inc(x_in_s, 16)
                sp.wait_ge(added, 2 * QT * b + 2 * QT)
                sp.dma_start(yk[0][:], seq(x1, b)).then_inc(x1_in, 16)
                sp.wait_ge(finished, QT * b + QT)
                sp.dma_start(seq(out, b), f[:]).then_inc(stored, 16)

            turns(sp, turn)
            sp.wait_ge(stored, 16 * NB)

        @block.tensor
        def _(pe):
            g = GatedProducts(nc, pe, rows, xT, act_s, gate_up_ps, out_ps, s)
            pe.wait_ge(x_in_s, 16)
            for c in range(C):
                g.transpose_x(x_in, c, idf)

            def turn(b, last):
                pe.wait_ge(s["xT_lo"], C * b + C)
                for c in range(NC):
                    pe.wait_ge(w_lo, c + 1)
                    g.gate_up(b, c, lambda j, k: gate_s[j][:, k, c * P:(c + 1) * P],
                              lambda j, k: up_s[j][:, k, c * P:(c + 1) * P])
                    if c == NC - 1 and not last:
                        pe.wait_ge(x_in_s, 16 * b + 32)
                        pe.wait_ge(s["act_ready"], NC * b + NC - 1)
                        g.transpose_x(x_in, 0, idf)
                        g.transpose_x(x_in, 1, idf)
                    if c > 0:
                        g.down(b, c - 1, lambda k: dn_s[k][:, c - 1, :])
                if not last:
                    pe.wait_ge(s["act_ready"], NC * b + NC)
                    g.transpose_x(x_in, 2, idf)
                    g.transpose_x(x_in, 3, idf)
                g.down(b, NC - 1, lambda k: dn_s[k][:, NC - 1, :])

            turns(pe, turn)

        def pieces(c, j):
            r, cols = c % 2, slice(c * P, (c + 1) * P)
            return [(gate_s[j][:, :, cols], stage[r][:, :, 0:P]), (up_s[j][:, :, cols], stage[r][:, :, P:2 * P]),
                    (dn_s[j][:, c, :].rearrange("p (a d) -> p a d", a=2), stage[r][:, 0:2, 2 * P:4 * P])]

        @block.scalar
        def _(act):
            def split_hi(c):
                act.wait_ge(w_in[c % 2], 64 * (c // 2) + 64)
                for dst, src in pieces(c, 0):
                    last = nc.scalar.activation(dst, src, ACT.Copy)
                last.then_inc(w_hi, 1)

            split_hi(0)
            for c in range(C):
                high_x(nc, 0, c, xT, gate_up_ps, s)
            for c in range(1, NC):
                split_hi(c)
                gate_silu(nc, 0, c - 1, rows, silu, gate_up_ps, s)

            def normalize(b):
                for i in range(QT):
                    act.wait_ge(norm.ready, b + 1)
                    nc.scalar.activation(f[:, i, :], f[:, i, :], ACT.Identity, bias=norm.bias[:, i:i + 1],
                                         scale=norm.rstd[:, i:i + 1]).then_inc(normed, 1)

            def turn(b, last, begun=0):
                for c in range(begun, NC):
                    gate_silu(nc, b, c, rows, silu, gate_up_ps, s)
                    if c == 3 and begun == 0:
                        normalize(b - 1)
                if not last:
                    for c in range(C):
                        high_x(nc, b + 1, c, xT, gate_up_ps, s)
                act.wait_ge(scales_ready, b + 1)
                act.wait_ge(stored, 16 * b)
                for i in range(QT):
                    act.wait_ge(s["out_done"], QT * b + i + 1)
                    nc.scalar.activation(f[:, i, :], out_ps[i][:], ACT.Copy,
                                         scale=scales[:, 2, i:i + 1]).then_inc(s["out_taken"], 1)

            turn(0, False, NC - 1)
            with act.Fori(1, NB - 1) as b:
                turn(b, False)
            turn(NB - 1, True)
            normalize(NB - 1)

        @block.vector
        def _(dve):
            def split_lo(c):
                dve.wait_ge(w_hi, c + 1)
                for (dst, src), (high, _) in zip(pieces(c, 1), pieces(c, 0)):
                    last = nc.vector.tensor_tensor(dst, src, high.bitcast(F32), ALU.subtract)
                last.then_inc(w_lo, 1)

            split_lo(0)
            for c in range(C):
                low_x(nc, 0, c, xT, gate_up_ps, s)
            for c in range(1, NC):
                split_lo(c)
                gate_times_up(nc, 0, c - 1, rows, silu, act_s, gate_up_ps, s)

            def turn(b, last, begun=0):
                for c in range(begun, NC):
                    gate_times_up(nc, b, c, rows, silu, act_s, gate_up_ps, s)
                if not last:
                    for c in range(C):
                        low_x(nc, b + 1, c, xT, gate_up_ps, s)
                dve.wait_ge(normed, QT * b)
                nc.vector.tensor_copy(scales[:, 0:2, :], weight[:, :, bass.ds(QT * b, QT)])
                nc.vector.tensor_copy(scales[:, 2, :], gate[:, bass.ds(QT * b, QT)]).then_inc(scales_ready, 1)
                for i in range(QT):
                    if i > 0:
                        norm.await_stats(b, i)
                    dve.wait_ge(s["out_taken"], QT * b + i + 1)
                    dve.wait_ge(gathered[i], 32 * b + 32)
                    for k in range(2):
                        nc.vector.scalar_tensor_tensor(out=f[:, i, :], in0=yk[k][:, i, :], scalar=scales[:, k, i:i + 1],
                                                       in1=f[:, i, :], op0=ALU.mult, op1=ALU.add).then_inc(added, 1)
                        if k == 0 and i > 0:
                            norm.aggregate([i - 1])
                        dve.wait_ge(added, 2 * QT * b + 2 * i + k + 1)
                    norm.row_stats(f, i)
                norm.await_stats(b)
                nc.vector.memset(norm.half[:], 0.0)
                norm.aggregate([QT - 1])
                norm.halve(b)
                norm.shift_bits(b)
                norm.guess(b)

            turn(0, False, NC - 1)
            with dve.Fori(1, NB - 1) as b:
                turn(b, False)
            turn(NB - 1, True)

        @block.gpsimd
        def _(pool):
            def turn(b, turns_begun):
                nc.gpsimd.tensor_copy(index[:], slot[:, :, bass.ds(QT * b, QT)]).then_inc(index_ready, 1)
                pool.wait_ge(w_lo, NC)
                pool.wait_ge(index_ready, turns_begun)
                for i in range(QT):
                    for k in range(2):
                        pool.indirect_dma_start(out=yk[k][:, i, :], out_offset=None, in_=ys,
                                                in_offset=bass.IndirectOffsetOnAxis(ap=index[:, k, i:i + 1], axis=0)
                                                ).then_inc(gathered[i], 16)
                norm.refine(b)
                for i in range(QT):
                    pool.wait_ge(normed, QT * b + i + 1)
                    pool.wait_ge(x1_in, 16 * b + 16)
                    nc.gpsimd.tensor_tensor(f[:, i, :], f[:, i, :], yk[0][:, i, :], ALU.add).then_inc(finished, 1)

            with pool.Fori(1, NB + 1) as turns_begun:
                turn(turns_begun - 1, turns_begun)


def build_constants(nc, idf, idb, mask, norm_constants):
    with nc.semaphore("made") as made, nc.sbuf_tensor("mask_f", [P, P], F32) as mask_f, nc.Block() as block:
        @block.gpsimd
        def _(pool):
            nc.gpsimd.memset(idf[:], 0.0)
            nc.gpsimd.memset(norm_constants[:, 0, :], 0.0)
            nc.gpsimd.memset(norm_constants[:, 1, :], 1.5)
            nc.gpsimd.memset(mask_f[:], 0.0).then_inc(made, 1)
            pool.wait_ge(made, 1)
            nc.gpsimd.affine_select(out=idf[:], in_=idf[:], compare_op=ALU.not_equal, fill=1.0, base=0,
                                    pattern=[[-1, P]], channel_multiplier=1)
            nc.gpsimd.affine_select(out=mask_f[:], in_=mask_f[:], compare_op=ALU.is_ge, fill=MASKED, base=0,
                                    pattern=[[-1, P]], channel_multiplier=1).then_inc(made, 1)
            pool.wait_ge(made, 2)
            for k in range(2):
                nc.gpsimd.tensor_copy(idb[:, k, :], idf[:])
                last = nc.gpsimd.tensor_copy(mask[:, k, :], mask_f[:])
            last.then_inc(made, 1)
            pool.wait_ge(made, 3)


def build_layer(nc, x, wq, wvk, wo, wr, qb, vkb, ob, gu, dn, shg, shu, shd, out):
    def scratch(name, rows):
        return nc.dram_tensor(name, (rows, D), F32, kind="Internal").ap()

    def by_sequence(dram):
        return dram.rearrange("(b t p) d -> b p t d", t=QT, p=P)

    x1, xn, ys = scratch("x1", NB * S), scratch("xn", NB * S), scratch("ys", NT * TS)
    with ExitStack() as ctx:
        def sb(name, shape, dt=F32):
            return ctx.enter_context(nc.sbuf_tensor(name, shape, dt))

        idf, idb, mask = sb("idf", [P, P]), sb("idb", [P, 2, P], BF16), sb("mask", [P, 2, P], BF16)
        norm_constants = sb("norm_constants", [P, 2, QT])
        logits = sb("logits", [P, NTT, R])
        build_constants(nc, idf, idb, mask, norm_constants)
        build_attention(nc, by_sequence(x), wq, wvk, wo, wr, qb, vkb, ob, by_sequence(x1), by_sequence(xn),
                        logits, idf, idb, mask, norm_constants)
        gate = sb("gate", [P, NTT])
        weight = sb("weight", [P, 2, NTT])
        slot = sb("slot", [P, 2, NTT], I32)
        token_of_slot = sb("token_of_slot", [P, SC], I32)
        tile_expert = sb("tile_expert", [1, NT], I32)
        build_routing(nc, logits, gate, weight, slot, token_of_slot, tile_expert)
        build_experts(nc, xn, gu, dn, ys.rearrange("(n t p) d -> n p t d", t=QT, p=P), token_of_slot, tile_expert, idf)
        build_shared(nc, by_sequence(xn), shg, shu, shd, ys, by_sequence(x1), by_sequence(out), gate, weight, slot, idf,
                     norm_constants)


def kernel(**inputs):
    import numpy as np
    import concourse.bacc as bacc
    from concourse.bass_utils import run_bass_kernel_spmd

    a = {k.split("_", 2)[2]: np.asarray(v) for k, v in inputs.items()}

    def chunked(w):
        return np.ascontiguousarray(w.T.reshape(-1, P, w.shape[0]).transpose(1, 0, 2))

    arrays = {
        "x_in": a["hidden_states"].reshape(NB * S, D),
        "wq_in": chunked(a["q_w"]),
        "wvk_in": chunked(np.concatenate([a["v_w"], a["k_w"]])),
        "wo_in": chunked(a["o_w"]),
        "wr_in": chunked(np.concatenate([a["router_weight"], a["shared_gate_w"]])),
        "qb_in": np.ascontiguousarray(a["q_b"].reshape(C, P).T),
        "vkb_in": np.concatenate([a["v_b"], a["k_b"]]).reshape(2 * HD, 1),
        "ob_in": a["o_b"],
        "gu_in": np.stack([chunked(w) for w in a["gate_up_proj"]]),
        "dn_in": np.ascontiguousarray(a["down_proj"].transpose(0, 2, 1)),
        "shg_in": chunked(a["sh_gate_w"]),
        "shu_in": chunked(a["sh_up_w"]),
        "shd_in": chunked(a["sh_down_w"]),
    }
    nc = bacc.Bacc("TRN2", target_bir_lowering=False, num_devices=1)
    args = [nc.dram_tensor(k, v.shape, F32, kind="ExternalInput").ap() for k, v in arrays.items()]
    out = nc.dram_tensor("out", (NB * S, D), F32, kind="ExternalOutput").ap()
    build_layer(nc, *args, out)
    r = run_bass_kernel_spmd(nc, [arrays], core_ids=[0])
    return r.results[0]["out"].reshape(NB, S, D)
```

```python
import concourse.bass as bass
from concourse import mybir
from contextlib import ExitStack

F32 = mybir.dt.float32
F32R = mybir.dt.float32r
BF16 = mybir.dt.bfloat16
I32 = mybir.dt.int32
U32 = mybir.dt.uint32
ALU = mybir.AluOpType
ACT = mybir.ActivationFunctionType
AX_X = mybir.AxisListType.X

P = 128
S = 512
NB = 8
D = 512
C = D // P
QT = S // P
H = 16
HD = D // H
HG = P // HD
E = 8
R = E + 1
EPS = 1e-5
SCALE = float(HD) ** -0.5
MASKED = -3.0e38
I_MOE = 352
I_SH = 1408
TS = 512
NTT = NB * QT
NT = (2 * NB * S + E * (TS - 1)) // TS
SC = NT * TS // P
PASSES = ((0, 0), (0, 1), (1, 0))
MAGIC = float(0x5F3759DF - (1 << 22))
NEWTON = 3


class Steps:

    def __init__(self, engine, sem):
        self.engine, self.sem, self.n = engine, sem, 0

    def then_wait(self, instruction):
        instruction.then_inc(self.sem, 1)
        self.n += 1
        self.engine.wait_ge(self.sem, self.n)


class InverseStd:
    STEPS = 4 * NEWTON + 1

    def __init__(self, nc, sb, sem, name, constants):
        self.nc, self.constants = nc, constants
        self.stats = sb("stats" + name, [P, QT, 6])
        self.mean_var = sb("mean_var" + name, [P, QT, 2])
        self.half = sb("half" + name, [P, QT])
        self.bits = sb("bits" + name, [P, QT])
        self.t = sb("t" + name, [P, 3, QT])
        self.rstd = sb("rstd" + name, [P, QT])
        self.bias = sb("bias" + name, [P, QT])
        self.row_six = sem("row_six" + name)
        self.row_var = sem("row_var" + name)
        self.guessed = sem("guessed" + name)
        self.newton = sem("newton" + name)
        self.ready = sem("std_ready" + name)

    def row_stats(self, src, i):
        self.nc.vector.bn_stats(self.stats[:, i, :], src[:, i, :]).then_inc(self.row_six, 1)

    def await_stats(self, n, tiles=QT):
        self.nc.vector.wait_ge(self.row_six, QT * n + tiles)

    def aggregate(self, tiles=range(QT)):
        for i in tiles:
            last = self.nc.vector.bn_aggr(self.mean_var[:, i, :], self.stats[:, i, :])
        if tiles[-1] == QT - 1:
            last.then_inc(self.row_var, 1)

    def halve(self, n):
        self.nc.vector.wait_ge(self.row_var, 3 * n + 1)
        self.nc.vector.tensor_scalar(self.half[:], self.mean_var[:, :, 1], EPS, 0.5, ALU.add,
                                     ALU.mult).then_inc(self.row_var, 1)

    def shift_bits(self, n):
        self.nc.vector.wait_ge(self.row_var, 3 * n + 2)
        self.nc.vector.tensor_scalar(self.bits[:].bitcast(I32), self.half[:].bitcast(I32), 1, None,
                                     ALU.logical_shift_right).then_inc(self.row_var, 1)

    def guess(self, n):
        self.nc.vector.wait_ge(self.row_var, 3 * n + 3)
        self.nc.vector.tensor_scalar(self.t[:, 2, :].bitcast(I32), self.bits[:].bitcast(I32), -1.0, MAGIC,
                                     ALU.mult, ALU.add).then_inc(self.guessed, 1)

    def refine(self, n):
        zero, three_halves = self.constants[:, 0, :], self.constants[:, 1, :]
        a, b, y = self.t[:, 0, :], self.t[:, 1, :], self.t[:, 2, :]
        at = self.STEPS * n
        self.nc.gpsimd.wait_ge(self.guessed, n + 1)

        def step(out, in0, in1, op):
            nonlocal at
            at += 1
            self.nc.gpsimd.tensor_tensor(out, in0, in1, op).then_inc(self.newton, 1)
            self.nc.gpsimd.wait_ge(self.newton, at)

        for k in range(NEWTON):
            step(a, y, y, ALU.mult)
            step(b, a, self.half[:], ALU.mult)
            step(a, three_halves, b, ALU.subtract)
            y_next = self.rstd[:] if k == NEWTON - 1 else y
            step(y_next, y, a, ALU.mult)
        step(b, self.mean_var[:, :, 0], self.rstd[:], ALU.mult)
        self.nc.gpsimd.tensor_tensor(self.bias[:], zero, b, ALU.subtract).then_inc(self.ready, 1)


def build_attention(nc, x, wq, wvk, wo, wr, qb, vkb, ob, x1_out, xn_out, logits, idf, idb, mask, norm_constants):
    ctx = ExitStack()
    with ctx:
        def sb(name, shape, dt=F32):
            return ctx.enter_context(nc.sbuf_tensor("at_" + name, shape, dt))

        def sem(name):
            return ctx.enter_context(nc.semaphore("at_" + name))

        wq_s = [sb(f"wq{j}", [P, C, D], F32R) for j in range(2)]
        wvk_s = [sb(f"wvk{j}", [P, C, 2 * HD], F32R) for j in range(2)]
        wo_s = [sb(f"wo{j}", [P, C, D], F32R) for j in range(2)]
        wr_s = [sb(f"wr{j}", [P, C, R], F32R) for j in range(2)]
        qb_s = sb("qb", [P, C])
        vkb_s = sb("vkb", [2 * HD, 1])
        vks_s = sb("vks", [2 * HD, 1])
        vkbs_s = sb("vkbs", [2 * HD, 1])
        ob_s = sb("ob", [P, D])
        x_in = sb("x_in", [P, QT, D])
        x_res = sb("x_res", [P, QT, D])
        y = sb("y", [P, QT, D])
        xn2 = sb("xn2", [P, QT, D])
        xT = [sb(f"xT{j}", [P, C, S], F32R) for j in range(2)]
        vk = sb("vk", [2 * HD, S])
        vk_h = [sb(f"vk_h{j}", [2 * HD, S], F32R) for j in range(2)]
        q_h = [[sb(f"q_h{j}{r}", [P, S], F32R) for j in range(2)] for r in range(2)]
        Qs = sb("Qs", [3 * HD, H, S], F32R)
        Ks = sb("Ks", [3 * HD, S], F32R)
        V = sb("V", [P, QT, HD])
        ones_f = sb("ones_f", [P, QT, HD])
        mask_f = sb("mask_f", [P, P])
        PW = QT * (QT + 1) // 2 * P
        minus_max = [sb(f"minus_max{r}", [P, QT, P], F32R) for r in range(3)]
        PT = [sb(f"PT{r}", [P, HG, PW]) for r in range(2)]
        OT = [sb(f"OT{j}", [P, C, S], F32R) for j in range(2)]
        nmax = sb("nmax", [P, 3, QT])
        over_sum, mixed_f = sb("over_sum", [P, S]), sb("mixed_f", [P, S])
        ones = sb("ones", [P, P], F32R)
        norm = [InverseStd(nc, sb, sem, f"_{of}", norm_constants) for of in ("x", "projection", "x1")]
        lgT = over_sum[0:R, :]

        bank = [ctx.enter_context(nc.psum_tensor(f"at_bank{i}", [P, 512], F32)) for i in range(8)]
        S_ps, T_ps = bank[0:3], bank[4:7]
        sum_ps, A_ps = bank[3], bank[7]
        X_ps = bank[0:4]
        O_ps = [bank[4], bank[5], bank[6], bank[7]]

        xn2_moved = sem("xn2_moved")
        w_in, w_hi, w_split = [sem("w_in0"), sem("w_in1"), xn2_moved, sem("w_in3")], sem("w_hi"), sem("w_split")
        WEIGHTS = [(x_res[:, :, 0:2 * HD], wvk_s, wvk), (y[:], wq_s, wq), (xn2[:], wo_s, wo),
                   (x_res[:, :, 2 * HD:2 * HD + R], wr_s, wr)]
        b_in = sem("b_in")
        x_in_s, x_res_s = sem("x_in_s"), sem("x_res_s")
        q_moved = [sem(f"q_moved{c}") for c in range(C)]
        q_spilled = [sem(f"q_spilled{c}") for c in range(C)]
        k_moved = sem("k_moved")
        q_dram = nc.dram_tensor("q_dram", (2, C, P, S), F32, kind="Internal").ap()
        x1_stored = sem("x1_stored")
        scores, shifted, summed, mixed, projected = (sem("scores"), sem("shifted"), sem("summed"), sem("mixed"),
                                                     sem("projected"))
        xT1_ps, qkv_ps, v_ps, xT2_ps = sem("xT1_ps"), sem("qkv_ps"), sem("v_ps"), sem("xT2_ps")
        rt_ps, lg_ps = sem("rt_ps"), sem("lg_ps")
        vk_high, inverted, mixed_taken = sem("vk_high"), sem("inverted"), sem("mixed_taken")
        max_ready, xT1_lo, xT2_lo, OT_lo = sem("max_ready"), sem("xT1_lo"), sem("xT2_lo"), sem("OT_lo")
        qkv_lo, v_ready, y_ready, lg_ready = sem("qkv_lo"), sem("v_ready"), sem("y_ready"), sem("lg_ready")
        pt_ready, xT1_hi, xT2_hi, OT_hi = sem("pt_ready"), sem("xT1_hi"), sem("xT2_hi"), sem("OT_hi")
        qkv_hi, x_normed, y_normed, xn_ready, lgT_ready = (sem("qkv_hi"), sem("x_normed"), sem("y_normed"),
                                                           sem("xn_ready"), sem("lgT_ready"))
        x1_ready, diagonal_ready, made = sem("x1_ready"), sem("diagonal_ready"), sem("made")

        S_UNITS = [((2, 0), (0, (QT - 1) * P)), ((3, 0),), ((1, 0),)]
        T_UNITS = [((0, 0),), ((3, 0), (1, P)), ((2, 0),)]
        TOFF = [0, (QT + 1) * P, 2 * QT * P, QT * P]
        TFROM = [0, QT * P, 2 * QT * P]
        TW = [QT * P, QT * P, 2 * P]
        UNIT_PS = [S_ps[0], S_ps[1], S_ps[2], S_ps[0], S_ps[1]]
        AV_STEP = [HG * g + HG + 1 for g in range(C - 1)]

        block = ctx.enter_context(nc.Block())

        def turns(engine, turn):
            turn(0, True, False)
            with engine.Fori(1, NB - 1) as b:
                turn(b, False, False)
            turn(NB - 1, False, True)

        def seq(dram, b):
            return dram[bass.ds(b, 1)].rearrange("o p t d -> p (o t) d")

        @block.sync
        def _(sp):
            sp.dma_start(x_in[:], seq(x, 0)).then_inc(x_in_s, 16)
            for part, (staged, _, dram) in enumerate(WEIGHTS[0:2]):
                sp.dma_start(staged, dram).then_inc(w_in[part], 16)
            sp.dma_start(qb_s[:], qb).then_inc(b_in, 16)
            sp.dma_start(vkb_s[:], vkb).then_inc(b_in, 16)
            sp.dma_start(ob_s[:], ob.partition_broadcast(P)).then_inc(b_in, 16)
            for part, (staged, _, dram) in enumerate(WEIGHTS[2:4]):
                sp.dma_start(staged, dram).then_inc(w_in[2 + part], 16)

            def store_x1(n):
                sp.wait_ge(x1_ready, QT * n + QT)
                sp.dma_start(seq(x1_out, n), y[:]).then_inc(x1_stored, 16)

            def store_xn(n):
                sp.wait_ge(xn_ready, QT * n + QT)
                sp.dma_start(seq(xn_out, n), xn2[:]).then_inc(xn2_moved, 16)

            def move_qkv(n):
                sp.wait_ge(qkv_lo, 5 * n + 1)
                for at, half in ((0, 0), (1, 0), (2, 1)):
                    sp.dma_start(Ks[HD * at:HD * at + HD, :].bitcast(F32),
                                 vk_h[half][HD:2 * HD, :].bitcast(F32)).then_inc(k_moved, 16)
                for c in range(C + 1):
                    if c < C:
                        sp.wait_ge(qkv_lo, 5 * n + 2 + c)
                        for half in range(2):
                            sp.dma_start(q_dram[half, c], q_h[c % 2][half][:].bitcast(F32)).then_inc(q_spilled[c], 16)
                    if c > 0:
                        sp.wait_ge(q_spilled[c - 1], 32 * n + 32)
                        for at, half in ((0, 0), (1, 1), (2, 0)):
                            sp.dma_start(Qs[HD * at:HD * at + HD, HG * (c - 1):HG * c, :].bitcast(F32),
                                         q_dram[half, c - 1].rearrange("(g d) t -> d g t", g=HG)
                                         ).then_inc(q_moved[c - 1], 16)

            move_qkv(0)
            sp.wait_ge(w_split, 6)
            sp.dma_start(x_res[:], seq(x, 0)).then_inc(x_res_s, 16)

            def turn(b, first, last):
                if not last:
                    sp.wait_ge(xT1_ps, C * b + C)
                    sp.dma_start(x_in[:], seq(x, b + 1)).then_inc(x_in_s, 16)
                if not first:
                    sp.wait_ge(x1_ready, QT * b)
                    sp.dma_start(x_res[:], seq(x, b)).then_inc(x_res_s, 16)
                    store_x1(b - 1)
                if not last:
                    sp.wait_ge(shifted, 3 * H * b + 3 * H)
                    move_qkv(b + 1)
                if not first:
                    store_xn(b - 1)

            turns(sp, turn)
            store_x1(NB - 1)
            store_xn(NB - 1)
            sp.wait_ge(x1_stored, 16 * NB)
            sp.wait_ge(xn2_moved, 16 * NB + 16)

        @block.tensor
        def _(pe):
            def split_product(out, w, x_, cols, xcols):
                n = 0
                for c in range(C):
                    for i, j in PASSES:
                        last = nc.tensor.matmul(out, w[i][:, c, cols], x_[j][:, c, xcols],
                                                start=(n == 0), stop=(n == 3 * C - 1))
                        n += 1
                return last

            def transpose_x(src, c, out, done):
                for t in range(QT):
                    last = nc.tensor.transpose(out[:, t * P:(t + 1) * P], src[:, t, c * P:(c + 1) * P], idf[:])
                last.then_inc(done, 1)

            def project_qkv(n, u, start=False):
                if u == 0:
                    pe.wait_ge(xT1_lo, C * n + C)
                if start and u < 2:
                    pe.wait_ge(w_split, 3 + u)
                if u >= 3:
                    pe.wait_ge(qkv_lo, 5 * n + u - 2)
                if u == 0:
                    last = split_product(S_ps[0][0:2 * HD, :], wvk_s, xT, slice(0, 2 * HD), slice(0, S))
                else:
                    last = split_product(UNIT_PS[u][:], wq_s, xT, slice((u - 1) * P, u * P), slice(0, S))
                last.then_inc(qkv_ps, 1)

            def transpose_v(n):
                pe.wait_ge(pt_ready, 3 * H * n)
                pe.wait_ge(qkv_lo, 5 * n + 1)
                for j in range(QT):
                    last = nc.tensor.matmul(T_ps[0][:, j * HD:(j + 1) * HD], vk[0:HD, j * P:(j + 1) * P],
                                            idf[0:HD, 0:HD], start=True, stop=True)
                last.then_inc(v_ps, 1)

            pe.wait_ge(made, 3)
            pe.wait_ge(x_normed, QT)
            for c in range(C):
                transpose_x(x_in, c, X_ps[c], xT1_ps)
            for u in range(5):
                project_qkv(0, u, True)
            transpose_v(0)

            def transpose_xn(n):
                pe.wait_ge(xn_ready, QT * n + QT)
                for c in range(C):
                    transpose_x(xn2, c, X_ps[c], xT2_ps)

            def route(n):
                pe.wait_ge(xT2_lo, C * n + C)
                split_product(sum_ps[0:R, :], wr_s, xT, slice(0, R), slice(0, S)).then_inc(rt_ps, 1)

            def transpose_logits(n):
                pe.wait_ge(lgT_ready, n + 1)
                for t in range(QT):
                    last = nc.tensor.matmul(sum_ps[:, t * R:(t + 1) * R], lgT[:, t * P:(t + 1) * P],
                                            idf[0:R, 0:R], start=True, stop=True)
                last.then_inc(lg_ps, 1)

            def over_keys(weights, out, g):
                for j in range(QT):
                    for k in range(HG):
                        last = nc.tensor.matmul(out[HD * k:HD * k + HD, j * P:S], weights[:, j, :],
                                                PT[g % 2][:, k, TOFF[j]:TOFF[j] + (QT - j) * P],
                                                start=(j == 0), stop=(j == QT - 1), tile_position=(0, HD * k))
                return last

            def query_scores(n, s):
                if s == 0:
                    pe.wait_ge(qkv_lo, 5 * n + 5)
                    pe.wait_ge(k_moved, 48 * n + 48)
                if s % HG == 0:
                    pe.wait_ge(q_moved[s // HG], 48 * n + 48)
                for units in ((0,), (1, 2)):
                    for u in units:
                        if s > 0:
                            pe.wait_ge(max_ready, 3 * H * n + 3 * (s - 1) + u + 1)
                        for i, col in S_UNITS[u]:
                            nc.tensor.matmul(S_ps[u][:, col:col + (i + 1) * P], Qs[:, s, i * P:(i + 1) * P],
                                             Ks[:, 0:(i + 1) * P], start=((i, col) == S_UNITS[u][0]), stop=False)
                    for u in units:
                        (i, col), k = S_UNITS[u][0], len(S_UNITS[u])
                        nc.tensor.matmul(S_ps[u][:, col + i * P:col + (i + k) * P], idb[:, 0, :],
                                         mask[:, 0:k, :].rearrange("p t k -> p (t k)"),
                                         start=False, stop=True).then_inc(scores, 1)

            pe.wait_ge(w_split, 6)
            query_scores(0, 0)

            def turn(b, first, last):
                for s in range(1, H + 2):
                    if s < H:
                        query_scores(b, s)
                    if s == H and not last:
                        pe.wait_ge(x_normed, QT * b + 2 * QT)
                        pe.wait_ge(max_ready, 3 * H * b + 3 * H)
                        for c in range(C):
                            if c == C - 1:
                                pe.wait_ge(inverted, QT * (C * b + C - 1))
                            transpose_x(x_in, c, X_ps[c], xT1_ps)
                    if s in AV_STEP:
                        g = AV_STEP.index(s)
                        pe.wait_ge(pt_ready, 3 * H * b + 3 * HG * (g + 1))
                        if g > 0:
                            pe.wait_ge(inverted, QT * (C * b + g))
                        elif not first:
                            pe.wait_ge(lg_ready, b)
                        over_keys(ones_f, sum_ps, g).then_inc(summed, 1)
                    if s - 1 in AV_STEP:
                        g = AV_STEP.index(s - 1)
                        if g > 0:
                            pe.wait_ge(mixed_taken, C * b + g)
                        over_keys(V, A_ps, g).then_inc(mixed, 1)
                    if s <= H:
                        h = s - 1
                        if h == 0:
                            pe.wait_ge(v_ready, b + 1)
                        pe.wait_ge(diagonal_ready, H * b + h + 1)
                        for tb, tiles in enumerate(T_UNITS):
                            if h > 0:
                                pe.wait_ge(pt_ready, 3 * H * b + 3 * (h - 1) + tb + 1)
                            elif not first:
                                pe.wait_ge(y_ready, QT * b)
                            for j, col in reversed(tiles):
                                n = (QT - j) * P
                                nc.tensor.matmul(T_ps[tb][:, col:col + n], Ks[:, j * P:(j + 1) * P], Qs[:, h, j * P:S],
                                                 start=((j, col) == tiles[-1]), stop=False)
                            nc.tensor.matmul(T_ps[tb][:, 0:len(tiles) * P], mask[:, 0, :],
                                             idb[:, 0:len(tiles), :].rearrange("p t k -> p (t k)"), start=False, stop=False)
                            for j, col in tiles:
                                n = (QT - j) * P
                                lastt = nc.tensor.matmul(T_ps[tb][:, col:col + n], ones[:],
                                                         minus_max[h % 3][:, j:QT, :].rearrange("p i k -> p (i k)"),
                                                         start=False, stop=((j, col) == tiles[-1]))
                            lastt.then_inc(shifted, 1)
                    if s == H and not last:
                        project_qkv(b + 1, 0)
                        project_qkv(b + 1, 1)
                    if s == H + 1 and not last:
                        for u in (2, 3, 4):
                            project_qkv(b + 1, u)
                pe.wait_ge(pt_ready, 3 * H * b + 3 * H)
                pe.wait_ge(inverted, QT * (C * b + C - 1))
                over_keys(ones_f, sum_ps, C - 1).then_inc(summed, 1)
                pe.wait_ge(mixed_taken, C * b + C - 1)
                over_keys(V, A_ps, C - 1).then_inc(mixed, 1)
                if not last:
                    transpose_v(b + 1)
                if not first:
                    if not last:
                        pe.wait_ge(qkv_lo, 5 * b + 10)
                    pe.wait_ge(inverted, QT * (C * b + C))
                    transpose_xn(b - 1)
                for c in range(C):
                    if c == C - 2:
                        if not first:
                            route(b - 1)
                        if not last:
                            query_scores(b + 1, 0)
                    pe.wait_ge(OT_lo, C * b + c + 1)
                    if c == 0 and not last:
                        pe.wait_ge(v_ready, b + 2)
                    for i in range(QT):
                        if c == 0 and i == QT - 1:
                            pe.wait_ge(mixed_taken, C * b + C)
                        for n, (j, k) in enumerate(PASSES):
                            lastt = nc.tensor.matmul(O_ps[i][:], OT[j][:, c, i * P:(i + 1) * P], wo_s[k][:, c, :],
                                                     start=(c == 0 and n == 0), stop=(c == C - 1 and n == 2))
                        if c == C - 1:
                            lastt.then_inc(projected, 1)
                if not first:
                    transpose_logits(b - 1)

            turns(pe, turn)
            pe.wait_ge(lg_ready, NB)
            transpose_xn(NB - 1)
            route(NB - 1)
            transpose_logits(NB - 1)

        @block.vector
        def _(dve):
            def whole_norm(k, n, src, ready):
                for i in range(QT):
                    dve.wait_ge(ready, QT * n + i + 1)
                    norm[k].row_stats(src, i)
                norm[k].await_stats(n)
                norm[k].aggregate()
                norm[k].halve(n)
                norm[k].shift_bits(n)
                norm[k].guess(n)

            def low_x(n, c, ps, hi_sem, lo_sem):
                dve.wait_ge(hi_sem, C * n + c + 1)
                nc.vector.tensor_tensor(xT[1][:, c, :], ps[:], xT[0][:, c, :].bitcast(F32),
                                        ALU.subtract).then_inc(lo_sem, 1)

            def low_qkv(n, u):
                dve.wait_ge(qkv_hi, 5 * n + u + 1)
                if u == 0:
                    nc.vector.tensor_copy(vk_h[0][:], vk[:]).then_inc(vk_high, 1)
                    dve.wait_ge(vk_high, n + 1)
                    nc.vector.tensor_tensor(vk_h[1][:], vk[:], vk_h[0][:].bitcast(F32),
                                            ALU.subtract).then_inc(qkv_lo, 1)
                else:
                    r = (u - 1) % 2
                    nc.vector.scalar_tensor_tensor(out=q_h[r][1][:], in0=UNIT_PS[u][:], scalar=qb_s[:, u - 1:u],
                                                   in1=q_h[r][0][:].bitcast(F32), op0=ALU.add,
                                                   op1=ALU.subtract).then_inc(qkv_lo, 1)

            def take_v(n):
                dve.wait_ge(v_ps, n + 1)
                nc.vector.tensor_copy(V[:], T_ps[0][:, 0:QT * HD].rearrange("p (t d) -> p t d", t=QT)).then_inc(v_ready, 1)

            dve.wait_ge(x_in_s, 16)
            for i in range(QT):
                norm[0].row_stats(x_in, i)
            norm[0].await_stats(0)
            norm[0].aggregate()
            norm[0].halve(0)
            norm[0].shift_bits(0)
            norm[0].guess(0)
            dve.wait_ge(b_in, 48)
            nc.vector.memset(vks_s[HD:2 * HD, :], SCALE).then_inc(lg_ready, 1)
            nc.vector.memset(vks_s[0:HD, :], 1.0).then_inc(w_split, 1)
            dve.wait_ge(w_split, 1)
            nc.vector.tensor_tensor(vkbs_s[:], vkb_s[:], vks_s[:], ALU.mult).then_inc(w_split, 1)

            def low_weights(part):
                staged, halves, _ = WEIGHTS[part]
                dve.wait_ge(w_hi, part + 1)
                nc.vector.tensor_tensor(halves[1][:], staged, halves[0][:].bitcast(F32), ALU.subtract).then_inc(w_split, 1)

            low_weights(0)
            low_weights(1)
            for c in range(C):
                low_x(0, c, X_ps[c], xT1_hi, xT1_lo)
            low_weights(2)
            low_weights(3)
            for u in range(5):
                low_qkv(0, u)
            take_v(0)

            def take_projection(n, first):
                if not first:
                    dve.wait_ge(x1_stored, 16 * n)
                    dve.wait_ge(xn_ready, QT * n)
                for i in range(QT):
                    dve.wait_ge(projected, QT * n + i + 1)
                    last = nc.vector.tensor_tensor(y[:, i, :], O_ps[i][:], ob_s[:], ALU.add)
                    last.then_inc(y_ready, 1)

            def take_logits(n):
                dve.wait_ge(lg_ps, n + 1)
                nc.vector.tensor_copy(logits[:, bass.ds(QT * n, QT), :],
                                      sum_ps[:, 0:QT * R].rearrange("p (t r) -> p t r", t=QT)).then_inc(lg_ready, 1)

            def invert_sums(n, g, i):
                dve.wait_ge(summed, C * n + g + 1)
                nc.vector.reciprocal(over_sum[:, i * P:(i + 1) * P], sum_ps[:, i * P:(i + 1) * P]).then_inc(inverted, 1)

            def maxima(n, s, u, start):
                if u == 0:
                    if s >= 3:
                        dve.wait_ge(diagonal_ready, H * n + s - 2)
                    elif not start:
                        dve.wait_ge(diagonal_ready, H * n)
                dve.wait_ge(scores, 3 * H * n + 3 * s + u + 1)
                for i, col in S_UNITS[u]:
                    last = nc.vector.tensor_reduce(nmax[:, s % 3, i:i + 1], S_ps[u][:, col:col + (i + 1) * P],
                                                   AX_X, ALU.max, negate=True)
                last.then_inc(max_ready, 1)

            def scale_mixed(n, g):
                dve.wait_ge(mixed, C * n + g + 1)
                dve.wait_ge(inverted, QT * (C * n + g + 1))
                nc.vector.tensor_tensor(mixed_f[:], A_ps[:], over_sum[:], ALU.mult).then_inc(mixed_taken, 1)

            def low_mixed(n, g):
                dve.wait_ge(OT_hi, C * n + g + 1)
                nc.vector.tensor_tensor(OT[1][:, g, :], mixed_f[:], OT[0][:, g, :].bitcast(F32),
                                        ALU.subtract).then_inc(OT_lo, 1)

            def turn(b, first, last):
                norms = []
                if not first:
                    norms += [(1, b - 1, y, y_ready, 0), (2, b - 1, y, x1_ready, 10)]
                if not last:
                    norms.append((0, b + 1, x_in, x_in_s, 4))
                for s in range(H):
                    ending = [(k, n) for k, n, _, _, at in norms if s == at + QT]
                    for u in range(3) if s > 0 else ():
                        if u == 0:
                            for k, n in ending:
                                norm[k].await_stats(n)
                        maxima(b, s, u, first)
                        for k, n in ending:
                            if u == 0:
                                norm[k].aggregate()
                            elif u == 1:
                                norm[k].halve(n)
                            else:
                                norm[k].shift_bits(n)
                        if s - 1 in AV_STEP:
                            invert_sums(b, AV_STEP.index(s - 1), u)
                    for k, n, src, ready, at in norms:
                        if at <= s < at + QT:
                            i = s - at
                            dve.wait_ge(ready, 16 * n + 16 if k == 0 else QT * n + i + 1)
                            norm[k].row_stats(src, i)
                    for k, n in ending:
                        norm[k].guess(n)
                    if s - 1 in AV_STEP:
                        invert_sums(b, AV_STEP.index(s - 1), QT - 1)
                    if s - 2 in AV_STEP:
                        scale_mixed(b, AV_STEP.index(s - 2))
                    if s - 3 in AV_STEP:
                        low_mixed(b, AV_STEP.index(s - 3))
                if not last:
                    for c in range(C):
                        low_x(b + 1, c, X_ps[c], xT1_hi, xT1_lo)
                low_mixed(b, C - 2)
                if not last:
                    for u in range(5):
                        low_qkv(b + 1, u)
                for i in range(QT):
                    invert_sums(b, C - 1, i)
                scale_mixed(b, C - 1)
                if not last:
                    take_v(b + 1)
                low_mixed(b, C - 1)
                if not first:
                    for c in range(C):
                        low_x(b - 1, c, X_ps[c], xT2_hi, xT2_lo)
                if not last:
                    for u in range(3):
                        maxima(b + 1, 0, u, False)
                take_projection(b, first)
                if not first:
                    take_logits(b - 1)

            for u in range(3):
                maxima(0, 0, u, True)
            turns(dve, turn)
            whole_norm(1, NB - 1, y, y_ready)
            whole_norm(2, NB - 1, y, x1_ready)
            for c in range(C):
                low_x(NB - 1, c, X_ps[c], xT2_hi, xT2_lo)
            take_logits(NB - 1)

        @block.scalar
        def _(act):
            def normalize(dst, src, k, n, i, done):
                act.wait_ge(norm[k].ready, n + 1)
                nc.scalar.activation(dst[:, i, :], src[:, i, :], ACT.Identity, bias=norm[k].bias[:, i:i + 1],
                                     scale=norm[k].rstd[:, i:i + 1]).then_inc(done, 1)

            def high_x(n, c, ps, ps_sem, hi_sem):
                act.wait_ge(ps_sem, C * n + c + 1)
                nc.scalar.activation(xT[0][:, c, :], ps[:], ACT.Copy).then_inc(hi_sem, 1)

            def high_qkv(n, u, start=False):
                act.wait_ge(qkv_ps, 5 * n + u + 1)
                if u == 0:
                    if start:
                        act.wait_ge(w_split, 2)
                    else:
                        act.wait_ge(k_moved, 48 * n)
                    nc.scalar.activation(vk[:], S_ps[0][0:2 * HD, :], ACT.Identity, bias=vkbs_s[:],
                                         scale=vks_s[:]).then_inc(qkv_hi, 1)
                else:
                    if u > 2:
                        act.wait_ge(q_spilled[u - 3], 32 * n + 32)
                    elif not start:
                        act.wait_ge(q_spilled[u + 1], 32 * n)
                    nc.scalar.activation(q_h[(u - 1) % 2][0][:], UNIT_PS[u][:], ACT.Identity,
                                         bias=qb_s[:, u - 1:u]).then_inc(qkv_hi, 1)

            def high_weights(part):
                staged, halves, _ = WEIGHTS[part]
                act.wait_ge(w_in[part], 16)
                nc.scalar.activation(halves[0][:], staged, ACT.Copy).then_inc(w_hi, 1)

            high_weights(0)
            high_weights(1)
            for i in range(QT):
                normalize(x_in, x_in, 0, 0, i, x_normed)
            for c in range(C):
                high_x(0, c, X_ps[c], xT1_ps, xT1_hi)
            high_weights(2)
            high_weights(3)
            for u in range(5):
                high_qkv(0, u, True)

            def high_mixed(n, g, start=False):
                act.wait_ge(mixed_taken, C * n + g + 1)
                if g == 0 and not start:
                    act.wait_ge(projected, QT * n)
                nc.scalar.activation(OT[0][:, g, :], mixed_f[:], ACT.Copy).then_inc(OT_hi, 1)

            def take_lgT(n):
                act.wait_ge(rt_ps, n + 1)
                nc.scalar.activation(lgT, sum_ps[0:R, :], ACT.Copy).then_inc(lgT_ready, 1)

            def turn(b, first, last):
                def exp(h, tb):
                    act.wait_ge(shifted, 3 * H * b + 3 * h + tb + 1)
                    g = h // HG
                    if h % HG == 0 and tb == 0:
                        if g >= 2:
                            act.wait_ge(mixed, C * b + g - 1)
                        elif not first:
                            act.wait_ge(mixed, C * b)
                    nc.scalar.activation(PT[g % 2][:, h % HG, TFROM[tb]:TFROM[tb] + TW[tb]],
                                         T_ps[tb][:, 0:TW[tb]], ACT.Exp).then_inc(pt_ready, 1)

                for s in range(1, H + 1):
                    if s - 3 in AV_STEP[:C - 2]:
                        high_mixed(b, AV_STEP.index(s - 3), first)
                    if s == H and not last:
                        for c in range(C):
                            high_x(b + 1, c, X_ps[c], xT1_ps, xT1_hi)
                    if s == H:
                        high_mixed(b, C - 2)
                    for tb in range(3):
                        exp(s - 1, tb)
                    for i in (0, 1) if s % 2 == 0 else (2, 3):
                        if s in (8, 9) and not first:
                            normalize(y, y, 1, b - 1, i, y_normed)
                        if s in (12, 13) and not last:
                            normalize(x_in, x_in, 0, b + 1, i, x_normed)
                    if s == H and not last:
                        high_qkv(b + 1, 0)
                        high_qkv(b + 1, 1)
                if not last:
                    for u in (2, 3, 4):
                        high_qkv(b + 1, u)
                if not first:
                    act.wait_ge(xn2_moved, 16 * b)
                    for i in range(QT):
                        normalize(xn2, y, 2, b - 1, i, xn_ready)
                high_mixed(b, C - 1)
                if not first:
                    for c in range(C):
                        high_x(b - 1, c, X_ps[c], xT2_ps, xT2_hi)
                    take_lgT(b - 1)

            turns(act, turn)
            for i in range(QT):
                normalize(y, y, 1, NB - 1, i, y_normed)
            act.wait_ge(xn2_moved, 16 * NB)
            for i in range(QT):
                normalize(xn2, y, 2, NB - 1, i, xn_ready)
            for c in range(C):
                high_x(NB - 1, c, X_ps[c], xT2_ps, xT2_hi)
            take_lgT(NB - 1)

        @block.gpsimd
        def _(pool):
            def add_residual(n, i):
                pool.wait_ge(x_res_s, 16 * n + 16)
                pool.wait_ge(y_normed, QT * n + i + 1)
                nc.gpsimd.tensor_tensor(y[:, i, :], y[:, i, :], x_res[:, i, :], ALU.add).then_inc(x1_ready, 1)


            def turn(b, first, last):
                for h in range(H):
                    pool.wait_ge(max_ready, 3 * H * b + 3 * h + 3)
                    if h >= 3:
                        pool.wait_ge(shifted, 3 * H * b + 3 * (h - 2))
                    elif not first:
                        pool.wait_ge(shifted, 3 * H * b)
                    nc.gpsimd.tensor_tensor(minus_max[h % 3][:], idf[:].unsqueeze(1).to_broadcast([P, QT, P]),
                                            nmax[:, h % 3, :].unsqueeze(2).to_broadcast([P, QT, P]),
                                            ALU.mult).then_inc(diagonal_ready, 1)
                    if h == 5 and not first:
                        norm[1].refine(b - 1)
                    if h == 8 and not last:
                        norm[0].refine(b + 1)
                    if 8 <= h < 8 + QT and not first:
                        add_residual(b - 1, h - 8)
                if not first:
                    norm[2].refine(b - 1)

            nc.gpsimd.memset(norm_constants[:, 0, :], 0.0)
            nc.gpsimd.memset(norm_constants[:, 1, :], 1.5)
            nc.gpsimd.memset(idf[:], 0.0)
            nc.gpsimd.memset(ones_f[:], 1.0)
            nc.gpsimd.memset(mask_f[:], 0.0).then_inc(made, 1)
            pool.wait_ge(made, 1)
            nc.gpsimd.affine_select(out=idf[:], in_=idf[:], compare_op=ALU.not_equal, fill=1.0, base=0,
                                    pattern=[[-1, P]], channel_multiplier=1)
            nc.gpsimd.affine_select(out=mask_f[:], in_=mask_f[:], compare_op=ALU.is_ge, fill=MASKED, base=0,
                                    pattern=[[-1, P]], channel_multiplier=1).then_inc(made, 1)
            pool.wait_ge(made, 2)
            for k in range(2):
                nc.gpsimd.tensor_copy(idb[:, k, :], idf[:])
                nc.gpsimd.tensor_copy(mask[:, k, :], mask_f[:])
            nc.gpsimd.tensor_copy(ones[:], ones_f[:].rearrange("p t d -> p (t d)")).then_inc(made, 1)

            norm[0].refine(0)
            turns(pool, turn)
            norm[1].refine(NB - 1)
            for i in range(QT):
                add_residual(NB - 1, i)
            norm[2].refine(NB - 1)


def build_routing(nc, logits, gate, weight, slot, token_of_slot, tile_expert, weights):
    ctx = ExitStack()
    with ctx:
        def sb(name, shape, dt=F32):
            return ctx.enter_context(nc.sbuf_tensor("ro_" + name, shape, dt))

        def sem(name):
            return ctx.enter_context(nc.semaphore("ro_" + name))

        first_place = sb("first_place", [P, E])
        slots_before = sb("slots_before", [P, E])
        tile_no = sb("tile_no", [P, NT])
        lane_no = sb("lane_no", [P, P])
        column_no = sb("column_no", [P, SC])
        token_no = sb("token_no", [P, NTT])
        before = sb("before", [P, P], BF16)
        ones = sb("ones", [P, P], BF16)
        top = sb("top", [P, 4, NTT])
        inv = sb("inv", [P, NTT])
        prob = sb("prob", [P, NTT, E])
        t1 = sb("t1", [P, NTT, E])
        t2 = sb("t2", [P, NTT, E])
        pick = [sb(f"pick{k}", [P, NTT, E]) for k in range(2)]
        picked = sb("picked", [P, NTT, E], BF16)
        count = [sb(f"count{k}", [P, NTT, E]) for k in range(2)]
        total = sb("total", [P, NTT, E])
        tiles = [sb(f"tiles{k}", [P, E]) for k in range(2)]
        over = sb("over", [P, NT, E])
        base = sb("base", [P, E])
        tile_e = sb("tile_e", [P, NT])
        place = sb("place", [P, 2, NTT])
        digit = sb("digit", [P, 2, 2, NTT], I32)
        digit_f = sb("digit_f", [P, 2, 2, NTT])
        lane_hot = [sb(f"lane_hot{k}", [P, P], F32R) for k in range(4)]
        column_hot = sb("column_hot", [P, 2, NTT, SC], F32R)
        rank_ps = ctx.enter_context(nc.psum_tensor("ro_rank_ps", [P, NTT * E], F32))
        total_ps = ctx.enter_context(nc.psum_tensor("ro_total_ps", [P, NTT * E], F32))
        inverse_ps = ctx.enter_context(nc.psum_tensor("ro_inverse_ps", [P, 512], F32))

        constants, shifted, exponentials = sem("constants"), sem("shifted"), sem("exponentials")
        picks_ready, counted, hot, used, inverse_done = (
            sem("picks_ready"), sem("counted"), sem("hot"), sem("used"), sem("inverse_done"))
        own, expert_ready = sem("own"), sem("expert_ready")
        PART = NTT // 4
        block = ctx.enter_context(nc.Block())

        def over_experts(ap):
            return ap.unsqueeze(2).to_broadcast([P, NTT, E])

        def over_tiles(ap):
            return ap.unsqueeze(1).to_broadcast([P, NTT, E])

        @block.gpsimd
        def _(pool):
            nc.gpsimd.iota(first_place[:], [[-1, E]], base=E, channel_multiplier=0, allow_small_or_imprecise_dtypes=True)
            nc.gpsimd.iota(slots_before[:], [[TS, E]], base=0, channel_multiplier=0, allow_small_or_imprecise_dtypes=True)
            nc.gpsimd.iota(tile_no[:], [[1, NT]], base=0, channel_multiplier=0, allow_small_or_imprecise_dtypes=True)
            nc.gpsimd.iota(lane_no[:], [[1, P]], base=0, channel_multiplier=0, allow_small_or_imprecise_dtypes=True)
            nc.gpsimd.iota(column_no[:], [[1, SC]], base=0, channel_multiplier=0, allow_small_or_imprecise_dtypes=True)
            nc.gpsimd.iota(token_no[:], [[P, NTT]], base=0, channel_multiplier=1, allow_small_or_imprecise_dtypes=True)
            nc.gpsimd.memset(ones[:], 1.0).then_inc(constants, 1)
            pool.wait_ge(constants, 1)
            nc.gpsimd.affine_select(out=before[:], in_=ones[:], compare_op=ALU.is_gt, fill=0.0, base=0,
                                    pattern=[[1, P]], channel_multiplier=-1).then_inc(constants, 1)

        @block.scalar
        def _(act):
            act.wait_ge(shifted, 1)
            nc.scalar.activation(prob[:], t1[:], ACT.Exp)
            nc.scalar.activation(gate[:], logits[:, :, E], ACT.Exp, scale=-1.0).then_inc(exponentials, 1)
            for q in range(weights.WN):
                weights.split_hi(0, 0, q)

        @block.sync
        def _(sp):
            sp.wait_ge(expert_ready, 1)
            weights.load(sp, 0)

        @block.tensor
        def _(pe):
            pe.wait_ge(constants, 2)
            pe.wait_ge(picks_ready, 1)
            nc.tensor.matmul(rank_ps[:], before[:], picked[:].rearrange("p t e -> p (t e)"), start=True, stop=True)
            nc.tensor.matmul(total_ps[:], ones[:], picked[:].rearrange("p t e -> p (t e)"),
                             start=True, stop=True).then_inc(counted, 1)
            for n in range(2 * NTT):
                pe.wait_ge(hot, n + 1)
                last = nc.tensor.matmul(inverse_ps[:, 0:SC], lane_hot[n % 4][:],
                                        column_hot[:, n // NTT, n % NTT, :],
                                        start=(n == 0), stop=(n == 2 * NTT - 1))
                last.then_inc(used, 1)

        @block.vector
        def _(dve):
            steps = Steps(dve, own)
            dve.wait_ge(constants, 2)
            scores = logits[:, :, 0:E]
            steps.then_wait(nc.vector.tensor_reduce(top[:, 0, :], scores, AX_X, ALU.max))
            nc.vector.tensor_tensor(t1[:], scores, over_experts(top[:, 0, :]), ALU.subtract).then_inc(shifted, 1)
            dve.wait_ge(exponentials, 1)
            steps.then_wait(nc.vector.tensor_scalar(gate[:], gate[:], 1.0, None, ALU.add))
            nc.vector.reciprocal(gate[:], gate[:])
            steps.then_wait(nc.vector.tensor_reduce(top[:, 1, :], prob[:], AX_X, ALU.add))
            steps.then_wait(nc.vector.reciprocal(inv[:], top[:, 1, :]))
            steps.then_wait(nc.vector.tensor_tensor(prob[:], prob[:], over_experts(inv[:]), ALU.mult))
            for k in range(2):
                src = prob if k == 0 else t2
                steps.then_wait(nc.vector.tensor_reduce(top[:, 2 + k, :], src[:], AX_X, ALU.max))
                steps.then_wait(nc.vector.tensor_tensor(t1[:], src[:], over_experts(top[:, 2 + k, :]), ALU.is_equal))
                steps.then_wait(nc.vector.tensor_tensor(t1[:], t1[:], over_tiles(first_place[:]), ALU.mult))
                steps.then_wait(nc.vector.tensor_reduce(inv[:], t1[:], AX_X, ALU.max))
                steps.then_wait(nc.vector.tensor_tensor(pick[k][:], over_tiles(first_place[:]),
                                                        over_experts(inv[:]), ALU.is_equal))
                if k == 0:
                    steps.then_wait(nc.vector.scalar_tensor_tensor(out=t2[:], in0=pick[0][:], scalar=-2.0,
                                                                   in1=prob[:], op0=ALU.mult, op1=ALU.add))
            nc.vector.tensor_tensor(picked[:], pick[0][:], pick[1][:], ALU.add).then_inc(picks_ready, 1)
            steps.then_wait(nc.vector.tensor_tensor(top[:, 1, :], top[:, 2, :], top[:, 3, :], ALU.add))
            steps.then_wait(nc.vector.reciprocal(inv[:], top[:, 1, :]))
            nc.vector.tensor_tensor(weight[:, 0, :], top[:, 2, :], inv[:], ALU.mult)
            nc.vector.tensor_tensor(weight[:, 1, :], top[:, 3, :], inv[:], ALU.mult)
            dve.wait_ge(counted, 1)
            nc.vector.tensor_copy(count[0][:].rearrange("p t e -> p (t e)"), total_ps[:])
            steps.then_wait(nc.vector.tensor_copy(total[:].rearrange("p t e -> p (t e)"), total_ps[:]))
            a, shift = 0, 1
            while shift < NTT:
                nc.vector.tensor_copy(count[1 - a][:, 0:shift, :], count[a][:, 0:shift, :])
                steps.then_wait(nc.vector.tensor_tensor(count[1 - a][:, shift:, :], count[a][:, shift:, :],
                                                        count[a][:, 0:NTT - shift, :], ALU.add))
                a, shift = 1 - a, 2 * shift
            n_of = count[a][:, NTT - 1, :]
            steps.then_wait(nc.vector.tensor_tensor(over[:, 0:E, :], n_of.unsqueeze(2).to_broadcast([P, E, E]),
                                                    slots_before[:].unsqueeze(1).to_broadcast([P, E, E]), ALU.is_gt))
            steps.then_wait(nc.vector.tensor_reduce(tiles[0][:], over[:, 0:E, :], AX_X, ALU.add))
            steps.then_wait(nc.vector.tensor_copy(base[:], tiles[0][:]))
            b, shift = 0, 1
            while shift < E:
                nc.vector.tensor_copy(tiles[1 - b][:, 0:shift], tiles[b][:, 0:shift])
                steps.then_wait(nc.vector.tensor_tensor(tiles[1 - b][:, shift:], tiles[b][:, shift:],
                                                        tiles[b][:, 0:E - shift], ALU.add))
                b, shift = 1 - b, 2 * shift
            end = tiles[b]
            steps.then_wait(nc.vector.tensor_tensor(over[:], tile_no[:].unsqueeze(2).to_broadcast([P, NT, E]),
                                                    end[:].unsqueeze(1).to_broadcast([P, NT, E]), ALU.is_ge))
            steps.then_wait(nc.vector.tensor_reduce(tile_e[:], over[:], AX_X, ALU.add))
            nc.vector.tensor_scalar(tile_expert[:], tile_e[0:1, :], float(E - 1), None, ALU.min).then_inc(expert_ready, 1)
            steps.then_wait(nc.vector.tensor_tensor(base[:], end[:], base[:], ALU.subtract))
            steps.then_wait(nc.vector.tensor_scalar(base[:], base[:], float(TS), None, ALU.mult))
            steps.then_wait(nc.vector.tensor_tensor(t1[:], count[a][:], total[:], ALU.subtract))
            steps.then_wait(nc.vector.tensor_tensor(t1[:], t1[:], over_tiles(base[:]), ALU.add))
            steps.then_wait(nc.vector.tensor_tensor(t1[:].rearrange("p t e -> p (t e)"),
                                                    t1[:].rearrange("p t e -> p (t e)"), rank_ps[:], ALU.add))
            for k in range(2):
                steps.then_wait(nc.vector.tensor_tensor(t2[:], pick[k][:], t1[:], ALU.mult))
                steps.then_wait(nc.vector.tensor_reduce(place[:, k, :], t2[:], AX_X, ALU.add))
            steps.then_wait(nc.vector.tensor_copy(slot[:], place[:]))
            nc.vector.tensor_scalar(digit[:, 0], slot[:], 7, None, ALU.logical_shift_right)
            steps.then_wait(nc.vector.tensor_scalar(digit[:, 1], slot[:], P - 1, None, ALU.bitwise_and))
            steps.then_wait(nc.vector.tensor_copy(digit_f[:], digit[:]))
            for n in range(2 * NTT):
                k, t = divmod(n, NTT)
                if t % PART == 0:
                    nc.vector.tensor_tensor(column_hot[:, k, t:t + PART, :],
                                            column_no[:].unsqueeze(1).to_broadcast([P, PART, SC]),
                                            digit_f[:, 0, k, t:t + PART].unsqueeze(2).to_broadcast([P, PART, SC]),
                                            ALU.is_equal)
                if n >= 4:
                    dve.wait_ge(used, n - 3)
                nc.vector.tensor_scalar(lane_hot[n % 4][:], lane_no[:], digit_f[:, 1, k, t:t + 1],
                                        token_no[:, t:t + 1], ALU.is_equal, ALU.mult).then_inc(hot, 1)
            dve.wait_ge(used, 2 * NTT)
            nc.vector.tensor_copy(token_of_slot[:], inverse_ps[:, 0:SC]).then_inc(inverse_done, 1)
            dve.wait_ge(inverse_done, 1)


class GatedProducts:

    def __init__(self, nc, pe, rows, xT, act, gate_up_ps, out_ps, sems):
        self.nc, self.pe, self.rows, self.xT, self.act = nc, pe, rows, xT, act
        self.gate_up_ps, self.out_ps, self.s = gate_up_ps, out_ps, sems
        self.NC = len(rows)

    def gate_up(self, n, c, gate_cols, up_cols):
        pe, m = self.pe, self.rows[c]
        if c >= 2:
            pe.wait_ge(self.s["act_ready"], self.NC * n + c - 1)
        for which, cols in enumerate((gate_cols, up_cols)):
            step = 0
            for k in range(C):
                for i, j in PASSES:
                    last = self.nc.tensor.matmul(self.gate_up_ps[c % 2][which][0:m, :], cols(i, k), self.xT[j][:, k, :],
                                                 start=(step == 0), stop=(step == 3 * C - 1))
                    step += 1
        last.then_inc(self.s["gate_up_done"], 1)

    def down(self, n, c, weights):
        pe, m = self.pe, self.rows[c]
        if c == 0:
            pe.wait_ge(self.s["out_taken"], QT * n)
        pe.wait_ge(self.s["act_ready"], self.NC * n + c + 1)
        for i in range(QT):
            for step, (j, k) in enumerate(PASSES):
                last = self.nc.tensor.matmul(self.out_ps[i][:], self.act[c % 2][j][0:m, i * P:(i + 1) * P], weights(k),
                                             start=(c == 0 and step == 0), stop=(c == self.NC - 1 and step == 2))
            if c == self.NC - 1:
                last.then_inc(self.s["out_done"], 1)
        if c < self.NC - 1:
            last.then_inc(self.s["down_done"], 1)

    def transpose_x(self, src, c, idf):
        ps = self.gate_up_ps[1 - c // 2][c % 2]
        for t in range(QT):
            last = self.nc.tensor.transpose(ps[:, t * P:(t + 1) * P], src[:, t, c * P:(c + 1) * P], idf[:])
        last.then_inc(self.s["xT_done"], 1)


def high_x(nc, n, c, xT, gate_up_ps, s):
    nc.scalar.wait_ge(s["xT_done"], C * n + c + 1)
    nc.scalar.activation(xT[0][:, c, :], gate_up_ps[1 - c // 2][c % 2][:], ACT.Copy).then_inc(s["xT_hi"], 1)


def low_x(nc, n, c, xT, gate_up_ps, s):
    nc.vector.wait_ge(s["xT_hi"], C * n + c + 1)
    nc.vector.tensor_tensor(xT[1][:, c, :], gate_up_ps[1 - c // 2][c % 2][:], xT[0][:, c, :].bitcast(F32),
                            ALU.subtract).then_inc(s["xT_lo"], 1)


def gate_silu(nc, n, c, rows, silu, gate_up_ps, s):
    NC, m = len(rows), rows[c]
    nc.scalar.wait_ge(s["gate_up_done"], NC * n + c + 1)
    nc.scalar.wait_ge(s["act_ready"], NC * n + max(c - 1, 0))
    nc.scalar.activation(silu[c % 2][0:m, :], gate_up_ps[c % 2][0][0:m, :], ACT.Silu).then_inc(s["silu_ready"], 1)


def gate_times_up(nc, n, c, rows, silu, act, gate_up_ps, s):
    NC, m = len(rows), rows[c]
    nc.vector.wait_ge(s["silu_ready"], NC * n + c + 1)
    nc.vector.tensor_tensor(silu[c % 2][0:m, :], silu[c % 2][0:m, :], gate_up_ps[c % 2][1][0:m, :],
                            ALU.mult).then_inc(s["product"], 1)
    nc.vector.wait_ge(s["product"], 2 * (NC * n + c) + 1)
    if c >= 2:
        nc.vector.wait_ge(s["down_done"], (NC - 1) * n + c - 1)
    else:
        nc.vector.wait_ge(s["out_done"], QT * n)
    nc.vector.tensor_copy(act[c % 2][0][0:m, :], silu[c % 2][0:m, :]).then_inc(s["product"], 1)
    nc.vector.wait_ge(s["product"], 2 * (NC * n + c) + 2)
    nc.vector.tensor_tensor(act[c % 2][1][0:m, :], silu[c % 2][0:m, :], act[c % 2][0][0:m, :].bitcast(F32),
                            ALU.subtract).then_inc(s["act_ready"], 1)


GATED_SEMS = ("xT_done", "xT_hi", "xT_lo", "gate_up_done", "silu_ready", "product", "act_ready", "down_done",
              "out_done", "out_taken")


class ExpertWeights:
    ROWS = [P] * (I_MOE // P) + [I_MOE % P]
    NC = len(ROWS)
    PIECES = [(0, k) for k in range(C)] + [(1, c) for c in range(NC)]
    TURN = [PIECES[0:3], PIECES[3:5], PIECES[5:7]]
    WN = len(PIECES)

    def __init__(self, nc, ctx, gu, dn, tile_expert):
        def sb(name, shape, dt=F32):
            return ctx.enter_context(nc.sbuf_tensor("ex_" + name, shape, dt))

        self.nc, self.gu, self.dn, self.tile_expert = nc, gu, dn, tile_expert
        self.whole = [sb("gu_in", [P, C, 2 * I_MOE]), sb("dn_in", [P, self.NC, D])]
        self.gu_s = [[sb(f"gu{r}{j}", [P, C, 2 * I_MOE], F32R) for j in range(2)] for r in range(2)]
        self.dn_s = [[sb(f"dn{r}{j}", [P, self.NC, D], F32R) for j in range(2)] for r in range(2)]
        self.loaded, self.hi, self.lo = [ctx.enter_context(nc.semaphore("ex_w_" + what))
                                         for what in ("loaded", "hi", "lo")]

    def load(self, sp, n):
        e = sp.value_load(self.tile_expert[0:1, bass.ds(n, 1)], min_val=0, max_val=E - 1)
        full, last = (self.NC - 1) * P, self.ROWS[-1]
        gu_in, dn_in = self.whole
        sp.dma_start(gu_in[:], self.gu[bass.ds(e, 1)].rearrange("o p k i -> p (o k) i")).then_inc(self.loaded, 16)
        sp.dma_start(dn_in[:, 0:self.NC - 1, :], self.dn[bass.ds(e, 1), 0:full].rearrange(
            "o (c p) d -> p (o c) d", p=P)).then_inc(self.loaded, 16)
        sp.dma_start(dn_in[0:last, self.NC - 1, :], self.dn[bass.ds(e, 1), full:I_MOE].rearrange(
            "o p d -> (o p) d")).then_inc(self.loaded, 16)

    def piece(self, q, r=None, j=None):
        which, k = self.PIECES[q]
        t = self.whole[which] if r is None else (self.gu_s, self.dn_s)[which][r][j]
        return t[0:(self.ROWS[k] if which else P), k, :]

    def split_hi(self, n, r, q):
        self.nc.scalar.wait_ge(self.loaded, 48 * n + 48)
        self.nc.scalar.activation(self.piece(q, r, 0), self.piece(q), ACT.Copy).then_inc(self.hi, 1)

    def split_lo(self, n, r, q):
        self.nc.vector.wait_ge(self.hi, self.WN * n + q + 1)
        self.nc.vector.tensor_tensor(self.piece(q, r, 1), self.piece(q), self.piece(q, r, 0).bitcast(F32),
                                     ALU.subtract).then_inc(self.lo, 1)


class SharedStage:

    def __init__(self, nc, ctx, xn, shg, shu, shd):
        def sb(name, shape):
            return ctx.enter_context(nc.sbuf_tensor("sh_" + name, shape, F32))

        def sem(name):
            return ctx.enter_context(nc.semaphore("sh_" + name))

        self.xn, self.shg, self.shu, self.shd = xn, shg, shu, shd
        self.x_in, self.f = sb("x_in", [P, QT, D]), sb("f", [P, QT, D])
        self.yk = [sb(f"yk{k}", [P, QT, D]) for k in range(2)]
        self.weights = [self.f, self.yk[0]]
        self.x_loaded, self.loaded = sem("x_loaded"), [sem(f"w_loaded{r}") for r in range(2)]

    def load_x(self, sp, b):
        sp.dma_start(self.x_in[:], self.xn[bass.ds(b, 1)].rearrange("o p t d -> p (o t) d")).then_inc(self.x_loaded, 16)

    def load_weights(self, sp, c):
        t, done, cols = self.weights[c % 2], self.loaded[c % 2], slice(c * P, (c + 1) * P)
        sp.dma_start(t[:, :, 0:P], self.shg[:, :, cols]).then_inc(done, 16)
        sp.dma_start(t[:, :, P:2 * P], self.shu[:, :, cols]).then_inc(done, 16)
        sp.dma_start(t[:, 0:2, 2 * P:4 * P], self.shd[:, c, :].rearrange("p (a d) -> p a d", a=2)).then_inc(done, 16)


def build_experts(nc, xn, weights, ys, token_of_slot, stored, stage, idf):
    ctx = ExitStack()
    with ctx:
        def sb(name, shape, dt=F32):
            return ctx.enter_context(nc.sbuf_tensor("ex_" + name, shape, dt))

        def sem(name):
            return ctx.enter_context(nc.semaphore("ex_" + name))

        rows, NC, WN, TURN = weights.ROWS, weights.NC, weights.WN, weights.TURN
        xg = [sb(f"xg{r}", [P, QT, D]) for r in range(2)]
        index = [sb(f"index{r}", [P, QT], U32) for r in range(2)]
        xT = [sb(f"xT{j}", [P, C, TS], F32R) for j in range(2)]
        silu = [sb(f"silu{r}", [P, TS]) for r in range(2)]
        act_s = [[sb(f"act{r}{j}", [P, TS], F32R) for j in range(2)] for r in range(2)]
        y_out = stage.yk[1]
        bank = [ctx.enter_context(nc.psum_tensor(f"ex_bank{i}", [P, 512], F32)) for i in range(8)]
        gate_up_ps, out_ps = [bank[0:2], bank[2:4]], bank[4:8]
        s = {name: sem(name) for name in GATED_SEMS}
        gathered = [sem(f"gathered{r}") for r in range(2)]
        index_ready = [sem(f"index_ready{r}") for r in range(2)]
        block = ctx.enter_context(nc.Block())

        def turns(engine, turn):
            with engine.Fori(0, NT // 2) as pair:
                turn(2 * pair, 0, False)
                turn(2 * pair + 1, 1, False)
            turn(NT - 1, 0, True)

        @block.sync
        def _(sp):
            def turn(n, r, last):
                if not last:
                    sp.wait_ge(weights.lo, WN * n + WN)
                    weights.load(sp, n + 1)
                else:
                    stage.load_x(sp, 0)
                    for c in range(2):
                        stage.load_weights(sp, c)
                sp.wait_ge(s["out_taken"], QT * n + QT)
                sp.dma_start(ys[bass.ds(n, 1)].rearrange("o p t d -> p (o t) d"), y_out[:]).then_inc(stored, 16)

            turns(sp, turn)

        @block.gpsimd
        def _(pool):
            def gather(n, r, uses):
                nc.gpsimd.tensor_copy(index[r][:], token_of_slot[:, bass.ds(QT * n, QT)]).then_inc(index_ready[r], 1)
                pool.wait_ge(index_ready[r], 1)
                pool.wait_ge(index_ready[r], uses)
                for t in range(QT):
                    pool.indirect_dma_start(out=xg[r][:, t, :], out_offset=None, in_=xn,
                                            in_offset=bass.IndirectOffsetOnAxis(ap=index[r][:, t:t + 1], axis=0)
                                            ).then_inc(gathered[r], 16)

            gather(0, 0, 1)
            gather(1, 1, 1)
            with pool.Fori(2, NT // 2 + 1) as uses:
                pool.wait_ge(s["xT_done"], 2 * C * uses - 3 * C)
                gather(2 * uses - 2, 0, uses)
                pool.wait_ge(s["xT_done"], 2 * C * uses - 2 * C)
                gather(2 * uses - 1, 1, uses)
            pool.wait_ge(s["xT_done"], C * (NT - 2))
            gather(NT - 1, 0, NT // 2 + 1)

        @block.tensor
        def _(pe):
            g = GatedProducts(nc, pe, rows, xT, act_s, gate_up_ps, out_ps, s)
            pe.wait_ge(gathered[0], 16 * QT)
            for c in range(C):
                g.transpose_x(xg[0], c, idf)

            def turn(n, r, last):
                def gate(c):
                    return lambda j, k: weights.gu_s[r][j][:, k, c * P:c * P + rows[c]]

                def up(c):
                    return lambda j, k: weights.gu_s[r][j][:, k, I_MOE + c * P:I_MOE + c * P + rows[c]]

                pe.wait_ge(s["xT_lo"], C * n + C)
                pe.wait_ge(weights.lo, WN * n + WN)
                for c in range(NC):
                    g.gate_up(n, c, gate(c), up(c))
                    if c == NC - 1 and not last:
                        pe.wait_ge(gathered[1 - r], 16 * QT * ((n - r) // 2 + 1 + r) if isinstance(n, int)
                                   else 8 * QT * (n - r) + 16 * QT * (1 + r))
                        pe.wait_ge(s["act_ready"], NC * n + NC - 1)
                        g.transpose_x(xg[1 - r], 0, idf)
                        g.transpose_x(xg[1 - r], 1, idf)
                    if c > 0:
                        g.down(n, c - 1, lambda k: weights.dn_s[r][k][0:rows[c - 1], c - 1, :])
                if not last:
                    pe.wait_ge(s["act_ready"], NC * n + NC)
                    g.transpose_x(xg[1 - r], 2, idf)
                    g.transpose_x(xg[1 - r], 3, idf)
                g.down(n, NC - 1, lambda k: weights.dn_s[r][k][0:rows[NC - 1], NC - 1, :])

            turns(pe, turn)

        @block.scalar
        def _(act):
            for c in range(C):
                high_x(nc, 0, c, xT, gate_up_ps, s)

            def turn(n, r, last):
                q = 0
                for c in range(NC):
                    gate_silu(nc, n, c, rows, silu, gate_up_ps, s)
                    if not last:
                        for _ in TURN[c]:
                            if q == 0:
                                act.wait_ge(s["out_done"], QT * n)
                            weights.split_hi(n + 1, 1 - r, q)
                            q += 1
                if not last:
                    for c in range(C):
                        high_x(nc, n + 1, c, xT, gate_up_ps, s)
                act.wait_ge(stored, 16 * n)
                for i in range(QT):
                    act.wait_ge(s["out_done"], QT * n + i + 1)
                    nc.scalar.activation(y_out[:, i, :], out_ps[i][:], ACT.Copy).then_inc(s["out_taken"], 1)

            turns(act, turn)

        @block.vector
        def _(dve):
            for q in range(WN):
                weights.split_lo(0, 0, q)
            for c in range(C):
                low_x(nc, 0, c, xT, gate_up_ps, s)

            def turn(n, r, last):
                q = 0
                for c in range(NC):
                    gate_times_up(nc, n, c, rows, silu, act_s, gate_up_ps, s)
                    if not last:
                        for _ in TURN[c]:
                            weights.split_lo(n + 1, 1 - r, q)
                            q += 1
                if not last:
                    for c in range(C):
                        low_x(nc, n + 1, c, xT, gate_up_ps, s)

            turns(dve, turn)


def build_shared(nc, stage, ys, ys_stored, x1, out, gate, weight, slot, idf, norm_constants):
    ctx = ExitStack()
    with ctx:
        def sb(name, shape, dt=F32):
            return ctx.enter_context(nc.sbuf_tensor("sh_" + name, shape, dt))

        def sem(name):
            return ctx.enter_context(nc.semaphore("sh_" + name))

        NC = I_SH // P
        rows = [P] * NC
        gate_s = [sb(f"gate{j}", [P, C, I_SH], F32R) for j in range(2)]
        up_s = [sb(f"up{j}", [P, C, I_SH], F32R) for j in range(2)]
        dn_s = [sb(f"dn{j}", [P, NC, D], F32R) for j in range(2)]
        x_in, f = stage.x_in, stage.f
        xT = [sb(f"xT{j}", [P, C, TS], F32R) for j in range(2)]
        silu = [sb(f"silu{r}", [P, TS]) for r in range(2)]
        act_s = [[sb(f"act{r}{j}", [P, TS], F32R) for j in range(2)] for r in range(2)]
        yk = stage.yk
        index = sb("index", [P, 2, QT], U32)
        scales = sb("scales", [P, 3, QT])
        norm = InverseStd(nc, sb, sem, "", norm_constants)
        bank = [ctx.enter_context(nc.psum_tensor(f"sh_bank{i}", [P, 512], F32)) for i in range(8)]
        gate_up_ps, out_ps = [bank[0:2], bank[2:4]], bank[4:8]
        s = {name: sem(name) for name in GATED_SEMS}
        w_hi, w_lo, x1_in, stored = sem("w_hi"), sem("w_lo"), sem("x1_in"), sem("stored")
        index_ready = sem("index_ready")
        gathered = [sem(f"gathered{i}") for i in range(QT)]
        scales_ready, added, normed, finished = sem("scales_ready"), sem("added"), sem("normed"), sem("finished")
        block = ctx.enter_context(nc.Block())

        def seq(dram, b):
            return dram[bass.ds(b, 1)].rearrange("o p t d -> p (o t) d")

        def turns(engine, turn):
            with engine.Fori(0, NB - 1) as b:
                turn(b, False)
            turn(NB - 1, True)

        @block.sync
        def _(sp):
            for c in range(2, NC):
                sp.wait_ge(w_lo, c - 1)
                stage.load_weights(sp, c)

            def turn(b, last):
                if not last:
                    sp.wait_ge(s["xT_done"], C * b + C)
                    stage.load_x(sp, b + 1)
                sp.wait_ge(added, 2 * QT * b + 2 * QT)
                sp.dma_start(yk[0][:], seq(x1, b)).then_inc(x1_in, 16)
                sp.wait_ge(finished, QT * b + QT)
                sp.dma_start(seq(out, b), f[:]).then_inc(stored, 16)

            turns(sp, turn)
            sp.wait_ge(stored, 16 * NB)

        @block.tensor
        def _(pe):
            g = GatedProducts(nc, pe, rows, xT, act_s, gate_up_ps, out_ps, s)
            pe.wait_ge(stage.x_loaded, 16)
            for c in range(C):
                g.transpose_x(x_in, c, idf)

            def turn(b, last):
                pe.wait_ge(s["xT_lo"], C * b + C)
                for c in range(NC):
                    pe.wait_ge(w_lo, c + 1)
                    g.gate_up(b, c, lambda j, k: gate_s[j][:, k, c * P:(c + 1) * P],
                              lambda j, k: up_s[j][:, k, c * P:(c + 1) * P])
                    if c == NC - 1 and not last:
                        pe.wait_ge(stage.x_loaded, 16 * b + 32)
                        pe.wait_ge(s["act_ready"], NC * b + NC - 1)
                        g.transpose_x(x_in, 0, idf)
                        g.transpose_x(x_in, 1, idf)
                    if c > 0:
                        g.down(b, c - 1, lambda k: dn_s[k][:, c - 1, :])
                if not last:
                    pe.wait_ge(s["act_ready"], NC * b + NC)
                    g.transpose_x(x_in, 2, idf)
                    g.transpose_x(x_in, 3, idf)
                g.down(b, NC - 1, lambda k: dn_s[k][:, NC - 1, :])

            turns(pe, turn)

        def pieces(c, j):
            r, cols = c % 2, slice(c * P, (c + 1) * P)
            t = stage.weights[r]
            return [(gate_s[j][:, :, cols], t[:, :, 0:P]), (up_s[j][:, :, cols], t[:, :, P:2 * P]),
                    (dn_s[j][:, c, :].rearrange("p (a d) -> p a d", a=2), t[:, 0:2, 2 * P:4 * P])]

        @block.scalar
        def _(act):
            def split_hi(c):
                act.wait_ge(stage.loaded[c % 2], 48 * (c // 2) + 48)
                for dst, src in pieces(c, 0):
                    last = nc.scalar.activation(dst, src, ACT.Copy)
                last.then_inc(w_hi, 1)

            split_hi(0)
            for c in range(C):
                high_x(nc, 0, c, xT, gate_up_ps, s)
            for c in range(1, NC):
                split_hi(c)
                gate_silu(nc, 0, c - 1, rows, silu, gate_up_ps, s)

            def normalize(b):
                for i in range(QT):
                    act.wait_ge(norm.ready, b + 1)
                    nc.scalar.activation(f[:, i, :], f[:, i, :], ACT.Identity, bias=norm.bias[:, i:i + 1],
                                         scale=norm.rstd[:, i:i + 1]).then_inc(normed, 1)

            def turn(b, last, begun=0):
                for c in range(begun, NC):
                    gate_silu(nc, b, c, rows, silu, gate_up_ps, s)
                    if c == 6 and begun == 0:
                        normalize(b - 1)
                if not last:
                    for c in range(C):
                        high_x(nc, b + 1, c, xT, gate_up_ps, s)
                act.wait_ge(scales_ready, b + 1)
                act.wait_ge(stored, 16 * b)
                for i in range(QT):
                    act.wait_ge(s["out_done"], QT * b + i + 1)
                    nc.scalar.activation(f[:, i, :], out_ps[i][:], ACT.Copy,
                                         scale=scales[:, 2, i:i + 1]).then_inc(s["out_taken"], 1)

            turn(0, False, NC - 1)
            with act.Fori(1, NB - 1) as b:
                turn(b, False)
            turn(NB - 1, True)
            normalize(NB - 1)

        @block.vector
        def _(dve):
            def split_lo(c):
                dve.wait_ge(w_hi, c + 1)
                for (dst, src), (high, _) in zip(pieces(c, 1), pieces(c, 0)):
                    last = nc.vector.tensor_tensor(dst, src, high.bitcast(F32), ALU.subtract)
                last.then_inc(w_lo, 1)

            split_lo(0)
            for c in range(C):
                low_x(nc, 0, c, xT, gate_up_ps, s)
            for c in range(1, NC):
                split_lo(c)
                gate_times_up(nc, 0, c - 1, rows, silu, act_s, gate_up_ps, s)

            def add_picks(b, i):
                if i > 0:
                    norm.await_stats(b, i)
                dve.wait_ge(s["out_taken"], QT * b + i + 1)
                dve.wait_ge(gathered[i], 32 * b + 32)
                for k in range(2):
                    nc.vector.scalar_tensor_tensor(out=f[:, i, :], in0=yk[k][:, i, :], scalar=scales[:, k, i:i + 1],
                                                   in1=f[:, i, :], op0=ALU.mult, op1=ALU.add).then_inc(added, 1)
                    if k == 0 and i > 0:
                        norm.aggregate([i - 1])
                    dve.wait_ge(added, 2 * QT * b + 2 * i + k + 1)
                norm.row_stats(f, i)

            def first_guess(b):
                norm.await_stats(b)
                nc.vector.memset(norm.half[:], 0.0)
                norm.aggregate([QT - 1])
                norm.halve(b)
                norm.shift_bits(b)
                norm.guess(b)

            def turn(b, last, begun=0):
                for c in range(begun, NC):
                    gate_times_up(nc, b, c, rows, silu, act_s, gate_up_ps, s)
                    if begun == 0 and c < QT:
                        add_picks(b - 1, c)
                    if begun == 0 and c == QT:
                        first_guess(b - 1)
                if not last:
                    for c in range(C):
                        low_x(nc, b + 1, c, xT, gate_up_ps, s)
                nc.vector.tensor_copy(scales[:, 0:2, :], weight[:, :, bass.ds(QT * b, QT)])
                nc.vector.tensor_copy(scales[:, 2, :], gate[:, bass.ds(QT * b, QT)]).then_inc(scales_ready, 1)

            turn(0, False, NC - 1)
            with dve.Fori(1, NB - 1) as b:
                turn(b, False)
            turn(NB - 1, True)
            for i in range(QT):
                add_picks(NB - 1, i)
            first_guess(NB - 1)

        @block.gpsimd
        def _(pool):
            def turn(b, turns_begun):
                nc.gpsimd.tensor_copy(index[:], slot[:, :, bass.ds(QT * b, QT)]).then_inc(index_ready, 1)
                pool.wait_ge(w_lo, NC)
                pool.wait_ge(index_ready, turns_begun)
                for i in range(QT):
                    for k in range(2):
                        pool.indirect_dma_start(out=yk[k][:, i, :], out_offset=None, in_=ys,
                                                in_offset=bass.IndirectOffsetOnAxis(ap=index[:, k, i:i + 1], axis=0)
                                                ).then_inc(gathered[i], 16)
                norm.refine(b)
                for i in range(QT):
                    pool.wait_ge(normed, QT * b + i + 1)
                    pool.wait_ge(x1_in, 16 * b + 16)
                    nc.gpsimd.tensor_tensor(f[:, i, :], f[:, i, :], yk[0][:, i, :], ALU.add).then_inc(finished, 1)

            pool.wait_ge(ys_stored, 16 * NT)
            with pool.Fori(1, NB + 1) as turns_begun:
                turn(turns_begun - 1, turns_begun)


def build_layer(nc, x, wq, wvk, wo, wr, qb, vkb, ob, gu, dn, shg, shu, shd, out):
    def scratch(name, rows):
        return nc.dram_tensor(name, (rows, D), F32, kind="Internal").ap()

    def by_sequence(dram):
        return dram.rearrange("(b t p) d -> b p t d", t=QT, p=P)

    x1, xn, ys = scratch("x1", NB * S), scratch("xn", NB * S), scratch("ys", NT * TS)
    with ExitStack() as ctx:
        def sb(name, shape, dt=F32):
            return ctx.enter_context(nc.sbuf_tensor(name, shape, dt))

        idf, idb, mask = sb("idf", [P, P]), sb("idb", [P, 2, P], BF16), sb("mask", [P, 2, P], BF16)
        norm_constants = sb("norm_constants", [P, 2, QT])
        logits = sb("logits", [P, NTT, R])
        build_attention(nc, by_sequence(x), wq, wvk, wo, wr, qb, vkb, ob, by_sequence(x1), by_sequence(xn),
                        logits, idf, idb, mask, norm_constants)
        gate = sb("gate", [P, NTT])
        weight = sb("weight", [P, 2, NTT])
        slot = sb("slot", [P, 2, NTT], I32)
        token_of_slot = sb("token_of_slot", [P, SC], I32)
        tile_expert = sb("tile_expert", [1, NT], I32)
        ys_stored = ctx.enter_context(nc.semaphore("ys_stored"))
        stage = SharedStage(nc, ctx, by_sequence(xn), shg, shu, shd)
        with ExitStack() as inner:
            weights = ExpertWeights(nc, inner, gu, dn, tile_expert)
            build_routing(nc, logits, gate, weight, slot, token_of_slot, tile_expert, weights)
            build_experts(nc, xn, weights, ys.rearrange("(n t p) d -> n p t d", t=QT, p=P), token_of_slot,
                          ys_stored, stage, idf)
        build_shared(nc, stage, ys, ys_stored, by_sequence(x1), by_sequence(out), gate, weight, slot, idf,
                     norm_constants)


def kernel(**inputs):
    import numpy as np
    import concourse.bacc as bacc
    from concourse.bass_utils import run_bass_kernel_spmd

    a = {k.split("_", 2)[2]: np.asarray(v) for k, v in inputs.items()}

    def chunked(w):
        return np.ascontiguousarray(w.T.reshape(-1, P, w.shape[0]).transpose(1, 0, 2))

    arrays = {
        "x_in": a["hidden_states"].reshape(NB * S, D),
        "wq_in": chunked(a["q_w"]),
        "wvk_in": chunked(np.concatenate([a["v_w"], a["k_w"]])),
        "wo_in": chunked(a["o_w"]),
        "wr_in": chunked(np.concatenate([a["router_weight"], a["shared_gate_w"]])),
        "qb_in": np.ascontiguousarray(a["q_b"].reshape(C, P).T),
        "vkb_in": np.concatenate([a["v_b"], a["k_b"]]).reshape(2 * HD, 1),
        "ob_in": a["o_b"],
        "gu_in": np.stack([chunked(w) for w in a["gate_up_proj"]]),
        "dn_in": np.ascontiguousarray(a["down_proj"].transpose(0, 2, 1)),
        "shg_in": chunked(a["sh_gate_w"]),
        "shu_in": chunked(a["sh_up_w"]),
        "shd_in": chunked(a["sh_down_w"]),
    }
    nc = bacc.Bacc("TRN2", target_bir_lowering=False, num_devices=1)
    args = [nc.dram_tensor(k, v.shape, F32, kind="ExternalInput").ap() for k, v in arrays.items()]
    out = nc.dram_tensor("out", (NB * S, D), F32, kind="ExternalOutput").ap()
    build_layer(nc, *args, out)
    r = run_bass_kernel_spmd(nc, [arrays], core_ids=[0])
    return r.results[0]["out"].reshape(NB, S, D)
```
